# Optimizing a Trainium2 kernel written in Bass

```python
import numpy as np
import jax
import jax.numpy as jnp

def _softmax(x, axis=-1):
    return jax.nn.softmax(x, axis=axis)

def _gelu(x):
    return jax.nn.gelu(x, approximate=True)

def _silu(x):
    return jax.nn.silu(x)

def _sigmoid(x):
    return jax.nn.sigmoid(x)

def _layernorm(x, axis=-1, eps=1e-05):
    m = jnp.mean(x, axis=axis, keepdims=True)
    v = jnp.var(x, axis=axis, keepdims=True)
    return (x - m) / jnp.sqrt(v + eps)

def _scatter_add(tgt, idx, src, axis=0):
    return tgt.at[idx].add(src)

def _segment_sum(src, seg, n):
    return jax.ops.segment_sum(src, seg, n)
kernel_name = 'mk_gnn_preln_d2_gnn_r8_fa6395'

def setup_inputs(seed: int=0):
    np.random.seed(seed)
    _w = jnp.asarray

    def _rec_inputs():
        import jax
        import jax.numpy as jnp
        _gk = jax.random.key(seed)
        x = -0.0003713 + 1 * jax.random.normal(jax.random.fold_in(_gk, 1), (6250, 256), jnp.float32)
        src = jax.random.randint(jax.random.fold_in(_gk, 2), (100000,), 0, 6250, jnp.int32)
        dst = jax.random.randint(jax.random.fold_in(_gk, 3), (100000,), 0, 6250, jnp.int32)
        _o = jnp.argsort(dst, stable=True)
        src = src[_o]
        dst = dst[_o]
        return (x, src, dst)
    x, src, dst = _rec_inputs()

    def _L0_gnn_setup():
        import jax, jax.numpy as jnp
        import numpy as np
        N_NODES = 6250
        N_EDGES = 100000
        D_MODEL = 256
        NUM_HEADS = 8
        HEAD_DIM = D_MODEL // NUM_HEADS
        D_FF = 2 * D_MODEL
        NEG_SLOPE = 0.2
        BN_EPS = 1e-05

        def _batch_norm(h, g, b):
            mean = jnp.mean(h, axis=0)
            var = jnp.mean((h - mean) ** 2, axis=0)
            return (h - mean) * jax.lax.rsqrt(var + BN_EPS) * g + b
        key = jax.random.key(seed)
        ks = jax.random.split(key, 16)
        x = jax.random.normal(ks[0], (N_NODES, D_MODEL), dtype=jnp.float32)
        src = jax.random.randint(ks[1], (N_EDGES,), 0, N_NODES)
        off = jax.random.randint(ks[2], (N_EDGES,), 1, N_NODES)
        dst = (src + off) % N_NODES
        edge_index = jnp.stack([src, dst]).astype(jnp.int64)

        def lin(k, fi, fo):
            s = 1.0 / np.sqrt(fi)
            return jax.random.uniform(k, (fi, fo), jnp.float32, -s, s)
        inp = {'x': x, 'edge_index': edge_index, 'Wq': lin(ks[3], D_MODEL, D_MODEL), 'bq': jnp.zeros((D_MODEL,), jnp.float32), 'Wk': lin(ks[4], D_MODEL, D_MODEL), 'bk': jnp.zeros((D_MODEL,), jnp.float32), 'Wv': lin(ks[5], D_MODEL, D_MODEL), 'bv': jnp.zeros((D_MODEL,), jnp.float32), 'Wo': lin(ks[6], D_MODEL, D_MODEL), 'bo': jnp.zeros((D_MODEL,), jnp.float32), 'W1': lin(ks[7], D_MODEL, D_FF), 'b1': jnp.zeros((D_FF,), jnp.float32), 'W2': lin(ks[8], D_FF, D_MODEL), 'b2': jnp.zeros((D_MODEL,), jnp.float32), 'bn1_g': jnp.ones((D_MODEL,), jnp.float32), 'bn1_b': jnp.zeros((D_MODEL,), jnp.float32), 'bn2_g': jnp.ones((D_MODEL,), jnp.float32), 'bn2_b': jnp.zeros((D_MODEL,), jnp.float32)}
        return inp
    _L0_gnn_all = _L0_gnn_setup()
    _L0_gnn_in = {k: v for k, v in _L0_gnn_all.items() if k in ('Wq', 'bq', 'Wk', 'bk', 'Wv', 'bv', 'Wo', 'bo', 'W1', 'b1', 'W2', 'b2', 'bn1_g', 'bn1_b', 'bn2_g', 'bn2_b')}
    del _L0_gnn_all

    def _L1_gnn_setup():
        import jax, jax.numpy as jnp
        import numpy as np
        N_NODES = 6250
        N_EDGES = 100000
        IN_C, HID_C, OUT_C = (256, 512, 256)

        def _linear_params(key, fan_in, fan_out):
            kw, kb = jax.random.split(key)
            bound = 1.0 / np.sqrt(fan_in)
            w = jax.random.uniform(kw, (fan_in, fan_out), jnp.float32, -bound, bound)
            b = jax.random.uniform(kb, (fan_out,), jnp.float32, -bound, bound)
            return (w, b)

        def _gin_conv(h, src, dst, w, b, eps, n_nodes):
            agg = jax.ops.segment_sum(h[src], dst, num_segments=n_nodes)
            return ((1.0 + eps) * h + agg) @ w + b
        key = jax.random.key(seed)
        ks = jax.random.split(key, 6)
        x = jax.random.normal(ks[0], (N_NODES, IN_C), jnp.float32)
        src = jax.random.randint(ks[1], (N_EDGES,), 0, N_NODES, jnp.int32)
        dst = jax.random.randint(ks[2], (N_EDGES,), 0, N_NODES, jnp.int32)
        w1, b1 = _linear_params(ks[3], IN_C, HID_C)
        w2, b2 = _linear_params(ks[4], HID_C, HID_C)
        w3, b3 = _linear_params(ks[5], HID_C, OUT_C)
        eps = jnp.zeros((), jnp.float32)
        return {'x': x, 'src': src, 'dst': dst, 'w1': w1, 'b1': b1, 'eps1': eps, 'w2': w2, 'b2': b2, 'eps2': eps, 'w3': w3, 'b3': b3, 'eps3': eps}
    _L1_gnn_all = _L1_gnn_setup()
    _L1_gnn_in = {k: v for k, v in _L1_gnn_all.items() if k in ('w1', 'b1', 'eps1', 'w2', 'b2', 'eps2', 'w3', 'b3', 'eps3')}
    del _L1_gnn_all
    return {'x': x, 'src': src, 'dst': dst, 'L0_gnn_Wq': _L0_gnn_in['Wq'], 'L0_gnn_bq': _L0_gnn_in['bq'], 'L0_gnn_Wk': _L0_gnn_in['Wk'], 'L0_gnn_bk': _L0_gnn_in['bk'], 'L0_gnn_Wv': _L0_gnn_in['Wv'], 'L0_gnn_bv': _L0_gnn_in['bv'], 'L0_gnn_Wo': _L0_gnn_in['Wo'], 'L0_gnn_bo': _L0_gnn_in['bo'], 'L0_gnn_W1': _L0_gnn_in['W1'], 'L0_gnn_b1': _L0_gnn_in['b1'], 'L0_gnn_W2': _L0_gnn_in['W2'], 'L0_gnn_b2': _L0_gnn_in['b2'], 'L0_gnn_bn1_g': _L0_gnn_in['bn1_g'], 'L0_gnn_bn1_b': _L0_gnn_in['bn1_b'], 'L0_gnn_bn2_g': _L0_gnn_in['bn2_g'], 'L0_gnn_bn2_b': _L0_gnn_in['bn2_b'], 'L1_gnn_w1': _L1_gnn_in['w1'], 'L1_gnn_b1': _L1_gnn_in['b1'], 'L1_gnn_eps1': _L1_gnn_in['eps1'], 'L1_gnn_w2': _L1_gnn_in['w2'], 'L1_gnn_b2': _L1_gnn_in['b2'], 'L1_gnn_eps2': _L1_gnn_in['eps2'], 'L1_gnn_w3': _L1_gnn_in['w3'], 'L1_gnn_b3': _L1_gnn_in['b3'], 'L1_gnn_eps3': _L1_gnn_in['eps3']}

def reference(x, src, dst, L0_gnn_Wq, L0_gnn_bq, L0_gnn_Wk, L0_gnn_bk, L0_gnn_Wv, L0_gnn_bv, L0_gnn_Wo, L0_gnn_bo, L0_gnn_W1, L0_gnn_b1, L0_gnn_W2, L0_gnn_b2, L0_gnn_bn1_g, L0_gnn_bn1_b, L0_gnn_bn2_g, L0_gnn_bn2_b, L1_gnn_w1, L1_gnn_b1, L1_gnn_eps1, L1_gnn_w2, L1_gnn_b2, L1_gnn_eps2, L1_gnn_w3, L1_gnn_b3, L1_gnn_eps3):
    import jax
    import jax.numpy as jnp

    def _L0_gnn_ref(x, edge_index, Wq, bq, Wk, bk, Wv, bv, Wo, bo, W1, b1, W2, b2, bn1_g, bn1_b, bn2_g, bn2_b):
        import jax, jax.numpy as jnp
        import numpy as np
        N_NODES = 6250
        N_EDGES = 100000
        D_MODEL = 256
        NUM_HEADS = 8
        HEAD_DIM = D_MODEL // NUM_HEADS
        D_FF = 2 * D_MODEL
        NEG_SLOPE = 0.2
        BN_EPS = 1e-05

        def _batch_norm(h, g, b):
            mean = jnp.mean(h, axis=0)
            var = jnp.mean((h - mean) ** 2, axis=0)
            return (h - mean) * jax.lax.rsqrt(var + BN_EPS) * g + b
        N = x.shape[0]
        Qh = (x @ Wq + bq).reshape(N, NUM_HEADS, HEAD_DIM)
        Kh = (x @ Wk + bk).reshape(N, NUM_HEADS, HEAD_DIM)
        Vh = (x @ Wv + bv).reshape(N, NUM_HEADS, HEAD_DIM)
        s = jnp.einsum('nhc,nhc->nh', Qh, Kh) / jnp.sqrt(jnp.float32(HEAD_DIM))
        loops = jnp.arange(N, dtype=edge_index.dtype)
        src = jnp.concatenate([edge_index[0], loops])
        dst = jnp.concatenate([edge_index[1], loops])
        alpha = jax.nn.leaky_relu(s[src] + s[dst], NEG_SLOPE)
        m = jax.ops.segment_max(alpha, dst, num_segments=N)
        e = jnp.exp(alpha - m[dst])
        denom = jax.ops.segment_sum(e, dst, num_segments=N)
        a = e / denom[dst]
        msg = Vh[src] * a[:, :, None]
        attn = jax.ops.segment_sum(msg, dst, num_segments=N).reshape(N, D_MODEL)
        h = attn @ Wo + bo
        h = x + h
        h = _batch_norm(h, bn1_g, bn1_b)
        h2 = jax.nn.relu(h @ W1 + b1) @ W2 + b2
        h = _batch_norm(h + h2, bn2_g, bn2_b)
        return h

    def _L1_gnn_ref(x, src, dst, w1, b1, eps1, w2, b2, eps2, w3, b3, eps3):
        import jax, jax.numpy as jnp
        import numpy as np
        N_NODES = 6250
        N_EDGES = 100000
        IN_C, HID_C, OUT_C = (256, 512, 256)

        def _linear_params(key, fan_in, fan_out):
            kw, kb = jax.random.split(key)
            bound = 1.0 / np.sqrt(fan_in)
            w = jax.random.uniform(kw, (fan_in, fan_out), jnp.float32, -bound, bound)
            b = jax.random.uniform(kb, (fan_out,), jnp.float32, -bound, bound)
            return (w, b)

        def _gin_conv(h, src, dst, w, b, eps, n_nodes):
            agg = jax.ops.segment_sum(h[src], dst, num_segments=n_nodes)
            return ((1.0 + eps) * h + agg) @ w + b
        n = x.shape[0]
        h = jax.nn.relu(_gin_conv(x, src, dst, w1, b1, eps1, n))
        h = jax.nn.relu(_gin_conv(h, src, dst, w2, b2, eps2, n))
        return _gin_conv(h, src, dst, w3, b3, eps3, n)
    edge_index = jnp.stack([src, dst])
    h = jnp.maximum(_layernorm(x, axis=-1), 0.0)
    x = x + _L0_gnn_ref(h, edge_index, L0_gnn_Wq, L0_gnn_bq, L0_gnn_Wk, L0_gnn_bk, L0_gnn_Wv, L0_gnn_bv, L0_gnn_Wo, L0_gnn_bo, L0_gnn_W1, L0_gnn_b1, L0_gnn_W2, L0_gnn_b2, L0_gnn_bn1_g, L0_gnn_bn1_b, L0_gnn_bn2_g, L0_gnn_bn2_b)
    h = jnp.maximum(_layernorm(x, axis=-1), 0.0)
    x = x + _L1_gnn_ref(h, src, dst, L1_gnn_w1, L1_gnn_b1, L1_gnn_eps1, L1_gnn_w2, L1_gnn_b2, L1_gnn_eps2, L1_gnn_w3, L1_gnn_b3, L1_gnn_eps3)
    return x

_drawn_inputs = setup_inputs


def setup_inputs(seed=0):
    import zlib

    import numpy as np

    out = dict(_drawn_inputs(seed))
    spreads = {'L0_gnn_bq': (0.0, 2.0),
     'L0_gnn_bk': (0.0, 2.0),
     'L0_gnn_bv': (0.0, 2.0),
     'L0_gnn_bo': (0.0, 2.0),
     'L0_gnn_b1': (0.0, 2.0),
     'L0_gnn_b2': (0.0, 2.0),
     'L0_gnn_bn1_g': (1.0, 0.6),
     'L0_gnn_bn1_b': (0.0, 2.0),
     'L0_gnn_bn2_g': (1.0, 0.2),
     'L0_gnn_bn2_b': (0.0, 0.1)}
    factors = {'L0_gnn_Wq': 70.419,
     'L0_gnn_Wk': 69.318,
     'L0_gnn_Wv': 65.067,
     'L0_gnn_Wo': 61.564,
     'L0_gnn_W1': 64.103,
     'L0_gnn_W2': 61.376,
     'L1_gnn_b1': 6.045,
     'L1_gnn_b2': 61.946,
     'L1_gnn_b3': 200.0}
    for name, (base, spread) in spreads.items():
        noise = np.random.default_rng([zlib.crc32(name.encode()), seed]).standard_normal(out[name].shape)
        drawn = base * np.exp(spread * noise) if base else spread * noise
        out[name] = jnp.asarray(drawn.astype(out[name].dtype))
    for name, factor in factors.items():
        out[name] = (out[name] * factor).astype(out[name].dtype)
    return out
```

```python
import concourse.bass as bass
from concourse import mybir
from contextlib import ExitStack
import itertools

F32 = mybir.dt.float32
BF16 = mybir.dt.bfloat16
I32 = mybir.dt.int32
ALU = mybir.AluOpType
ACT = mybir.ActivationFunctionType
AX = mybir.AxisListType

N = 6250
E = 100000
D = 256
HEADS = 8
DH = D // HEADS
DFF = 512
HID = 512
P = 128
NB = 125
BLOCKS = N // NB
PAIRS = BLOCKS // 2
T = 17
RE = T * P
TW = D + HEADS
EPP = 800
EP = E // EPP
REC = 4
GATHERED = 16 * T
BIG = 1.0e30
LN_EPS = 1e-5
BN_EPS = 1e-5
SLOPE = 0.2


WAIT_REGISTERS = itertools.count()


def wait_apart(engine, sem, value, least):
    if not isinstance(value, int):
        held = engine.alloc_register(f"wait_value{next(WAIT_REGISTERS)}")
        engine.reg_mov(held, value)
        value = engine.snap(held, min_val=1, max_val=1 << 20)
    engine.wait_ge(sem, least)
    engine.wait_ge(sem, value)


class InOrder:

    def __init__(self, engine, sem):
        self.engine, self.sem, self.n = engine, sem, 0

    def step(self, instruction):
        self.n += 1
        instruction.then_inc(self.sem, 1)
        self.engine.wait_ge(self.sem, self.n)

    def restart(self):
        if self.n:
            self.engine.sem_clear(self.sem)
        self.n = 0


def build(nc, x, src, dst, Wq, bq, Wk, bk, Wv, bv, Wo, bo, W1, b1, W2, b2, g1, be1, g2, be2,
          w1, c1, eps1, w2, c2, eps2, w3, c3, eps3, out):
    edges = nc.dram_tensor("edge_records", (E + RE, REC), I32).ap()
    table0 = nc.dram_tensor("table0", (N, TW), F32).ap()
    table1 = nc.dram_tensor("table1", (N, D), F32).ap()
    table2 = nc.dram_tensor("table2", (N, HID), F32).ap()
    table3 = nc.dram_tensor("table3", (N, D), F32).ap()
    x1 = nc.dram_tensor("x1", (N, D), F32).ap()
    spare = nc.dram_tensor("spare", (16, P), F32).ap()
    spare_rows = iter(range(16))

    with ExitStack() as ctx:
        def sb(name, shape, dt=F32):
            return ctx.enter_context(nc.sbuf_tensor(name, shape, dt))

        banks = [ctx.enter_context(nc.psum_tensor(f"bank{n}", [P, 512], F32)) for n in range(8)]

        arena = sb("arena", [P, 2 * N + 2 * T * TW])
        hT = arena[:, 0:2 * N].rearrange("p (k n) -> p k n", k=2)
        gathered0 = [arena[:, 2 * N + s * T * TW:2 * N + (s + 1) * T * TW] for s in range(2)]

        def gathered(s, w):
            return arena[:, s * T * w:(s + 1) * T * w]

        onehot = [sb(f"onehot{s}", [P, T, NB]) for s in range(2)]
        record = [sb(f"record{s}", [P, T, REC], I32) for s in range(2)]
        relative = [sb(f"relative{s}", [P, T]) for s in range(2)]
        identity = sb("identity", [P, P])
        column = sb("column", [P, NB])
        minus_base = sb("minus_base", [P, BLOCKS])
        zeros = sb("zeros", [P, 512], BF16)
        ones = sb("ones", [P, 1])
        end_mask = sb("end_mask", [P, T])
        eps_ln = sb("eps_ln", [P, 1])
        eps_bn = sb("eps_bn", [P, 1])
        counts = sb("counts", [P, BLOCKS + 1])
        first_edge = sb("first_edge", [1, BLOCKS + 1], I32)
        scores = sb("scores", [NB, BLOCKS, HEADS])
        stats = sb("stats", [P, 2, BLOCKS, 6])
        moments = sb("moments", [P, 2, 2])
        gain = sb("gain", [P, 2])
        shift = sb("shift", [P, 2])
        spread = sb("spread", [P, 2])
        wqkv_sb = sb("wqkv_sb", [P, 2, 3 * D])
        bqkv_sb = sb("bqkv_sb", [NB, 3 * D])
        wo_sb = sb("wo_sb", [P, 2, D])
        wf1_sb = sb("wf1_sb", [P, 2, DFF])
        wf2_sb = sb("wf2_sb", [P, 4, D])
        w1_sb = sb("w1_sb", [P, 2, HID])
        w2_sb = sb("w2_sb", [P, 4, HID])
        w3_sb = sb("w3_sb", [P, 4, D])
        c1_sb = sb("c1_sb", [NB, HID])
        c3_sb = sb("c3_sb", [NB, D])
        boT = sb("boT", [P, 2])
        b1T = sb("b1T", [P, 4])
        b2T = sb("b2T", [P, 2])
        bnT = sb("bnT", [P, 4, 2])
        c2T = sb("c2T", [P, 4])
        one_eps = sb("one_eps", [P, 3])

        def phase_semaphores(phase):
            taken = []

            def clear():
                nc.clear_and_free_semaphores(taken)
                nc.all_engine_barrier()

            def sem(name):
                taken.append(nc.alloc_semaphore(name))
                return taken[-1]

            phase.callback(clear)
            return sem

        def first_store(engine, stored):
            n = next(spare_rows)
            engine.dma_start(spare[n:n + 1, :], identity[0:1, :]).then_inc(stored, 16)

        def block_rows(table, b):
            return table[bass.ds(b * NB, NB), :]

        def node_columns(k, b):
            return hT[:, k, bass.ds(b * NB, NB)]

        with ExitStack() as phase:
            sem = phase_semaphores(phase)

            loaded = sem("weights_loaded")
            dst_loaded = sem("dst_loaded")
            src_loaded = sem("src_loaded")
            edge_memset = sem("edge_memset")
            made = sem("constants_made")
            masks = sem("masks_made")
            records_made = sem("records_made")
            records_stored = sem("records_stored")
            counted = sem("edges_counted")
            summed = sem("counts_summed")
            dve_order = sem("dve_order")
            pool_order = sem("pool_order")

            dst_int = arena[0:EP, 0:EPP + 2].bitcast(I32)
            dst_f = arena[0:EP, 1000:1000 + EPP + 2]
            record_all = arena[0:EP, 2000:2000 + EPP * REC].rearrange("p (e c) -> p e c", c=REC)
            compared = arena[0:EP, 6000:6000 + EPP]
            src_int = arena[0:EP, 7000:7000 + EPP].bitcast(I32)
            tail = arena[:, 8000:8000 + T * REC].rearrange("p (e c) -> p e c", c=REC)
            eps_f = arena[:, 9000:9003]
            block = phase.enter_context(nc.Block())

            @block.sync
            def _(sp):
                sp.wait_ge(edge_memset, 1)
                sp.dma_start(dst_int[:, 1:EPP + 1], dst.rearrange("(p e) -> p e", e=EPP)).then_inc(dst_loaded, 16)
                dst_rows = dst.rearrange("(p e) -> p e", e=EPP)
                with nc.allow_non_contiguous_dma("one neighbour per partition"):
                    sp.dma_start(dst_int[1:EP, 0:1], dst_rows[0:EP - 1, EPP - 1:EPP]).then_inc(dst_loaded, 16)
                    sp.dma_start(dst_int[0:EP - 1, EPP + 1:EPP + 2], dst_rows[1:EP, 0:1]).then_inc(dst_loaded, 16)
                sp.dma_start(src_int, src.rearrange("(p e) -> p e", e=EPP)).then_inc(src_loaded, 16)
                for n, w in enumerate((Wq, Wk, Wv)):
                    sp.dma_start(wqkv_sb[:, :, n * D:(n + 1) * D], w.rearrange("(k p) n -> p k n", p=P)).then_inc(loaded, 16)
                for n, b in enumerate((bq, bk, bv)):
                    sp.dma_start(bqkv_sb[:, n * D:(n + 1) * D], b.partition_broadcast(NB)).then_inc(loaded, 16)
                for tile, w in ((wo_sb, Wo), (wf1_sb, W1), (wf2_sb, W2), (w1_sb, w1), (w2_sb, w2), (w3_sb, w3)):
                    sp.dma_start(tile[:, :, :], w.rearrange("(k p) n -> p k n", p=P)).then_inc(loaded, 16)
                sp.dma_start(c1_sb[:, :], c1.partition_broadcast(NB)).then_inc(loaded, 16)
                sp.dma_start(c3_sb[:, :], c3.partition_broadcast(NB)).then_inc(loaded, 16)
                n_loads = 14
                sp.wait_ge(records_made, 1)
                sp.dma_start(edges[0:E, :].rearrange("(p e) c -> p (e c)", e=EPP),
                             record_all.bitcast(I32).rearrange("p e c -> p (e c)")).then_inc(records_stored, 16)
                sp.dma_start(edges[E:E + RE, :].rearrange("(p e) c -> p (e c)", e=T),
                             tail.bitcast(I32).rearrange("p e c -> p (e c)")).then_inc(records_stored, 16)
                sp.wait_ge(loaded, 16 * n_loads)
                sp.wait_ge(records_stored, 32)

            @block.scalar
            def _(act):
                with nc.allow_non_contiguous_dma("vectors of one value per channel"):
                    loads = [(boT[:, :], bo), (b1T[:, :], b1), (b2T[:, :], b2), (c2T[:, :], c2),
                             (bnT[:, 0, :], g1), (bnT[:, 1, :], be1), (bnT[:, 2, :], g2), (bnT[:, 3, :], be2)]
                    for tile, v in loads:
                        act.dma_start(tile, v.rearrange("(k p) -> p k", p=P)).then_inc(made, 16)
                    for n, e in enumerate((eps1, eps2, eps3)):
                        act.dma_start(eps_f[:, n:n + 1], e.partition_broadcast(P)).then_inc(made, 16)
                act.wait_ge(made, 16 * (len(loads) + 3))

            @block.gpsimd
            def _(pool):
                order = InOrder(pool, pool_order)
                order.step(pool.memset(identity[:, :], 0.0))
                pool.affine_select(out=identity[:, :], in_=identity[:, :], compare_op=ALU.not_equal, fill=1.0,
                                   base=0, pattern=[[-1, P]], channel_multiplier=1).then_inc(masks, 1)
                order.step(pool.memset(end_mask[:, :], 0.0))
                pool.affine_select(out=end_mask[:, :], in_=end_mask[:, :], compare_op=ALU.not_equal, fill=1.0,
                                   base=-(T - 1) - (P - 1), pattern=[[1, T]], channel_multiplier=1)
                pool.iota(column[:, :], pattern=[[1, NB]], base=0, channel_multiplier=0,
                          allow_small_or_imprecise_dtypes=True).then_inc(masks, 1)
                pool.iota(minus_base[:, :], pattern=[[-NB, BLOCKS]], base=0, channel_multiplier=0,
                          allow_small_or_imprecise_dtypes=True).then_inc(masks, 1)
                pool.memset(zeros[:, :], 0.0).then_inc(masks, 1)
                pool.memset(ones[:, :], 1.0).then_inc(masks, 1)
                pool.memset(eps_ln[:, :], LN_EPS).then_inc(masks, 1)
                pool.memset(eps_bn[:, :], BN_EPS).then_inc(masks, 1)

            @block.vector
            def _(dve):
                order = InOrder(dve, dve_order)
                dve.memset(dst_int, -1).then_inc(edge_memset, 1)
                order.step(dve.memset(tail, 0.0))
                order.step(dve.memset(tail[:, :, 1], BIG))
                dve.wait_ge(dst_loaded, 48)
                order.step(dve.tensor_copy(dst_f, dst_int))
                own = dst_f[:, 1:EPP + 1]
                order.step(dve.tensor_copy(record_all[:, :, 1], own))
                order.step(dve.tensor_tensor(compared, own, dst_f[:, 0:EPP], ALU.not_equal))
                order.step(dve.tensor_scalar(record_all[:, :, 2], compared, -BIG, None, ALU.mult))
                order.step(dve.tensor_tensor(record_all[:, :, 3], own, dst_f[:, 2:EPP + 2], ALU.not_equal))
                dve.wait_ge(src_loaded, 16)
                dve.tensor_copy(record_all[:, :, 0].bitcast(I32), src_int).then_inc(records_made, 1)
                for b in range(BLOCKS + 1):
                    order.step(dve.tensor_scalar(compared, own, float(b * NB), 0.0, ALU.is_lt, ALU.add,
                                                 accum_out=counts[0:EP, b:b + 1]))
                dve.wait_ge(made, 16 * 11)
                order.step(dve.tensor_scalar(one_eps[:, :], eps_f, 1.0, None, ALU.add))
                order.restart()
                dve.sem_inc(counted, 1)
                dve.wait_ge(summed, 1)
                order.step(dve.tensor_copy(first_edge[:, :], banks[0][0:1, 0:BLOCKS + 1]))

            @block.tensor
            def _(pe):
                pe.wait_ge(counted, 1)
                pe.wait_ge(masks, 7)
                pe.matmul(banks[0][0:1, 0:BLOCKS + 1], ones[0:EP, :], counts[0:EP, :], start=True, stop=True).then_inc(summed, 1)

        with ExitStack() as phase:
            sem = phase_semaphores(phase)

            def pair(name):
                return [sem(f"{name}{s}") for s in range(2)]

            def tiles(name, shape):
                return [phase.enter_context(nc.sbuf_tensor(f"{name}{s}", shape, F32)) for s in range(2)]

            x_loaded, x_used = pair("x_loaded"), pair("x_used")
            var_ready, std_ready = sem("var_ready"), sem("std_ready")
            norm_ready, norm_transposed, hT_ready = pair("norm_ready"), pair("norm_transposed"), pair("hT_ready")
            qkv_ready, row_ready, row_stored = pair("qkv_ready"), pair("row_ready"), pair("row_stored")
            dve_order = sem("dve_order2")
            x_sb, norm, row = tiles("x_sb", [NB, D]), tiles("norm", [NB, D]), tiles("row", [NB, TW])
            hTs, qk = tiles("hTs", [P, 2, NB]), tiles("qk", [NB, 2 * D])
            six, two = tiles("six", [NB, 6]), tiles("two", [NB, 2])
            std, head_sum = tiles("std", [NB, 1]), tiles("head_sum", [NB, HEADS])
            qk_ps, v_ps, t_ps = banks[0:2], banks[2:4], banks[4:6]
            block = phase.enter_context(nc.Block())

            @block.sync
            def _(sp):
                with sp.Fori(0, PAIRS) as i:
                    for s in range(2):
                        sp.wait_ge(x_used[s], i + 1)
                        sp.dma_start(x_sb[s][:, :], block_rows(x, 2 * i + s)).then_inc(x_loaded[s], 16)

            @block.vector
            def _(dve):
                order = InOrder(dve, dve_order)
                for s in range(2):
                    dve.sem_inc(x_used[s], 1)
                    dve.sem_inc(row_ready[s], 1)

                def normalise(s, i):
                    dve.wait_ge(x_loaded[s], (i + 1) * 16)
                    order.step(dve.bn_stats(six[s][:, :], x_sb[s][:, :]))
                    order.step(dve.bn_aggr(two[s][:, :], six[s][:, :]))
                    dve.sem_inc(var_ready, 1)
                    dve.wait_ge(std_ready, i * 2 + s + 1)
                    order.step(dve.reciprocal(std[s][:, :], std[s][:, :]))
                    order.step(dve.tensor_scalar(norm[s][:, :], x_sb[s][:, :], two[s][:, 0:1], std[s][:, 0:1],
                                                 ALU.subtract, ALU.mult))
                    dve.sem_inc(norm_ready[s], 1)
                    dve.sem_inc(x_used[s], 1)
                    order.restart()

                def finish(s, i):
                    dve.wait_ge(qkv_ready[s], i + 1)
                    dve.wait_ge(row_stored[s], (i + 1) * 16)
                    order.step(dve.tensor_tensor(qk[s][:, :], qk_ps[s][0:NB, :], bqkv_sb[:, 0:2 * D], ALU.add))
                    order.step(dve.tensor_tensor(qk[s][:, 0:D], qk[s][:, 0:D], qk[s][:, D:2 * D], ALU.mult))
                    order.step(dve.tensor_reduce(head_sum[s][:, :], qk[s][:, 0:D].rearrange("p (h c) -> p h c", c=DH),
                                                 op=ALU.add, axis=AX.X))
                    dve.tensor_scalar(scores[:, bass.ds(2 * i + s, 1), :], head_sum[s][:, :], float(DH) ** -0.5, None, ALU.mult)
                    dve.tensor_scalar(row[s][:, D:TW], head_sum[s][:, :], float(DH) ** -0.5, None, ALU.mult)
                    order.step(dve.tensor_tensor(row[s][:, 0:D], v_ps[s][0:NB, 0:D], bqkv_sb[:, 2 * D:3 * D], ALU.add))
                    dve.sem_inc(row_ready[s], 1)
                    order.restart()

                normalise(0, 0)
                with dve.Fori(0, PAIRS - 1) as i:
                    normalise(1, i)
                    finish(0, i)
                    normalise(0, i + 1)
                    finish(1, i)
                normalise(1, PAIRS - 1)
                finish(0, PAIRS - 1)
                finish(1, PAIRS - 1)

            @block.gpsimd
            def _(pool):
                for s in range(2):
                    first_store(pool, row_stored[s])
                with pool.Fori(0, PAIRS) as i:
                    for s in range(2):
                        wait_apart(pool, row_ready[s], i + 2, 1)
                        pool.dma_start(block_rows(table0, 2 * i + s), row[s][:, :]).then_inc(row_stored[s], 16)
                for s in range(2):
                    pool.wait_ge(row_stored[s], 16 * (PAIRS + 1))

            @block.scalar
            def _(act):
                with act.Fori(0, PAIRS) as i:
                    for s in range(2):
                        act.wait_ge(var_ready, i * 2 + s + 1)
                        act.activation(std[s][:, :], two[s][:, 1:2], ACT.Sqrt, bias=eps_ln[0:NB, :]).then_inc(std_ready, 1)
                        act.wait_ge(norm_transposed[s], i + 1)
                        for k in range(2):
                            act.activation(node_columns(k, 2 * i + s), t_ps[s][:, k * NB:(k + 1) * NB], ACT.Relu)
                        act.activation(hTs[s][:, :, :].rearrange("p k n -> p (k n)"), t_ps[s][:, 0:2 * NB],
                                       ACT.Relu).then_inc(hT_ready[s], 1)

            @block.tensor
            def _(pe):
                with pe.Fori(0, PAIRS) as i:
                    for s in range(2):
                        pe.wait_ge(norm_ready[s], i + 1)
                        for k in range(2):
                            last = pe.transpose(t_ps[s][:, k * NB:(k + 1) * NB], norm[s][:, k * P:(k + 1) * P],
                                                identity[0:NB, 0:NB])
                        last.then_inc(norm_transposed[s], 1)
                        pe.wait_ge(hT_ready[s], i + 1)
                        pe.wait_ge(row_ready[s], i + 1)
                        for ps, w in ((qk_ps[s][0:NB, :], wqkv_sb[:, :, 0:2 * D]), (v_ps[s][0:NB, 0:D], wqkv_sb[:, :, 2 * D:3 * D])):
                            for k in range(2):
                                last = pe.matmul(ps, hTs[s][:, k, :], w[:, k, :], start=(k == 0), stop=(k == 1))
                        last.then_inc(qkv_ready[s], 1)

        with ExitStack() as phase:
            sem = phase_semaphores(phase)

            def pair(name):
                return [sem(f"a_{name}{s}") for s in range(2)]

            def tiles(name, shape):
                return [phase.enter_context(nc.sbuf_tensor(f"a_{name}{s}", shape, F32)) for s in range(2)]

            record_loaded, rows_gathered, round_used = pair("record_loaded"), pair("rows_gathered"), pair("round_used")
            onehot_ready, T_ready, T_copied = pair("onehot_ready"), pair("T_ready"), pair("T_copied")
            summary_ready, summary_T, scan_ready = pair("summary_ready"), pair("summary_T"), pair("scan_ready")
            carry_ready, ends_ready, max_selected = pair("carry_ready"), pair("ends_ready"), pair("max_selected")
            node_ready, rescale_ready, spread_ready = pair("node_ready"), pair("rescale_ready"), pair("spread_ready")
            shifted_ready, weights_ready, weighted = pair("shifted_ready"), pair("weights_ready"), pair("weighted")
            self_loaded, self_used, self_shifted, self_weight = pair("self_loaded"), pair("self_used"), pair("self_shifted"), pair("self_weight")
            attended, att_transposed, att_copied, projected = pair("attended"), pair("att_transposed"), pair("att_copied"), pair("projected")
            block_done = pair("block_done")
            dve_order = sem("dve_order3")

            onehotT = tiles("onehotT", [NB, T, P])
            last_flag, reset, data = tiles("last_flag", [P, T]), tiles("reset", [P, HEADS, T]), tiles("data", [P, HEADS, T])
            local, summary = tiles("local", [P, HEADS, T]), tiles("summary", [P, 2 * HEADS])
            biasT, scanned = tiles("biasT", [HEADS, P]), tiles("scanned", [HEADS, P + 1])
            ends = tiles("ends", [P, T, HEADS + 1])
            run_max, run_m, nodes = tiles("run_max", [NB, HEADS]), tiles("run_m", [NB, HEADS]), tiles("nodes", [NB, 2 * HEADS])
            tmp8, none_bias = tiles("tmp8", [NB, HEADS]), tiles("none_bias", [NB, 1])
            rescale, alpha = tiles("rescale", [NB, HEADS]), tiles("alpha", [P, T, HEADS])
            alpha2, weight = tiles("alpha2", [P, T, HEADS]), tiles("weight", [P, T, HEADS])
            acc, self_row, selfw = tiles("acc", [NB, TW]), tiles("self_row", [NB, D]), tiles("selfw", [NB, HEADS])
            attT = tiles("attT", [P, 2, NB])
            turn_ps, acc_ps, mix_ps, node_ps = banks[0:2], banks[2:4], banks[4:6], banks[6:8]
            CHUNKS = [(c, min(c + 4, T)) for c in range(0, T, 4)]
            block = phase.enter_context(nc.Block())

            def edge_range(engine, b):
                lo = engine.value_load(first_edge[0:1, bass.ds(b, 1)], min_val=0, max_val=E)
                hi = engine.value_load(first_edge[0:1, bass.ds(b + 1, 1)], min_val=0, max_val=E)
                return lo, hi

            def counters(engine, name):
                regs = [engine.alloc_register(f"{name}{s}") for s in range(2)]
                for r in regs:
                    engine.reg_mov(r, 0)
                return regs

            def next_round(engine, reg):
                engine.reg_add(reg, reg, 1)
                return engine.snap(reg, min_val=1, max_val=4 * BLOCKS)

            @block.sync
            def _(sp):
                rounds = counters(sp, "sp_rounds")
                with sp.Fori(0, PAIRS) as i:
                    for s in range(2):
                        lo, hi = edge_range(sp, 2 * i + s)
                        with sp.Fori(lo, hi, RE) as at:
                            r = next_round(sp, rounds[s])
                            sp.wait_ge(round_used[s], r)
                            sp.dma_start(record[s][:, :, :].rearrange("p j c -> p (j c)"),
                                         edges[bass.ds(at, RE), :].rearrange("(p j) c -> p (j c)", j=T)).then_inc(record_loaded[s], 16)
                        sp.wait_ge(self_used[s], i + 1)
                        sp.dma_start(self_row[s][:, :], table0[bass.ds((2 * i + s) * NB, NB), 0:D]).then_inc(self_loaded[s], 16)

            @block.gpsimd
            def _(pool):
                rounds = counters(pool, "pool_rounds")
                with pool.Fori(0, PAIRS) as i:
                    for s in range(2):
                        lo, hi = edge_range(pool, 2 * i + s)
                        with pool.Fori(lo, hi, RE) as at:
                            r = next_round(pool, rounds[s])
                            pool.wait_ge(round_used[s], r)
                            wait_apart(pool, record_loaded[s], r * 16, 16)
                            for j in range(T):
                                pool.indirect_dma_start(
                                    out=gathered0[s][:, j * TW:(j + 1) * TW], out_offset=None, in_=table0,
                                    in_offset=bass.IndirectOffsetOnAxis(ap=record[s][:, j, 0:1], axis=0),
                                ).then_inc(rows_gathered[s], 16)

            @block.vector
            def _(dve):
                order = InOrder(dve, dve_order)
                rounds = counters(dve, "dve_rounds")
                for s in range(2):
                    order.step(dve.memset(scanned[s][:, 0:1], -BIG))
                    dve.sem_inc(self_used[s], 1)
                    dve.sem_inc(block_done[s], 1)
                order.restart()

                def heads(t, n=DH):
                    return t.unsqueeze(2).broadcast_to([NB, HEADS, n])

                def fold(s, used):
                    dve.wait_ge(rescale_ready[s], used)
                    dve.wait_ge(round_used[s], used + 1)
                    order.step(dve.tensor_tensor(acc[s][:, 0:D].rearrange("p (h c) -> p h c", c=DH),
                                                 acc[s][:, 0:D].rearrange("p (h c) -> p h c", c=DH),
                                                 heads(rescale[s][:, :]), ALU.mult))
                    order.step(dve.tensor_tensor(acc[s][:, D:TW], acc[s][:, D:TW], rescale[s][:, :], ALU.mult))
                    order.step(dve.tensor_tensor(acc[s][:, :], acc[s][:, :], acc_ps[s][0:NB, 0:TW], ALU.add))

                def lrelu(out_, in_):
                    order.step(dve.scalar_tensor_tensor(out_, in_, SLOPE, in_, ALU.mult, ALU.max))

                def round_body(s, b, at, lo):
                    r_old = dve.snap(rounds[s], min_val=0, max_val=4 * BLOCKS)
                    with dve.If(at > lo):
                        fold(s, r_old)
                        order.restart()
                    r = next_round(dve, rounds[s])
                    rec = record[s][:, :, :].bitcast(F32)
                    rows = gathered0[s].rearrange("p (j c) -> p j c", c=TW)
                    dve.wait_ge(record_loaded[s], r * 16)
                    dve.wait_ge(round_used[s], r)
                    order.step(dve.tensor_scalar(relative[s][:, :], rec[:, :, 1], minus_base[:, bass.ds(b, 1)], None, ALU.add))
                    dve.tensor_tensor(onehot[s][:, :, :], column[:, :].unsqueeze(1).broadcast_to([P, T, NB]),
                                      relative[s][:, :].unsqueeze(2).broadcast_to([P, T, NB]), ALU.is_equal).then_inc(onehot_ready[s], 1)
                    order.step(dve.tensor_copy(reset[s][:, :, :], rec[:, :, 2].unsqueeze(1).broadcast_to([P, HEADS, T])))
                    order.step(dve.memset(reset[s][:, :, 0], -BIG))
                    order.step(dve.tensor_reduce(summary[s][:, HEADS:HEADS + 1], rec[:, :, 2], op=ALU.min, axis=AX.X))
                    order.step(dve.tensor_copy(summary[s][:, HEADS + 1:2 * HEADS],
                                               summary[s][:, HEADS:HEADS + 1].broadcast_to([P, HEADS - 1])))
                    order.step(dve.tensor_tensor(last_flag[s][:, :], rec[:, :, 3], end_mask[:, :], ALU.max))
                    dve.wait_ge(rows_gathered[s], r * GATHERED)
                    order.step(dve.tensor_copy(data[s][:, :, :], rows[:, :, D:TW].rearrange("p j h -> p h j")))
                    flat = "p h j -> p (h j)"
                    order.step(dve.tensor_tensor_scan(local[s][:, :, :].rearrange(flat), reset[s][:, :, :].rearrange(flat),
                                                      data[s][:, :, :].rearrange(flat), -BIG, ALU.add, ALU.max))
                    dve.tensor_copy(summary[s][:, 0:HEADS], local[s][:, :, T - 1]).then_inc(summary_ready[s], 1)
                    dve.wait_ge(summary_T[s], r)
                    order.step(dve.tensor_copy(biasT[s][:, :], mix_ps[s][0:HEADS, P:2 * P]))
                    dve.tensor_tensor_scan(scanned[s][:, 1:P + 1], biasT[s][:, :], mix_ps[s][0:HEADS, 0:P],
                                           -BIG, ALU.add, ALU.max).then_inc(scan_ready[s], 1)
                    dve.wait_ge(carry_ready[s], r)
                    order.step(dve.scalar_tensor_tensor(data[s][:, :, 0], node_ps[s][:, 288:288 + HEADS], rec[:, 0, 2:3],
                                                        data[s][:, :, 0], ALU.add, ALU.max))
                    order.step(dve.tensor_tensor_scan(local[s][:, :, :].rearrange(flat), reset[s][:, :, :].rearrange(flat),
                                                      data[s][:, :, :].rearrange(flat), -BIG, ALU.add, ALU.max))
                    order.step(dve.tensor_copy(ends[s][:, :, HEADS], last_flag[s][:, :]))
                    dve.tensor_tensor(ends[s][:, :, 0:HEADS].rearrange("p j h -> p h j"), local[s][:, :, :],
                                      last_flag[s][:, :].unsqueeze(1).broadcast_to([P, HEADS, T]), ALU.mult).then_inc(ends_ready[s], 1)
                    own = nodes[s][:, 0:HEADS]
                    dve.wait_ge(max_selected[s], r)
                    order.step(dve.tensor_scalar(none_bias[s][:, :], node_ps[s][0:NB, 272 + HEADS:273 + HEADS], BIG, -BIG,
                                                 ALU.mult, ALU.add))
                    order.step(dve.scalar_tensor_tensor(run_max[s][:, :], node_ps[s][0:NB, 272:272 + HEADS], none_bias[s][:, :],
                                                        run_max[s][:, :], ALU.add, ALU.max))
                    order.step(dve.tensor_tensor(tmp8[s][:, :], run_max[s][:, :], own, ALU.add))
                    lrelu(nodes[s][:, HEADS:2 * HEADS], tmp8[s][:, :])
                    dve.sem_inc(node_ready[s], 1)
                    order.step(dve.tensor_tensor(rescale[s][:, :], run_m[s][:, :], nodes[s][:, HEADS:2 * HEADS], ALU.subtract))
                    order.step(dve.tensor_copy(run_m[s][:, :], nodes[s][:, HEADS:2 * HEADS]))
                    dve.wait_ge(spread_ready[s], r)
                    by_edge = node_ps[s][:, 0:T * 2 * HEADS].rearrange("p (j c) -> p j c", c=2 * HEADS)
                    order.step(dve.tensor_tensor(alpha[s][:, :, :], by_edge[:, :, 0:HEADS], rows[:, :, D:TW], ALU.add))
                    lrelu(alpha2[s][:, :, :], alpha[s][:, :, :])
                    order.step(dve.tensor_tensor(alpha[s][:, :, :], alpha2[s][:, :, :], by_edge[:, :, HEADS:2 * HEADS], ALU.subtract))
                    dve.tensor_scalar(alpha2[s][:, :, :], alpha[s][:, :, :], 0.0, None, ALU.min).then_inc(shifted_ready[s], 1)
                    dve.wait_ge(weights_ready[s], r)
                    values = rows[:, :, 0:D].rearrange("p j (h c) -> p j h c", c=DH)
                    order.step(dve.tensor_tensor(values, values, weight[s][:, :, :].unsqueeze(3).broadcast_to([P, T, HEADS, DH]), ALU.mult))
                    order.step(dve.tensor_copy(rows[:, :, D:TW], weight[s][:, :, :]))
                    dve.sem_inc(weighted[s], 1)
                    order.restart()

                def rounds_of(s, b):
                    own = nodes[s][:, 0:HEADS]
                    order.step(dve.tensor_copy(own, scores[:, bass.ds(b, 1), :].rearrange("p o h -> p (o h)")))
                    order.step(dve.tensor_copy(run_max[s][:, :], own))
                    order.step(dve.tensor_tensor(tmp8[s][:, :], own, own, ALU.add))
                    lrelu(run_m[s][:, :], tmp8[s][:, :])
                    order.step(dve.memset(acc[s][:, :], 0.0))
                    order.restart()
                    lo, hi = edge_range(dve, b)
                    with dve.Fori(lo, hi, RE) as at:
                        round_body(s, b, at, lo)

                def finish(s, i):
                    r = dve.snap(rounds[s], min_val=1, max_val=4 * BLOCKS)
                    fold(s, r)
                    own = nodes[s][:, 0:HEADS]
                    order.step(dve.tensor_tensor(tmp8[s][:, :], own, own, ALU.add))
                    lrelu(selfw[s][:, :], tmp8[s][:, :])
                    order.step(dve.tensor_tensor(tmp8[s][:, :], selfw[s][:, :], run_m[s][:, :], ALU.subtract))
                    dve.sem_inc(self_shifted[s], 1)
                    dve.wait_ge(self_weight[s], i + 1)
                    dve.wait_ge(self_loaded[s], (i + 1) * 16)
                    rows = self_row[s][:, :].rearrange("p (h c) -> p h c", c=DH)
                    order.step(dve.tensor_tensor(rows, rows, heads(selfw[s][:, :]), ALU.mult))
                    order.step(dve.tensor_tensor(self_row[s][:, :], self_row[s][:, :], acc[s][:, 0:D], ALU.add))
                    order.step(dve.tensor_tensor(selfw[s][:, :], selfw[s][:, :], acc[s][:, D:TW], ALU.add))
                    order.step(dve.reciprocal(tmp8[s][:, :], selfw[s][:, :]))
                    order.step(dve.tensor_tensor(rows, rows, heads(tmp8[s][:, :]), ALU.mult))
                    dve.sem_inc(attended[s], 1)
                    dve.wait_ge(projected[s], i + 1)
                    dve.sem_inc(self_used[s], 1)
                    b = 2 * i + s
                    for m in range(2):
                        order.step(dve.scalar_tensor_tensor(node_columns(m, b), acc_ps[s][:, m * NB:(m + 1) * NB], boT[:, m:m + 1],
                                                            node_columns(m, b), ALU.add, ALU.add))
                        order.step(dve.bn_stats(stats[:, m, bass.ds(b, 1), :].rearrange("p o c -> p (o c)"), node_columns(m, b)))
                    dve.sem_inc(block_done[s], 1)
                    order.restart()

                rounds_of(0, 0)
                with dve.Fori(0, PAIRS - 1) as i:
                    rounds_of(1, 2 * i + 1)
                    finish(0, i)
                    rounds_of(0, 2 * i + 2)
                    finish(1, i)
                rounds_of(1, BLOCKS - 1)
                finish(0, PAIRS - 1)
                finish(1, PAIRS - 1)

            @block.scalar
            def _(act):
                rounds = counters(act, "act_rounds")

                def rounds_of(s, b):
                    lo, hi = edge_range(act, b)
                    with act.Fori(lo, hi, RE) as at:
                        before = act.snap(rounds[s], min_val=0, max_val=4 * BLOCKS)
                        r = next_round(act, rounds[s])
                        for c, (j0, j1) in enumerate(CHUNKS):
                            act.wait_ge(T_ready[s], before * len(CHUNKS) + c + 1)
                            act.activation(onehotT[s][:, j0:j1, :].rearrange("p j e -> p (j e)"),
                                           turn_ps[c % 2][0:NB, 0:(j1 - j0) * P], ACT.Copy).then_inc(T_copied[s], 1)
                        act.wait_ge(shifted_ready[s], r)
                        act.activation(weight[s][:, :, :].rearrange("p j h -> p (j h)"),
                                       alpha2[s][:, :, :].rearrange("p j h -> p (j h)"), ACT.Exp).then_inc(weights_ready[s], 1)
                        act.activation(rescale[s][:, :], rescale[s][:, :], ACT.Exp).then_inc(rescale_ready[s], 1)

                def finish(s, i):
                    act.wait_ge(self_shifted[s], i + 1)
                    act.activation(selfw[s][:, :], tmp8[s][:, :], ACT.Exp).then_inc(self_weight[s], 1)
                    act.wait_ge(att_transposed[s], i + 1)
                    act.activation(attT[s][:, :, :].rearrange("p k n -> p (k n)"), mix_ps[s][:, 256:256 + 2 * NB],
                                   ACT.Copy).then_inc(att_copied[s], 1)

                rounds_of(0, 0)
                with act.Fori(0, PAIRS - 1) as i:
                    rounds_of(1, 2 * i + 1)
                    finish(0, i)
                    rounds_of(0, 2 * i + 2)
                    finish(1, i)
                rounds_of(1, BLOCKS - 1)
                finish(0, PAIRS - 1)
                finish(1, PAIRS - 1)

            @block.tensor
            def _(pe):
                rounds = counters(pe, "pe_rounds")
                for s in range(2):
                    pe.sem_inc(round_used[s], 1)

                def rounds_of(s, b, i):
                    rows = gathered0[s].rearrange("p (j c) -> p j c", c=TW)
                    lo, hi = edge_range(pe, b)
                    wait_apart(pe, block_done[s], i + 1, 1)
                    with pe.Fori(lo, hi, RE) as at:
                        before = pe.snap(rounds[s], min_val=0, max_val=4 * BLOCKS)
                        r = next_round(pe, rounds[s])
                        pe.wait_ge(onehot_ready[s], r)
                        for c, (j0, j1) in enumerate(CHUNKS):
                            if c >= 2:
                                pe.wait_ge(T_copied[s], before * len(CHUNKS) + c - 1)
                            for j in range(j0, j1):
                                last = pe.transpose(turn_ps[c % 2][0:NB, (j - j0) * P:(j - j0 + 1) * P], onehot[s][:, j, :], identity[:, :])
                            last.then_inc(T_ready[s], 1)
                        pe.wait_ge(summary_ready[s], r)
                        pe.transpose(mix_ps[s][0:HEADS, 0:P], summary[s][:, 0:HEADS], identity[:, :])
                        pe.transpose(mix_ps[s][0:HEADS, P:2 * P], summary[s][:, HEADS:2 * HEADS], identity[:, :]).then_inc(summary_T[s], 1)
                        wait_apart(pe, scan_ready[s], r, 1)
                        pe.transpose(node_ps[s][:, 288:288 + HEADS], scanned[s][:, 0:P], identity[0:HEADS, 0:HEADS]).then_inc(carry_ready[s], 1)
                        pe.wait_ge(ends_ready[s], r)
                        for j in range(T):
                            last = pe.matmul(node_ps[s][0:NB, 272:273 + HEADS], onehot[s][:, j, :], ends[s][:, j, :],
                                             start=(j == 0), stop=(j == T - 1))
                        last.then_inc(max_selected[s], 1)
                        pe.wait_ge(node_ready[s], r)
                        pe.wait_ge(T_copied[s], r * len(CHUNKS))
                        for j in range(T):
                            last = pe.matmul(node_ps[s][:, j * 2 * HEADS:(j + 1) * 2 * HEADS], onehotT[s][:, j, :], nodes[s][:, :],
                                             start=True, stop=True)
                        last.then_inc(spread_ready[s], 1)
                        pe.wait_ge(weighted[s], r)
                        for j in range(T):
                            last = pe.matmul(acc_ps[s][0:NB, 0:TW], onehot[s][:, j, :], rows[:, j, :], start=(j == 0), stop=(j == T - 1))
                        last.then_inc(round_used[s], 1)

                def finish(s, i):
                    pe.wait_ge(attended[s], i + 1)
                    for k in range(2):
                        last = pe.transpose(mix_ps[s][:, 256 + k * NB:256 + (k + 1) * NB], self_row[s][:, k * P:(k + 1) * P],
                                            identity[0:NB, 0:NB])
                    last.then_inc(att_transposed[s], 1)
                    pe.wait_ge(att_copied[s], i + 1)
                    for m in range(2):
                        for k in range(2):
                            last = pe.matmul(acc_ps[s][:, m * NB:(m + 1) * NB], wo_sb[:, k, m * P:(m + 1) * P], attT[s][:, k, :],
                                             start=(k == 0), stop=(k == 1))
                    last.then_inc(projected[s], 1)

                rounds_of(0, 0, 0)
                with pe.Fori(0, PAIRS - 1) as i:
                    rounds_of(1, 2 * i + 1, i)
                    finish(0, i)
                    rounds_of(0, 2 * i + 2, i + 1)
                    finish(1, i)
                rounds_of(1, BLOCKS - 1, PAIRS - 1)
                finish(0, PAIRS - 1)
                finish(1, PAIRS - 1)

        def norm_affine(dve, order, n, variance_ready, spread_ready):
            for m in range(2):
                order.step(dve.bn_aggr(moments[:, m, :], stats[:, m, :, :].rearrange("p b c -> p (b c)")))
            dve.sem_inc(variance_ready, 1)
            dve.wait_ge(spread_ready, 1)
            order.step(dve.reciprocal(spread[:, :], spread[:, :]))
            order.step(dve.tensor_tensor(gain[:, :], spread[:, :], bnT[:, 2 * n, :], ALU.mult))
            order.step(dve.tensor_tensor(shift[:, :], moments[:, :, 0], gain[:, :], ALU.mult))
            order.step(dve.tensor_tensor(shift[:, :], bnT[:, 2 * n + 1, :], shift[:, :], ALU.subtract))

        with ExitStack() as phase:
            sem = phase_semaphores(phase)

            def pair(name):
                return [sem(f"f_{name}{s}") for s in range(2)]

            variance_ready, spread_ready = sem("f_variance"), sem("f_spread")
            normed, up_ready, hidden_ready, down_ready, out_read = (pair("normed"), pair("up_ready"), pair("hidden_ready"),
                                                                    pair("down_ready"), pair("out_read"))
            dve_order = sem("dve_order4")
            hidden = [phase.enter_context(nc.sbuf_tensor(f"hidden{s}", [P, 4, NB], F32)) for s in range(2)]
            up_ps, down_ps = banks[0:2], banks[2:4]
            block = phase.enter_context(nc.Block())

            @block.vector
            def _(dve):
                order = InOrder(dve, dve_order)
                norm_affine(dve, order, 0, variance_ready, spread_ready)
                order.restart()
                for s in range(2):
                    dve.sem_inc(out_read[s], 1)

                def normalise(s, b):
                    for m in range(2):
                        order.step(dve.tensor_scalar(node_columns(m, b), node_columns(m, b), gain[:, m:m + 1], shift[:, m:m + 1],
                                                     ALU.mult, ALU.add))
                    dve.sem_inc(normed[s], 1)
                    order.restart()

                def finish(s, i):
                    b = 2 * i + s
                    dve.wait_ge(down_ready[s], i + 1)
                    for m in range(2):
                        order.step(dve.scalar_tensor_tensor(node_columns(m, b), down_ps[s][:, m * NB:(m + 1) * NB], b2T[:, m:m + 1],
                                                            node_columns(m, b), ALU.add, ALU.add))
                        order.step(dve.bn_stats(stats[:, m, bass.ds(b, 1), :].rearrange("p o c -> p (o c)"), node_columns(m, b)))
                    dve.sem_inc(out_read[s], 1)
                    order.restart()

                normalise(0, 0)
                with dve.Fori(0, PAIRS - 1) as i:
                    normalise(1, 2 * i + 1)
                    finish(0, i)
                    normalise(0, 2 * i + 2)
                    finish(1, i)
                normalise(1, BLOCKS - 1)
                finish(0, PAIRS - 1)
                finish(1, PAIRS - 1)

            @block.scalar
            def _(act):
                act.wait_ge(variance_ready, 1)
                act.activation(spread[:, :], moments[:, :, 1], ACT.Sqrt, bias=eps_bn[:, :]).then_inc(spread_ready, 1)
                with act.Fori(0, PAIRS) as i:
                    for s in range(2):
                        act.wait_ge(up_ready[s], i + 1)
                        for m in range(4):
                            last = act.activation(hidden[s][:, m, :], up_ps[s][:, m * NB:(m + 1) * NB], ACT.Relu, bias=b1T[:, m:m + 1])
                        last.then_inc(hidden_ready[s], 1)

            @block.tensor
            def _(pe):
                def up(s, i):
                    pe.wait_ge(normed[s], i + 1)
                    for m in range(4):
                        for k in range(2):
                            last = pe.matmul(up_ps[s][:, m * NB:(m + 1) * NB], wf1_sb[:, k, m * P:(m + 1) * P],
                                             node_columns(k, 2 * i + s), start=(k == 0), stop=(k == 1))
                    last.then_inc(up_ready[s], 1)

                def down(s, i):
                    pe.wait_ge(hidden_ready[s], i + 1)
                    pe.wait_ge(out_read[s], i + 1)
                    for m in range(2):
                        for k in range(4):
                            last = pe.matmul(down_ps[s][:, m * NB:(m + 1) * NB], wf2_sb[:, k, m * P:(m + 1) * P], hidden[s][:, k, :],
                                             start=(k == 0), stop=(k == 3))
                    last.then_inc(down_ready[s], 1)

                up(0, 0)
                with pe.Fori(0, PAIRS - 1) as i:
                    up(1, i)
                    down(0, i)
                    up(0, i + 1)
                    down(1, i)
                up(1, PAIRS - 1)
                down(0, PAIRS - 1)
                down(1, PAIRS - 1)

        with ExitStack() as phase:
            sem = phase_semaphores(phase)

            def pair(name):
                return [sem(f"g_{name}{s}") for s in range(2)]

            def tiles(name, shape):
                return [phase.enter_context(nc.sbuf_tensor(f"g_{name}{s}", shape, F32)) for s in range(2)]

            variance_ready, spread_ready = sem("g_variance"), sem("g_spread")
            x_loaded, x_used, normed, turned = pair("x_loaded"), pair("x_used"), pair("normed"), pair("turned")
            var_ready, std_ready = pair("var_ready"), pair("std_ready")
            x1_ready, x1_stored, centred, h_ready, h_stored = (pair("x1_ready"), pair("x1_stored"), pair("centred"),
                                                               pair("h_ready"), pair("h_stored"))
            dve_order = sem("dve_order5")
            x_sb, yT, x1_sb, norm, h_sb = (tiles("x_sb", [NB, D]), tiles("yT", [P, 2, NB]), tiles("x1_sb", [NB, D]),
                                           tiles("norm", [NB, D]), tiles("h_sb", [NB, D]))
            six, two, std = tiles("six", [NB, 6]), tiles("two", [NB, 2]), tiles("std", [NB, 1])
            y_ps = banks[0:2]
            block = phase.enter_context(nc.Block())

            @block.sync
            def _(sp):
                with sp.Fori(0, PAIRS) as i:
                    for s in range(2):
                        sp.wait_ge(x_used[s], i + 1)
                        sp.dma_start(x_sb[s][:, :], block_rows(x, 2 * i + s)).then_inc(x_loaded[s], 16)

            @block.vector
            def _(dve):
                order = InOrder(dve, dve_order)
                norm_affine(dve, order, 1, variance_ready, spread_ready)
                order.restart()
                for s in range(2):
                    dve.sem_inc(x_used[s], 1)
                    dve.sem_inc(std_ready[s], 1)

                def affine(s, i):
                    for m in range(2):
                        order.step(dve.tensor_scalar(yT[s][:, m, :], node_columns(m, 2 * i + s), gain[:, m:m + 1], shift[:, m:m + 1],
                                                     ALU.mult, ALU.add))
                    dve.sem_inc(normed[s], 1)
                    order.restart()

                def residual(s, i):
                    dve.wait_ge(turned[s], i + 1)
                    dve.wait_ge(x_loaded[s], (i + 1) * 16)
                    dve.wait_ge(x1_stored[s], (i + 1) * 16)
                    order.step(dve.tensor_tensor(x1_sb[s][:, :], y_ps[s][0:NB, 0:D], x_sb[s][:, :], ALU.add))
                    dve.sem_inc(x1_ready[s], 1)
                    dve.sem_inc(x_used[s], 1)
                    order.step(dve.bn_stats(six[s][:, :], x1_sb[s][:, :]))
                    order.step(dve.bn_aggr(two[s][:, :], six[s][:, :]))
                    dve.sem_inc(var_ready[s], 1)
                    order.restart()

                def centre(s, i):
                    dve.wait_ge(std_ready[s], i + 2)
                    dve.wait_ge(h_ready[s], i + 1)
                    order.step(dve.reciprocal(std[s][:, :], std[s][:, :]))
                    order.step(dve.tensor_scalar(norm[s][:, :], x1_sb[s][:, :], two[s][:, 0:1], std[s][:, 0:1],
                                                 ALU.subtract, ALU.mult))
                    dve.sem_inc(centred[s], 1)
                    order.restart()

                affine(0, 0)
                affine(1, 0)
                residual(0, 0)
                with dve.Fori(0, PAIRS - 1) as i:
                    residual(1, i)
                    affine(0, i + 1)
                    centre(0, i)
                    affine(1, i + 1)
                    residual(0, i + 1)
                    centre(1, i)
                residual(1, PAIRS - 1)
                centre(0, PAIRS - 1)
                centre(1, PAIRS - 1)

            @block.scalar
            def _(act):
                for s in range(2):
                    act.sem_inc(h_ready[s], 1)
                act.wait_ge(variance_ready, 1)
                act.activation(spread[:, :], moments[:, :, 1], ACT.Sqrt, bias=eps_bn[:, :]).then_inc(spread_ready, 1)

                def deviation(s, i):
                    act.wait_ge(var_ready[s], i + 1)
                    act.activation(std[s][:, :], two[s][:, 1:2], ACT.Sqrt, bias=eps_ln[0:NB, :]).then_inc(std_ready[s], 1)

                def rectify(s, i):
                    act.wait_ge(centred[s], i + 1)
                    act.wait_ge(h_stored[s], (i + 1) * 16)
                    act.activation(h_sb[s][:, :], norm[s][:, :], ACT.Relu).then_inc(h_ready[s], 1)

                deviation(0, 0)
                with act.Fori(0, PAIRS - 1) as i:
                    deviation(1, i)
                    rectify(0, i)
                    deviation(0, i + 1)
                    rectify(1, i)
                deviation(1, PAIRS - 1)
                rectify(0, PAIRS - 1)
                rectify(1, PAIRS - 1)

            @block.gpsimd
            def _(pool):
                for s in range(2):
                    first_store(pool, x1_stored[s])
                    first_store(pool, h_stored[s])
                with pool.Fori(0, PAIRS) as i:
                    for s in range(2):
                        wait_apart(pool, x1_ready[s], i + 1, 1)
                        pool.dma_start(block_rows(x1, 2 * i + s), x1_sb[s][:, :]).then_inc(x1_stored[s], 16)
                        wait_apart(pool, h_ready[s], i + 2, 1)
                        pool.dma_start(block_rows(table1, 2 * i + s), h_sb[s][:, :]).then_inc(h_stored[s], 16)
                for s in range(2):
                    pool.wait_ge(x1_stored[s], 16 * (PAIRS + 1))
                    pool.wait_ge(h_stored[s], 16 * (PAIRS + 1))

            @block.tensor
            def _(pe):
                with pe.Fori(0, PAIRS) as i:
                    for s in range(2):
                        pe.wait_ge(normed[s], i + 1)
                        for m in range(2):
                            last = pe.transpose(y_ps[s][0:NB, m * P:(m + 1) * P], yT[s][:, m, :], identity[:, :])
                        last.then_inc(turned[s], 1)

        def graph_layer(n, table, w):
            last_layer = n == 2
            k_tiles = w // P
            with ExitStack() as phase:
                sem = phase_semaphores(phase)

                def pair(name):
                    return [sem(f"l{n}_{name}{s}") for s in range(2)]

                def tiles(name, shape):
                    return [phase.enter_context(nc.sbuf_tensor(f"l{n}_{name}{s}", shape, F32)) for s in range(2)]

                record_loaded, rows_gathered, round_used = pair("record_loaded"), pair("rows_gathered"), pair("round_used")
                onehot_ready, sums_ready, sums_read = pair("onehot_ready"), pair("sums_ready"), pair("sums_read")
                own_loaded, own_used, sum_turned, zT_ready = pair("own_loaded"), pair("own_used"), pair("sum_turned"), pair("zT_ready")
                product, hidden_ready, result_read, result_ready, stored = (pair("product"), pair("hidden_ready"),
                                                                            pair("result_read"), pair("result_ready"), pair("stored"))
                hidden_product = pair("hidden_product")
                dve_order = sem(f"dve_order{6 + n}")
                own = tiles("own", [NB, w])
                z = tiles("z", [NB, w])
                zT = tiles("zT", [P, 4, NB]) if not last_layer else None
                x1_sb = tiles("x1_sb", [NB, D]) if last_layer else None
                hiddenT = tiles("hiddenT", [P, 4, NB]) if n == 1 else None
                width = (HID, D, D)[n]
                z2 = tiles("z2", [NB, HID]) if n == 0 else None
                result = tiles("result", [NB, width])
                sum_ps, turn_ps, product_ps, hidden_ps = banks[0:2], banks[2:4], banks[4:6], banks[6:8]
                target = (table2, table3, out)[n]
                block = phase.enter_context(nc.Block())

                def edge_range(engine, b):
                    lo = engine.value_load(first_edge[0:1, bass.ds(b, 1)], min_val=0, max_val=E)
                    hi = engine.value_load(first_edge[0:1, bass.ds(b + 1, 1)], min_val=0, max_val=E)
                    return lo, hi

                def counters(engine, name):
                    regs = [engine.alloc_register(f"{name}{n}_{s}") for s in range(2)]
                    for r in regs:
                        engine.reg_mov(r, 0)
                    return regs

                def next_round(engine, reg):
                    engine.reg_add(reg, reg, 1)
                    return engine.snap(reg, min_val=1, max_val=4 * BLOCKS)

                own_loads = 32 if last_layer else 16

                @block.sync
                def _(sp):
                    rounds = counters(sp, "sp_r")
                    with sp.Fori(0, PAIRS) as i:
                        for s in range(2):
                            lo, hi = edge_range(sp, 2 * i + s)
                            with sp.Fori(lo, hi, RE) as at:
                                r = next_round(sp, rounds[s])
                                sp.wait_ge(round_used[s], r)
                                sp.dma_start(record[s][:, :, :].rearrange("p j c -> p (j c)"),
                                             edges[bass.ds(at, RE), :].rearrange("(p j) c -> p (j c)", j=T)).then_inc(record_loaded[s], 16)
                            sp.wait_ge(own_used[s], i + 1)
                            sp.dma_start(own[s][:, :], block_rows(table, 2 * i + s)).then_inc(own_loaded[s], 16)
                            if last_layer:
                                sp.dma_start(x1_sb[s][:, :], block_rows(x1, 2 * i + s)).then_inc(own_loaded[s], 16)

                @block.gpsimd
                def _(pool):
                    rounds = counters(pool, "pool_r")
                    with pool.Fori(0, PAIRS) as i:
                        for s in range(2):
                            lo, hi = edge_range(pool, 2 * i + s)
                            with pool.Fori(lo, hi, RE) as at:
                                r = next_round(pool, rounds[s])
                                pool.wait_ge(round_used[s], r)
                                wait_apart(pool, record_loaded[s], r * 16, 16)
                                for j in range(T):
                                    pool.indirect_dma_start(
                                        out=gathered(s, w)[:, j * w:(j + 1) * w], out_offset=None, in_=table,
                                        in_offset=bass.IndirectOffsetOnAxis(ap=record[s][:, j, 0:1], axis=0),
                                    ).then_inc(rows_gathered[s], 16)

                @block.vector
                def _(dve):
                    order = InOrder(dve, dve_order)
                    rounds = counters(dve, "dve_r")
                    for s in range(2):
                        dve.sem_inc(own_used[s], 1)
                        dve.sem_inc(sums_read[s], 1)
                        dve.sem_inc(result_read[s], 1)

                    def rounds_of(s, b):
                        lo, hi = edge_range(dve, b)
                        with dve.Fori(lo, hi, RE) as at:
                            r = next_round(dve, rounds[s])
                            dve.wait_ge(record_loaded[s], r * 16)
                            dve.wait_ge(round_used[s], r)
                            order.step(dve.tensor_scalar(relative[s][:, :], record[s][:, :, 1].bitcast(F32),
                                                         minus_base[:, bass.ds(b, 1)], None, ALU.add))
                            dve.tensor_tensor(onehot[s][:, :, :], column[:, :].unsqueeze(1).broadcast_to([P, T, NB]),
                                              relative[s][:, :].unsqueeze(2).broadcast_to([P, T, NB]),
                                              ALU.is_equal).then_inc(onehot_ready[s], 1)
                            order.restart()

                    def finish(s, i):
                        dve.wait_ge(sums_ready[s], i + 1)
                        dve.wait_ge(own_loaded[s], (i + 1) * own_loads)
                        order.step(dve.scalar_tensor_tensor(z[s][:, :], own[s][:, :], one_eps[0:NB, n:n + 1],
                                                            sum_ps[s][0:NB, 0:w], ALU.mult, ALU.add))
                        dve.sem_inc(sums_read[s], 1)
                        if last_layer:
                            order.step(dve.tensor_tensor(z[s][:, :], z[s][:, :], c3_sb[:, :], ALU.add))
                            dve.wait_ge(stored[s], (i + 1) * 16)
                            order.step(dve.tensor_tensor(result[s][:, :], z[s][:, :], x1_sb[s][:, :], ALU.add))
                            dve.sem_inc(result_ready[s], 1)
                            dve.sem_inc(own_used[s], 1)
                        else:
                            dve.sem_inc(own_used[s], 1)
                        if n == 0:
                            dve.wait_ge(product[s], i + 1)
                            dve.wait_ge(result_ready[s], i + 1)
                            order.step(dve.tensor_tensor(z2[s][:, :], product_ps[s][0:NB, :], c1_sb[:, :], ALU.add))
                            dve.sem_inc(result_read[s], 1)
                        order.restart()

                    rounds_of(0, 0)
                    with dve.Fori(0, PAIRS - 1) as i:
                        rounds_of(1, 2 * i + 1)
                        finish(0, i)
                        rounds_of(0, 2 * i + 2)
                        finish(1, i)
                    rounds_of(1, BLOCKS - 1)
                    finish(0, PAIRS - 1)
                    finish(1, PAIRS - 1)

                @block.scalar
                def _(act):
                    if n == 0:
                        for s in range(2):
                            act.sem_inc(result_ready[s], 1)
                    for s in range(2):
                        first_store(act, stored[s])

                    def finish(s, i):
                        if not last_layer:
                            act.wait_ge(sum_turned[s], i + 1)
                            act.activation(zT[s][:, 0:k_tiles, :].rearrange("p k n -> p (k n)"), turn_ps[s][:, 0:k_tiles * NB],
                                           ACT.Copy).then_inc(zT_ready[s], 1)
                        if n == 0:
                            act.wait_ge(result_read[s], i + 2)
                            act.wait_ge(stored[s], (i + 1) * 16)
                            act.activation(result[s][:, :], z2[s][:, :], ACT.Relu).then_inc(result_ready[s], 1)
                            act.wait_ge(result_ready[s], i + 2)
                        if n == 1:
                            act.wait_ge(hidden_product[s], i + 1)
                            for m in range(4):
                                last = act.activation(hiddenT[s][:, m, :], hidden_ps[s][:, m * NB:(m + 1) * NB], ACT.Relu,
                                                      bias=c2T[:, m:m + 1])
                            last.then_inc(hidden_ready[s], 1)
                            act.wait_ge(product[s], i + 1)
                            act.wait_ge(stored[s], (i + 1) * 16)
                            act.activation(result[s][:, :], product_ps[s][0:NB, 0:D], ACT.Copy).then_inc(result_ready[s], 1)
                            act.wait_ge(result_ready[s], i + 1)
                        if last_layer:
                            act.wait_ge(result_ready[s], i + 1)
                        act.dma_start(block_rows(target, 2 * i + s), result[s][:, :]).then_inc(stored[s], 16)

                    with act.Fori(0, PAIRS) as i:
                        finish(0, i)
                        finish(1, i)
                    for s in range(2):
                        act.wait_ge(stored[s], 16 * (PAIRS + 1))

                @block.tensor
                def _(pe):
                    rounds = counters(pe, "pe_r")
                    for s in range(2):
                        pe.sem_inc(round_used[s], 1)

                    def rounds_of(s, b, i):
                        rows = gathered(s, w).rearrange("p (j c) -> p j c", c=w)
                        lo, hi = edge_range(pe, b)
                        pe.wait_ge(sums_read[s], i + 1)
                        pe.matmul(sum_ps[s][0:NB, 0:w], zeros[:, 0:NB], zeros[:, 0:w], start=True, stop=True)
                        with pe.Fori(lo, hi, RE) as at:
                            r = next_round(pe, rounds[s])
                            pe.wait_ge(onehot_ready[s], r)
                            pe.wait_ge(rows_gathered[s], r * GATHERED)
                            for j in range(T):
                                last = pe.matmul(sum_ps[s][0:NB, 0:w], onehot[s][:, j, :], rows[:, j, :], start=False,
                                                 stop=(j == T - 1), skip_group_check=True)
                            last.then_inc(round_used[s], 1)
                        pe.matmul(sum_ps[s][0:NB, 0:2], zeros[:, 0:NB], zeros[:, 0:2], start=False, stop=True,
                                  skip_group_check=True).then_inc(sums_ready[s], 1)

                    def finish(s, i):
                        if last_layer:
                            return
                        pe.wait_ge(sums_read[s], i + 2)
                        for k in range(k_tiles):
                            last = pe.transpose(turn_ps[s][:, k * NB:(k + 1) * NB], z[s][:, k * P:(k + 1) * P], identity[0:NB, 0:NB])
                        last.then_inc(sum_turned[s], 1)
                        pe.wait_ge(zT_ready[s], i + 1)
                        if n == 0:
                            pe.wait_ge(result_read[s], i + 1)
                            for k in range(2):
                                last = pe.matmul(product_ps[s][0:NB, :], zT[s][:, k, :], w1_sb[:, k, :], start=(k == 0), stop=(k == 1))
                            last.then_inc(product[s], 1)
                        else:
                            for m in range(4):
                                for k in range(4):
                                    last = pe.matmul(hidden_ps[s][:, m * NB:(m + 1) * NB], w2_sb[:, k, m * P:(m + 1) * P], zT[s][:, k, :],
                                                     start=(k == 0), stop=(k == 3))
                            last.then_inc(hidden_product[s], 1)
                            pe.wait_ge(hidden_ready[s], i + 1)
                            for k in range(4):
                                last = pe.matmul(product_ps[s][0:NB, 0:D], hiddenT[s][:, k, :], w3_sb[:, k, :], start=(k == 0), stop=(k == 3))
                            last.then_inc(product[s], 1)

                    rounds_of(0, 0, 0)
                    with pe.Fori(0, PAIRS - 1) as i:
                        rounds_of(1, 2 * i + 1, i)
                        finish(0, i)
                        rounds_of(0, 2 * i + 2, i + 1)
                        finish(1, i)
                    rounds_of(1, BLOCKS - 1, PAIRS - 1)
                    finish(0, PAIRS - 1)
                    finish(1, PAIRS - 1)

        graph_layer(0, table1, D)
        graph_layer(1, table2, HID)
        graph_layer(2, table3, D)


_INS = ['x', 'src', 'dst', 'L0_gnn_Wq', 'L0_gnn_bq', 'L0_gnn_Wk', 'L0_gnn_bk', 'L0_gnn_Wv', 'L0_gnn_bv', 'L0_gnn_Wo', 'L0_gnn_bo',
        'L0_gnn_W1', 'L0_gnn_b1', 'L0_gnn_W2', 'L0_gnn_b2', 'L0_gnn_bn1_g', 'L0_gnn_bn1_b', 'L0_gnn_bn2_g', 'L0_gnn_bn2_b',
        'L1_gnn_w1', 'L1_gnn_b1', 'L1_gnn_eps1', 'L1_gnn_w2', 'L1_gnn_b2', 'L1_gnn_eps2', 'L1_gnn_w3', 'L1_gnn_b3', 'L1_gnn_eps3']


def kernel(**inputs):
    import numpy as np
    import concourse.bacc as bacc
    from concourse.bass_utils import run_bass_kernel_spmd

    nc = bacc.Bacc("TRN2", target_bir_lowering=False, num_devices=1)
    arrays, args = {}, []
    for name in _INS:
        a = np.ascontiguousarray(inputs[name])
        if a.ndim == 0:
            a = a.reshape(1)
        arrays[f"in_{name}"] = a
        args.append(nc.dram_tensor(f"in_{name}", a.shape, mybir.dt.from_np(a.dtype), kind="ExternalInput").ap())
    args.append(nc.dram_tensor("out_0", (N, D), F32, kind="ExternalOutput").ap())
    build(nc, *args)
    r = run_bass_kernel_spmd(nc, [arrays], core_ids=[0])
    return r.results[0]["out_0"]
```

```python
import concourse.bass as bass
from concourse import mybir
from contextlib import ExitStack
import itertools

F32 = mybir.dt.float32
BF16 = mybir.dt.bfloat16
I32 = mybir.dt.int32
ALU = mybir.AluOpType
ACT = mybir.ActivationFunctionType
AX = mybir.AxisListType

N = 6250
E = 100000
D = 256
HEADS = 8
DH = D // HEADS
DFF = 512
HID = 512
P = 128
NB = 125
BLOCKS = N // NB
PAIRS = BLOCKS // 2
T = 17
RE = T * P
TW = D + HEADS
EPP = 800
EP = E // EPP
REC = 4
GATHERED = 16 * T
BIG = 1.0e30
LN_EPS = 1e-5
BN_EPS = 1e-5
SLOPE = 0.2


WAIT_REGISTERS = itertools.count()


def wait_apart(engine, sem, value, least):
    if not isinstance(value, int):
        held = engine.alloc_register(f"wait_value{next(WAIT_REGISTERS)}")
        engine.reg_mov(held, value)
        value = engine.snap(held, min_val=1, max_val=1 << 20)
    engine.wait_ge(sem, least)
    engine.wait_ge(sem, value)


class InOrder:

    def __init__(self, engine, sem):
        self.engine, self.sem, self.n = engine, sem, 0

    def step(self, instruction):
        self.n += 1
        instruction.then_inc(self.sem, 1)
        self.engine.wait_ge(self.sem, self.n)

    def restart(self):
        if self.n:
            self.engine.sem_clear(self.sem)
        self.n = 0


def build(nc, x, src, dst, Wq, bq, Wk, bk, Wv, bv, Wo, bo, W1, b1, W2, b2, g1, be1, g2, be2,
          w1, c1, eps1, w2, c2, eps2, w3, c3, eps3, out):
    edges = nc.dram_tensor("edge_records", (E + RE, REC), I32).ap()
    table0 = nc.dram_tensor("table0", (N, TW), F32).ap()
    table1 = nc.dram_tensor("table1", (N, D), F32).ap()
    table2 = nc.dram_tensor("table2", (N, HID), F32).ap()
    table3 = nc.dram_tensor("table3", (N, D), F32).ap()
    x1 = nc.dram_tensor("x1", (N, D), F32).ap()
    spare = nc.dram_tensor("spare", (16, P), F32).ap()
    spare_rows = iter(range(16))

    with ExitStack() as ctx:
        def sb(name, shape, dt=F32):
            return ctx.enter_context(nc.sbuf_tensor(name, shape, dt))

        banks = [ctx.enter_context(nc.psum_tensor(f"bank{n}", [P, 512], F32)) for n in range(8)]

        arena = sb("arena", [P, 2 * N + 2 * T * TW])
        hT = arena[:, 0:2 * N].rearrange("p (k n) -> p k n", k=2)
        gathered0 = [arena[:, 2 * N + s * T * TW:2 * N + (s + 1) * T * TW] for s in range(2)]

        def gathered(s, w):
            return arena[:, s * T * w:(s + 1) * T * w]

        onehot = [sb(f"onehot{s}", [P, T, NB]) for s in range(2)]
        record = [sb(f"record{s}", [P, T, REC], I32) for s in range(2)]
        relative = [sb(f"relative{s}", [P, T]) for s in range(2)]
        identity = sb("identity", [P, P])
        identity_bf = sb("identity_bf", [P, P], BF16)
        column = sb("column", [P, NB])
        minus_base = sb("minus_base", [P, BLOCKS])
        zeros = sb("zeros", [P, 512], BF16)
        ones = sb("ones", [P, 1])
        end_mask = sb("end_mask", [P, T])
        eps_ln = sb("eps_ln", [P, 1])
        eps_bn = sb("eps_bn", [P, 1])
        counts = sb("counts", [P, BLOCKS + 1])
        first_edge = sb("first_edge", [1, BLOCKS + 1], I32)
        scores = sb("scores", [NB, BLOCKS, HEADS])
        stats = sb("stats", [P, 2, BLOCKS, 6])
        moments = sb("moments", [P, 2, 2])
        gain = sb("gain", [P, 2])
        shift = sb("shift", [P, 2])
        spread = sb("spread", [P, 2])
        wqkv_sb = sb("wqkv_sb", [P, 2, 3 * D])
        bqkv_sb = sb("bqkv_sb", [NB, 3 * D])
        wo_sb = sb("wo_sb", [P, 2, D])
        wf1_sb = sb("wf1_sb", [P, 2, DFF])
        wf2_sb = sb("wf2_sb", [P, 4, D])
        w1_sb = sb("w1_sb", [P, 2, HID])
        w2_sb = sb("w2_sb", [P, 4, HID])
        w3_sb = sb("w3_sb", [P, 4, D])
        c1_sb = sb("c1_sb", [NB, HID])
        c3_sb = sb("c3_sb", [NB, D])
        boT = sb("boT", [P, 2])
        b1T = sb("b1T", [P, 4])
        b2T = sb("b2T", [P, 2])
        bnT = sb("bnT", [P, 4, 2])
        c2T = sb("c2T", [P, 4])
        one_eps = sb("one_eps", [P, 3])

        def phase_semaphores(phase):
            taken = []

            def clear():
                nc.clear_and_free_semaphores(taken)
                nc.all_engine_barrier()

            def sem(name):
                taken.append(nc.alloc_semaphore(name))
                return taken[-1]

            phase.callback(clear)
            return sem

        def first_store(engine, stored):
            n = next(spare_rows)
            engine.dma_start(spare[n:n + 1, :], identity[0:1, :]).then_inc(stored, 16)

        def block_rows(table, b):
            return table[bass.ds(b * NB, NB), :]

        def node_columns(k, b):
            return hT[:, k, bass.ds(b * NB, NB)]

        with ExitStack() as phase:
            sem = phase_semaphores(phase)

            loaded = sem("weights_loaded")
            dst_loaded = sem("dst_loaded")
            src_loaded = sem("src_loaded")
            edge_memset = sem("edge_memset")
            made = sem("constants_made")
            masks = sem("masks_made")
            records_made = sem("records_made")
            records_stored = sem("records_stored")
            counted = sem("edges_counted")
            summed = sem("counts_summed")
            dve_order = sem("dve_order")
            pool_order = sem("pool_order")

            dst_int = arena[0:EP, 0:EPP + 2].bitcast(I32)
            dst_f = arena[0:EP, 1000:1000 + EPP + 2]
            record_all = arena[0:EP, 2000:2000 + EPP * REC].rearrange("p (e c) -> p e c", c=REC)
            compared = arena[0:EP, 6000:6000 + EPP]
            src_int = arena[0:EP, 7000:7000 + EPP].bitcast(I32)
            tail = arena[:, 8000:8000 + T * REC].rearrange("p (e c) -> p e c", c=REC)
            eps_f = arena[:, 9000:9003]
            block = phase.enter_context(nc.Block())

            @block.sync
            def _(sp):
                sp.wait_ge(edge_memset, 1)
                sp.dma_start(dst_int[:, 1:EPP + 1], dst.rearrange("(p e) -> p e", e=EPP)).then_inc(dst_loaded, 16)
                dst_rows = dst.rearrange("(p e) -> p e", e=EPP)
                with nc.allow_non_contiguous_dma("one neighbour per partition"):
                    sp.dma_start(dst_int[1:EP, 0:1], dst_rows[0:EP - 1, EPP - 1:EPP]).then_inc(dst_loaded, 16)
                    sp.dma_start(dst_int[0:EP - 1, EPP + 1:EPP + 2], dst_rows[1:EP, 0:1]).then_inc(dst_loaded, 16)
                sp.dma_start(src_int, src.rearrange("(p e) -> p e", e=EPP)).then_inc(src_loaded, 16)
                for n, w in enumerate((Wq, Wk, Wv)):
                    sp.dma_start(wqkv_sb[:, :, n * D:(n + 1) * D], w.rearrange("(k p) n -> p k n", p=P)).then_inc(loaded, 16)
                for n, b in enumerate((bq, bk, bv)):
                    sp.dma_start(bqkv_sb[:, n * D:(n + 1) * D], b.partition_broadcast(NB)).then_inc(loaded, 16)
                for tile, w in ((wo_sb, Wo), (wf1_sb, W1), (wf2_sb, W2), (w1_sb, w1), (w2_sb, w2), (w3_sb, w3)):
                    sp.dma_start(tile[:, :, :], w.rearrange("(k p) n -> p k n", p=P)).then_inc(loaded, 16)
                sp.dma_start(c1_sb[:, :], c1.partition_broadcast(NB)).then_inc(loaded, 16)
                sp.dma_start(c3_sb[:, :], c3.partition_broadcast(NB)).then_inc(loaded, 16)
                n_loads = 14
                sp.wait_ge(records_made, 1)
                sp.dma_start(edges[0:E, :].rearrange("(p e) c -> p (e c)", e=EPP),
                             record_all.bitcast(I32).rearrange("p e c -> p (e c)")).then_inc(records_stored, 16)
                sp.dma_start(edges[E:E + RE, :].rearrange("(p e) c -> p (e c)", e=T),
                             tail.bitcast(I32).rearrange("p e c -> p (e c)")).then_inc(records_stored, 16)
                sp.wait_ge(loaded, 16 * n_loads)
                sp.wait_ge(records_stored, 32)

            @block.scalar
            def _(act):
                with nc.allow_non_contiguous_dma("vectors of one value per channel"):
                    loads = [(boT[:, :], bo), (b1T[:, :], b1), (b2T[:, :], b2), (c2T[:, :], c2),
                             (bnT[:, 0, :], g1), (bnT[:, 1, :], be1), (bnT[:, 2, :], g2), (bnT[:, 3, :], be2)]
                    for tile, v in loads:
                        act.dma_start(tile, v.rearrange("(k p) -> p k", p=P)).then_inc(made, 16)
                    for n, e in enumerate((eps1, eps2, eps3)):
                        act.dma_start(eps_f[:, n:n + 1], e.partition_broadcast(P)).then_inc(made, 16)
                act.wait_ge(made, 16 * (len(loads) + 3))

            @block.gpsimd
            def _(pool):
                order = InOrder(pool, pool_order)
                order.step(pool.memset(identity[:, :], 0.0))
                pool.affine_select(out=identity[:, :], in_=identity[:, :], compare_op=ALU.not_equal, fill=1.0,
                                   base=0, pattern=[[-1, P]], channel_multiplier=1).then_inc(masks, 1)
                order.step(pool.memset(end_mask[:, :], 0.0))
                pool.affine_select(out=end_mask[:, :], in_=end_mask[:, :], compare_op=ALU.not_equal, fill=1.0,
                                   base=-(T - 1) - (P - 1), pattern=[[1, T]], channel_multiplier=1)
                pool.iota(column[:, :], pattern=[[1, NB]], base=0, channel_multiplier=0,
                          allow_small_or_imprecise_dtypes=True).then_inc(masks, 1)
                pool.iota(minus_base[:, :], pattern=[[-NB, BLOCKS]], base=0, channel_multiplier=0,
                          allow_small_or_imprecise_dtypes=True).then_inc(masks, 1)
                pool.memset(zeros[:, :], 0.0).then_inc(masks, 1)
                pool.memset(ones[:, :], 1.0).then_inc(masks, 1)
                pool.memset(eps_ln[:, :], LN_EPS).then_inc(masks, 1)
                pool.memset(eps_bn[:, :], BN_EPS).then_inc(masks, 1)

            @block.vector
            def _(dve):
                order = InOrder(dve, dve_order)
                dve.memset(dst_int, -1).then_inc(edge_memset, 1)
                order.step(dve.memset(tail, 0.0))
                order.step(dve.memset(tail[:, :, 1], BIG))
                dve.wait_ge(dst_loaded, 48)
                order.step(dve.tensor_copy(dst_f, dst_int))
                own = dst_f[:, 1:EPP + 1]
                order.step(dve.tensor_copy(record_all[:, :, 1], own))
                order.step(dve.tensor_tensor(compared, own, dst_f[:, 0:EPP], ALU.not_equal))
                order.step(dve.tensor_scalar(record_all[:, :, 2], compared, -BIG, None, ALU.mult))
                order.step(dve.tensor_tensor(record_all[:, :, 3], own, dst_f[:, 2:EPP + 2], ALU.not_equal))
                dve.wait_ge(src_loaded, 16)
                dve.tensor_copy(record_all[:, :, 0].bitcast(I32), src_int).then_inc(records_made, 1)
                for b in range(BLOCKS + 1):
                    order.step(dve.tensor_scalar(compared, own, float(b * NB), 0.0, ALU.is_lt, ALU.add,
                                                 accum_out=counts[0:EP, b:b + 1]))
                dve.wait_ge(made, 16 * 11)
                order.step(dve.tensor_scalar(one_eps[:, :], eps_f, 1.0, None, ALU.add))
                order.restart()
                dve.sem_inc(counted, 1)
                dve.wait_ge(summed, 1)
                order.step(dve.tensor_copy(first_edge[:, :], banks[0][0:1, 0:BLOCKS + 1]))

            @block.tensor
            def _(pe):
                pe.wait_ge(counted, 1)
                pe.wait_ge(masks, 7)
                pe.matmul(banks[0][0:1, 0:BLOCKS + 1], ones[0:EP, :], counts[0:EP, :], start=True, stop=True).then_inc(summed, 1)

        with ExitStack() as phase:
            sem = phase_semaphores(phase)

            def pair(name):
                return [sem(f"{name}{s}") for s in range(2)]

            def tiles(name, shape):
                return [phase.enter_context(nc.sbuf_tensor(f"{name}{s}", shape, F32)) for s in range(2)]

            x_loaded, x_used = pair("x_loaded"), pair("x_used")
            var_ready, std_ready = sem("var_ready"), sem("std_ready")
            norm_ready, norm_transposed, hT_ready = pair("norm_ready"), pair("norm_transposed"), pair("hT_ready")
            qkv_ready, row_ready, row_stored = pair("qkv_ready"), pair("row_ready"), pair("row_stored")
            dve_order = sem("dve_order2")
            x_sb, norm, row = tiles("x_sb", [NB, D]), tiles("norm", [NB, D]), tiles("row", [NB, TW])
            hTs, qk = tiles("hTs", [P, 2, NB]), tiles("qk", [NB, 2 * D])
            six, two = tiles("six", [NB, 6]), tiles("two", [NB, 2])
            std, head_sum = tiles("std", [NB, 1]), tiles("head_sum", [NB, HEADS])
            qk_ps, v_ps, t_ps = banks[0:2], banks[2:4], banks[4:6]
            block = phase.enter_context(nc.Block())

            @block.sync
            def _(sp):
                with sp.Fori(0, PAIRS) as i:
                    for s in range(2):
                        sp.wait_ge(x_used[s], i + 1)
                        sp.dma_start(x_sb[s][:, :], block_rows(x, 2 * i + s)).then_inc(x_loaded[s], 16)

            @block.vector
            def _(dve):
                order = InOrder(dve, dve_order)
                for s in range(2):
                    dve.sem_inc(x_used[s], 1)
                    dve.sem_inc(row_ready[s], 1)

                def normalise(s, i):
                    dve.wait_ge(x_loaded[s], (i + 1) * 16)
                    order.step(dve.bn_stats(six[s][:, :], x_sb[s][:, :]))
                    order.step(dve.bn_aggr(two[s][:, :], six[s][:, :]))
                    dve.sem_inc(var_ready, 1)
                    dve.wait_ge(std_ready, i * 2 + s + 1)
                    order.step(dve.reciprocal(std[s][:, :], std[s][:, :]))
                    order.step(dve.tensor_scalar(norm[s][:, :], x_sb[s][:, :], two[s][:, 0:1], std[s][:, 0:1],
                                                 ALU.subtract, ALU.mult))
                    dve.sem_inc(norm_ready[s], 1)
                    dve.sem_inc(x_used[s], 1)
                    order.restart()

                def finish(s, i):
                    dve.wait_ge(qkv_ready[s], i + 1)
                    dve.wait_ge(row_stored[s], (i + 1) * 16)
                    order.step(dve.tensor_tensor(qk[s][:, :], qk_ps[s][0:NB, :], bqkv_sb[:, 0:2 * D], ALU.add))
                    order.step(dve.tensor_tensor(qk[s][:, 0:D], qk[s][:, 0:D], qk[s][:, D:2 * D], ALU.mult))
                    order.step(dve.tensor_reduce(head_sum[s][:, :], qk[s][:, 0:D].rearrange("p (h c) -> p h c", c=DH),
                                                 op=ALU.add, axis=AX.X))
                    dve.tensor_scalar(scores[:, bass.ds(2 * i + s, 1), :], head_sum[s][:, :], float(DH) ** -0.5, None, ALU.mult)
                    dve.tensor_scalar(row[s][:, D:TW], head_sum[s][:, :], float(DH) ** -0.5, None, ALU.mult)
                    order.step(dve.tensor_tensor(row[s][:, 0:D], v_ps[s][0:NB, 0:D], bqkv_sb[:, 2 * D:3 * D], ALU.add))
                    dve.sem_inc(row_ready[s], 1)
                    order.restart()

                normalise(0, 0)
                with dve.Fori(0, PAIRS - 1) as i:
                    normalise(1, i)
                    finish(0, i)
                    normalise(0, i + 1)
                    finish(1, i)
                normalise(1, PAIRS - 1)
                finish(0, PAIRS - 1)
                finish(1, PAIRS - 1)

            @block.gpsimd
            def _(pool):
                for s in range(2):
                    first_store(pool, row_stored[s])
                with pool.Fori(0, PAIRS) as i:
                    for s in range(2):
                        wait_apart(pool, row_ready[s], i + 2, 1)
                        pool.dma_start(block_rows(table0, 2 * i + s), row[s][:, :]).then_inc(row_stored[s], 16)
                for s in range(2):
                    pool.wait_ge(row_stored[s], 16 * (PAIRS + 1))

            @block.scalar
            def _(act):
                with act.Fori(0, PAIRS) as i:
                    for s in range(2):
                        act.wait_ge(var_ready, i * 2 + s + 1)
                        act.activation(std[s][:, :], two[s][:, 1:2], ACT.Sqrt, bias=eps_ln[0:NB, :]).then_inc(std_ready, 1)
                        act.wait_ge(norm_transposed[s], i + 1)
                        for k in range(2):
                            act.activation(node_columns(k, 2 * i + s), t_ps[s][:, k * NB:(k + 1) * NB], ACT.Relu)
                        act.activation(hTs[s][:, :, :].rearrange("p k n -> p (k n)"), t_ps[s][:, 0:2 * NB],
                                       ACT.Relu).then_inc(hT_ready[s], 1)

            @block.tensor
            def _(pe):
                with pe.Fori(0, PAIRS) as i:
                    for s in range(2):
                        pe.wait_ge(norm_ready[s], i + 1)
                        for k in range(2):
                            last = pe.transpose(t_ps[s][:, k * NB:(k + 1) * NB], norm[s][:, k * P:(k + 1) * P],
                                                identity[0:NB, 0:NB])
                        last.then_inc(norm_transposed[s], 1)
                        pe.wait_ge(hT_ready[s], i + 1)
                        pe.wait_ge(row_ready[s], i + 1)
                        for ps, w in ((qk_ps[s][0:NB, :], wqkv_sb[:, :, 0:2 * D]), (v_ps[s][0:NB, 0:D], wqkv_sb[:, :, 2 * D:3 * D])):
                            for k in range(2):
                                last = pe.matmul(ps, hTs[s][:, k, :], w[:, k, :], start=(k == 0), stop=(k == 1))
                        last.then_inc(qkv_ready[s], 1)

        with ExitStack() as phase:
            sem = phase_semaphores(phase)

            def pair(name):
                return [sem(f"a_{name}{s}") for s in range(2)]

            def tiles(name, shape, dt=F32):
                return [phase.enter_context(nc.sbuf_tensor(f"a_{name}{s}", shape, dt)) for s in range(2)]

            record_loaded, rows_gathered, quarters_used = pair("record_loaded"), pair("rows_gathered"), pair("quarters_used")
            onehot_wide = pair("onehot_wide")
            onehot_ready, T_ready, T_copied, prepared = pair("onehot_ready"), pair("T_ready"), pair("T_copied"), pair("prepared")
            bias_ready, bias_turned, bias_copied = pair("bias_ready"), pair("bias_turned"), pair("bias_copied")
            scan1_ready, tops_turned = pair("scan1_ready"), pair("tops_turned")
            scan_ready, carry_ready, ends_ready, max_selected = (pair("scan_ready"), pair("carry_ready"), pair("ends_ready"),
                                                                 pair("max_selected"))
            node_ready, spread_ready, shifted_ready, weights_ready = (pair("node_ready"), pair("spread_ready"), pair("shifted_ready"),
                                                                      pair("weights_ready"))
            weighted, block_begun = pair("weighted"), pair("block_begun")
            self_loaded, self_shifted, self_weight = pair("self_loaded"), pair("self_shifted"), pair("self_weight")
            attended, att_turned, att_copied, projected = pair("attended"), pair("att_turned"), pair("att_copied"), pair("projected")
            block_done = pair("block_done")
            tables_ready = sem("tables_ready")
            dve_order = sem("dve_order3")

            onehot_bf, onehotT = tiles("onehot_bf", [P, T, NB], BF16), tiles("onehotT", [NB, T, P], BF16)
            last_flag, reset, data = tiles("last_flag", [P, T]), tiles("reset", [P, HEADS, T]), tiles("data", [P, HEADS, T])
            local, bias = tiles("local", [P, HEADS, T]), tiles("bias", [P, HEADS])
            biasT, scanned = tiles("biasT", [HEADS, P]), tiles("scanned", [HEADS, P + 1])
            ends, ends_parts = tiles("ends", [P, T, HEADS]), tiles("ends_parts", [P, 3, T, HEADS + 1], BF16)
            run_max, run_m, node_m = tiles("run_max", [NB, HEADS]), tiles("run_m", [NB, HEADS]), tiles("node_m", [NB, HEADS])
            node_parts = tiles("node_parts", [NB, 3, 2 * HEADS], BF16)
            tmp8, none_bias = tiles("tmp8", [NB, HEADS]), tiles("none_bias", [NB, 1])
            rescale, alpha, alpha2 = tiles("rescale", [NB, HEADS]), tiles("alpha", [P, T, HEADS]), tiles("alpha2", [P, T, HEADS])
            acc, self_row, selfw = tiles("acc", [NB, TW]), tiles("self_row", [NB, D]), tiles("selfw", [NB, HEADS])
            attT = tiles("attT", [P, 2, NB])
            self_alpha = phase.enter_context(nc.sbuf_tensor("self_alpha", [NB, BLOCKS, HEADS], F32))
            score_parts = phase.enter_context(nc.sbuf_tensor("score_parts", [NB, BLOCKS, 3, HEADS], BF16))
            score_rest = phase.enter_context(nc.sbuf_tensor("score_rest", [NB, BLOCKS, HEADS], F32))
            turn_ps, acc_ps, mix_ps, node_ps = banks[0:2], banks[2:4], banks[4:6], banks[6:8]
            CHUNKS = [(c, min(c + 4, T)) for c in range(0, T, 4)]
            QUARTERS = [(0, 4), (4, 8), (8, 12), (12, T)]
            NQ = len(QUARTERS)
            MOST = 4 * BLOCKS
            block = phase.enter_context(nc.Block())

            def edge_range(engine, b):
                lo = engine.value_load(first_edge[0:1, bass.ds(b, 1)], min_val=0, max_val=E)
                hi = engine.value_load(first_edge[0:1, bass.ds(b + 1, 1)], min_val=0, max_val=E)
                return lo, hi

            def counters(engine, name):
                regs = [engine.alloc_register(f"{name}{s}") for s in range(2)]
                for r in regs:
                    engine.reg_mov(r, 0)
                return regs

            def count_of(engine, reg):
                return engine.snap(reg, min_val=0, max_val=MOST)

            def next_round(engine, reg):
                engine.reg_add(reg, reg, 1)
                return engine.snap(reg, min_val=1, max_val=MOST)

            def over_blocks(engine, first_round, more_rounds):
                def one_pair(i, first=False, last=False):
                    first_round(0, i, None if first else (1, i - 1), None if first else (0, i - 1), (1, i))
                    more_rounds(0, i)
                    first_round(1, i, (0, i), None if first else (1, i - 1), None if last else (0, i + 1))
                    more_rounds(1, i)

                one_pair(0, first=True)
                with engine.Fori(1, PAIRS - 1) as i:
                    one_pair(i)
                one_pair(PAIRS - 1, last=True)

            @block.sync
            def _(sp):
                rounds = counters(sp, "sp_rounds")
                with sp.Fori(0, PAIRS) as i:
                    for s in range(2):
                        lo, hi = edge_range(sp, 2 * i + s)
                        with sp.Fori(lo, hi, RE) as at:
                            before = count_of(sp, rounds[s])
                            sp.wait_ge(ends_ready[s], before + 1)
                            sp.dma_start(record[s][:, :, :].rearrange("p j c -> p (j c)"),
                                         edges[bass.ds(at, RE), :].rearrange("(p j) c -> p (j c)", j=T)).then_inc(record_loaded[s], 16)
                            next_round(sp, rounds[s])

            @block.gpsimd
            def _(pool):
                rounds = counters(pool, "pool_rounds")
                with pool.Fori(0, PAIRS) as i:
                    for s in range(2):
                        lo, hi = edge_range(pool, 2 * i + s)
                        with pool.Fori(lo, hi, RE) as at:
                            before = count_of(pool, rounds[s])
                            wait_apart(pool, record_loaded[s], before * 16 + 16, 16)
                            for q, (j0, j1) in enumerate(QUARTERS):
                                wait_apart(pool, quarters_used[s], before * NQ + q + 1, 1)
                                for j in range(j0, j1):
                                    pool.indirect_dma_start(
                                        out=gathered0[s][:, j * TW:(j + 1) * TW], out_offset=None, in_=table0,
                                        in_offset=bass.IndirectOffsetOnAxis(ap=record[s][:, j, 0:1], axis=0),
                                    ).then_inc(rows_gathered[s], 16)
                            next_round(pool, rounds[s])

            @block.vector
            def _(dve):
                order = InOrder(dve, dve_order)
                rounds = counters(dve, "dve_rounds")
                extra = counters(dve, "dve_extra")
                for s in range(2):
                    dve.memset(scanned[s][:, 0:1], -BIG)
                    dve.memset(acc[s][:, :], 0.0)
                    dve.memset(reset[s][:, :, 0], -BIG)
                    order.step(dve.memset(ends_parts[s][:, :, :, :], 0.0))
                    dve.sem_inc(block_done[s], 1)
                    dve.sem_inc(weighted[s], NQ)
                    dve.sem_inc(ends_ready[s], 1)
                order.step(dve.tensor_copy(identity_bf[:, :], identity[:, :]))
                order.step(dve.tensor_tensor(score_rest[:, :, :], scores[:, :, :], scores[:, :, :], ALU.add))
                order.step(dve.scalar_tensor_tensor(self_alpha[:, :, :], score_rest[:, :, :], SLOPE, score_rest[:, :, :],
                                                    ALU.mult, ALU.max))
                order.step(dve.tensor_copy(score_parts[:, :, 0, :], scores[:, :, :]))
                order.step(dve.tensor_tensor(score_rest[:, :, :], scores[:, :, :], score_parts[:, :, 0, :], ALU.subtract))
                order.step(dve.tensor_copy(score_parts[:, :, 1, :], score_rest[:, :, :]))
                order.step(dve.tensor_tensor(score_parts[:, :, 2, :], score_rest[:, :, :], score_parts[:, :, 1, :], ALU.subtract))
                dve.sem_inc(tables_ready, 1)
                order.restart()
                flat = "p h j -> p (h j)"

                def heads(t):
                    return t.unsqueeze(2).broadcast_to([NB, HEADS, DH])

                def by_head(t):
                    return t.rearrange("p (h c) -> p h c", c=DH)

                def prepare_small(s, b):
                    before = count_of(dve, rounds[s])
                    rec = record[s][:, :, :].bitcast(F32)
                    dve.wait_ge(record_loaded[s], before * 16 + 16)
                    dve.tensor_scalar(relative[s][:, :], rec[:, :, 1], minus_base[:, bass.ds(b, 1)], None, ALU.add)
                    dve.tensor_tensor(last_flag[s][:, :], rec[:, :, 3], end_mask[:, :], ALU.max)
                    order.step(dve.tensor_reduce(bias[s][:, 0:1], rec[:, :, 2], op=ALU.min, axis=AX.X))
                    order.step(dve.tensor_copy(bias[s][:, 1:HEADS], bias[s][:, 0:1].broadcast_to([P, HEADS - 1])))
                    dve.sem_inc(bias_ready[s], 1)

                def prepare_onehot(s):
                    dve.tensor_tensor(onehot_bf[s][:, :, :], column[:, :].unsqueeze(1).broadcast_to([P, T, NB]),
                                      relative[s][:, :].unsqueeze(2).broadcast_to([P, T, NB]), ALU.is_equal).then_inc(onehot_ready[s], 1)

                def scan_edges(s):
                    return dve.tensor_tensor_scan(local[s][:, :, :].rearrange(flat), reset[s][:, :, :].rearrange(flat),
                                                  data[s][:, :, :].rearrange(flat), -BIG, ALU.add, ALU.max)

                def scores_of(s):
                    r = count_of(dve, rounds[s])
                    rows = gathered0[s].rearrange("p (j c) -> p j c", c=TW)
                    dve.wait_ge(prepared[s], r)
                    dve.wait_ge(rows_gathered[s], r * GATHERED)
                    order.step(dve.tensor_copy(data[s][:, :, :], rows[:, :, D:TW].rearrange("p j h -> p h j")))
                    scan_edges(s).then_inc(scan1_ready[s], 1)
                    return r

                def scan_partitions(s, r):
                    dve.wait_ge(tops_turned[s], r)
                    dve.wait_ge(bias_copied[s], r)
                    dve.tensor_tensor_scan(scanned[s][:, 1:P + 1], biasT[s][:, :], mix_ps[s][0:HEADS, 0:P],
                                           -BIG, ALU.add, ALU.max).then_inc(scan_ready[s], 1)

                def segment_maxima(s, r):
                    rec = record[s][:, :, :].bitcast(F32)
                    dve.wait_ge(carry_ready[s], r)
                    order.step(dve.scalar_tensor_tensor(data[s][:, :, 0], node_ps[s][:, 288:288 + HEADS], rec[:, 0, 2:3],
                                                        data[s][:, :, 0], ALU.add, ALU.max))
                    order.step(scan_edges(s))
                    order.step(dve.tensor_tensor(ends[s][:, :, :], local[s][:, :, :].rearrange("p h j -> p j h"),
                                                 last_flag[s][:, :].unsqueeze(2).broadcast_to([P, T, HEADS]), ALU.mult))
                    parts = ends_parts[s]
                    dve.tensor_copy(parts[:, 0, :, HEADS], last_flag[s][:, :])
                    order.step(dve.tensor_copy(parts[:, 0, :, 0:HEADS], ends[s][:, :, :]))
                    order.step(dve.tensor_tensor(ends[s][:, :, :], ends[s][:, :, :], parts[:, 0, :, 0:HEADS], ALU.subtract))
                    order.step(dve.tensor_copy(parts[:, 1, :, 0:HEADS], ends[s][:, :, :]))
                    dve.tensor_tensor(parts[:, 2, :, 0:HEADS], ends[s][:, :, :], parts[:, 1, :, 0:HEADS],
                                      ALU.subtract).then_inc(ends_ready[s], 1)

                def node_maxima(s, b, r):
                    own = scores[:, bass.ds(b, 1), :].rearrange("p o h -> p (o h)")
                    parts = node_parts[s]
                    dve.wait_ge(max_selected[s], r)
                    order.step(dve.tensor_scalar(none_bias[s][:, :], node_ps[s][0:NB, 272 + HEADS:273 + HEADS], BIG, -BIG,
                                                 ALU.mult, ALU.add))
                    order.step(dve.scalar_tensor_tensor(run_max[s][:, :], node_ps[s][0:NB, 272:272 + HEADS], none_bias[s][:, :],
                                                        run_max[s][:, :], ALU.add, ALU.max))
                    order.step(dve.tensor_tensor(tmp8[s][:, :], run_max[s][:, :], own, ALU.add))
                    order.step(dve.scalar_tensor_tensor(node_m[s][:, :], tmp8[s][:, :], SLOPE, tmp8[s][:, :], ALU.mult, ALU.max))
                    order.step(dve.tensor_copy(parts[:, 0, HEADS:2 * HEADS], node_m[s][:, :]))
                    order.step(dve.tensor_tensor(tmp8[s][:, :], node_m[s][:, :], parts[:, 0, HEADS:2 * HEADS], ALU.subtract))
                    order.step(dve.tensor_copy(parts[:, 1, HEADS:2 * HEADS], tmp8[s][:, :]))
                    dve.tensor_tensor(parts[:, 2, HEADS:2 * HEADS], tmp8[s][:, :], parts[:, 1, HEADS:2 * HEADS],
                                      ALU.subtract).then_inc(node_ready[s], 1)

                def shifted_alpha(s, r):
                    rows = gathered0[s].rearrange("p (j c) -> p j c", c=TW)
                    by_edge = node_ps[s][:, 0:T * 2 * HEADS].rearrange("p (j c) -> p j c", c=2 * HEADS)
                    dve.wait_ge(spread_ready[s], r)
                    order.step(dve.tensor_tensor(alpha[s][:, :, :], by_edge[:, :, 0:HEADS], rows[:, :, D:TW], ALU.add))
                    order.step(dve.scalar_tensor_tensor(alpha2[s][:, :, :], alpha[s][:, :, :], SLOPE, alpha[s][:, :, :], ALU.mult, ALU.max))
                    order.step(dve.tensor_tensor(alpha[s][:, :, :], alpha2[s][:, :, :], by_edge[:, :, HEADS:2 * HEADS], ALU.subtract))
                    dve.tensor_scalar(alpha2[s][:, :, :], alpha[s][:, :, :], 0.0, None, ALU.min).then_inc(shifted_ready[s], 1)

                def weigh(s, r):
                    rows = gathered0[s].rearrange("p (j c) -> p j c", c=TW)
                    values = rows[:, :, 0:D].rearrange("p j (h c) -> p j h c", c=DH)
                    dve.wait_ge(weights_ready[s], r)
                    for j0, j1 in QUARTERS:
                        dve.tensor_tensor(values[:, j0:j1], values[:, j0:j1],
                                          rows[:, j0:j1, D:TW].unsqueeze(3).broadcast_to([P, j1 - j0, HEADS, DH]),
                                          ALU.mult).then_inc(weighted[s], 1)

                def self_shift(s, i):
                    own = self_alpha[:, bass.ds(2 * i + s, 1), :].rearrange("p o h -> p (o h)")
                    dve.tensor_tensor(selfw[s][:, :], own, node_m[s][:, :], ALU.subtract).then_inc(self_shifted[s], 1)

                def self_values(s, i):
                    dve.wait_ge(self_weight[s], i + 1)
                    dve.wait_ge(self_loaded[s], (i + 1) * 16)
                    order.step(dve.tensor_tensor(by_head(self_row[s][:, :]), by_head(self_row[s][:, :]), heads(selfw[s][:, :]), ALU.mult))

                def attend(s):
                    dve.wait_ge(quarters_used[s], count_of(dve, rounds[s]) * NQ + NQ)
                    order.step(dve.tensor_tensor(self_row[s][:, :], self_row[s][:, :], acc_ps[s][0:NB, 0:D], ALU.add))
                    order.step(dve.tensor_tensor(selfw[s][:, :], selfw[s][:, :], acc_ps[s][0:NB, D:TW], ALU.add))
                    order.restart()
                    with dve.If(count_of(dve, extra[s]) > 0):
                        order.step(dve.tensor_tensor(self_row[s][:, :], self_row[s][:, :], acc[s][:, 0:D], ALU.add))
                        order.step(dve.tensor_tensor(selfw[s][:, :], selfw[s][:, :], acc[s][:, D:TW], ALU.add))
                        order.step(dve.memset(acc[s][:, :], 0.0))
                        order.restart()
                    dve.reg_mov(extra[s], 0)
                    order.step(dve.reciprocal(tmp8[s][:, :], selfw[s][:, :]))
                    dve.tensor_tensor(by_head(self_row[s][:, :]), by_head(self_row[s][:, :]), heads(tmp8[s][:, :]),
                                      ALU.mult).then_inc(attended[s], 1)

                def residual(s, i):
                    b = 2 * i + s
                    dve.wait_ge(projected[s], i + 1)
                    for m in range(2):
                        last = dve.scalar_tensor_tensor(node_columns(m, b), acc_ps[s][:, m * NB:(m + 1) * NB], boT[:, m:m + 1],
                                                        node_columns(m, b), ALU.add, ALU.add)
                    order.step(last)
                    dve.bn_stats(stats[:, 0, bass.ds(b, 1), :].rearrange("p o c -> p (o c)"), node_columns(0, b))
                    order.step(dve.bn_stats(stats[:, 1, bass.ds(b, 1), :].rearrange("p o c -> p (o c)"), node_columns(1, b)))
                    dve.sem_inc(block_done[s], 1)

                def first_round(s, i, before, done, after):
                    if before is not None:
                        self_shift(*before)
                    r = scores_of(s)
                    if before is not None:
                        self_values(*before)
                    if done is not None:
                        residual(*done)
                    scan_partitions(s, r)
                    segment_maxima(s, r)
                    if after is not None:
                        prepare_small(after[0], 2 * after[1] + after[0])
                        prepare_onehot(after[0])
                    dve.wait_ge(block_begun[s], i + 1)
                    node_maxima(s, 2 * i + s, r)
                    if before is not None:
                        attend(before[0])
                    if after is not None:
                        next_round(dve, rounds[after[0]])
                    shifted_alpha(s, r)
                    weigh(s, r)
                    order.restart()

                def more_rounds(s, i):
                    b = 2 * i + s
                    lo, hi = edge_range(dve, b)
                    with dve.If(hi > lo + RE):
                        with dve.Fori(lo + RE, hi, RE) as at:
                            dve.reg_add(extra[s], extra[s], 1)
                            before = count_of(dve, rounds[s])
                            dve.wait_ge(quarters_used[s], before * NQ + NQ)
                            order.step(dve.tensor_tensor(acc[s][:, :], acc[s][:, :], acc_ps[s][0:NB, 0:TW], ALU.add))
                            prepare_small(s, b)
                            prepare_onehot(s)
                            next_round(dve, rounds[s])
                            r = scores_of(s)
                            scan_partitions(s, r)
                            segment_maxima(s, r)
                            node_maxima(s, b, r)
                            order.step(dve.tensor_tensor(rescale[s][:, :], run_m[s][:, :], node_m[s][:, :], ALU.subtract))
                            shifted_alpha(s, r)
                            weigh(s, r)
                            order.step(dve.tensor_tensor(by_head(acc[s][:, 0:D]), by_head(acc[s][:, 0:D]), heads(rescale[s][:, :]), ALU.mult))
                            order.step(dve.tensor_tensor(acc[s][:, D:TW], acc[s][:, D:TW], rescale[s][:, :], ALU.mult))
                            order.restart()

                prepare_small(0, 0)
                prepare_onehot(0)
                next_round(dve, rounds[0])
                order.restart()
                over_blocks(dve, first_round, more_rounds)
                residual(0, PAIRS - 1)
                self_shift(1, PAIRS - 1)
                self_values(1, PAIRS - 1)
                attend(1)
                residual(1, PAIRS - 1)
                order.restart()

            @block.scalar
            def _(act):
                rounds = counters(act, "act_rounds")
                act.wait_ge(tables_ready, 1)

                def begin_block(s, i):
                    b = 2 * i + s
                    act.wait_ge(block_done[s], i + 1)
                    act.dma_start(self_row[s][:, :], table0[bass.ds(b * NB, NB), 0:D]).then_inc(self_loaded[s], 16)
                    act.activation(run_max[s][:, :], scores[:, bass.ds(b, 1), :].rearrange("p o h -> p (o h)"), ACT.Copy)
                    act.activation(node_parts[s][:, :, 0:HEADS], score_parts[:, bass.ds(b, 1), :, :].rearrange("p o k h -> p (o k) h"),
                                   ACT.Copy).then_inc(block_begun[s], 1)

                def prepare(s):
                    before = count_of(act, rounds[s])
                    rec = record[s][:, :, :].bitcast(F32)
                    act.wait_ge(bias_ready[s], before + 1)
                    act.activation(reset[s][:, :, 1:T], rec[:, 1:T, 2].unsqueeze(1).broadcast_to([P, HEADS, T - 1]), ACT.Copy)
                    act.wait_ge(bias_turned[s], before + 1)
                    act.activation(biasT[s][:, :], mix_ps[s][0:HEADS, P:2 * P], ACT.Copy).then_inc(bias_copied[s], 1)
                    for c, (j0, j1) in enumerate(CHUNKS):
                        act.wait_ge(T_ready[s], before * len(CHUNKS) + c + 1)
                        act.activation(onehotT[s][:, j0:j1, :].rearrange("p j e -> p (j e)"),
                                       turn_ps[c % 2][0:NB, 0:(j1 - j0) * P], ACT.Copy).then_inc(
                                           T_copied[s] if j1 < T else prepared[s], 1)
                    next_round(act, rounds[s])

                def widen(s):
                    r = count_of(act, rounds[s])
                    act.wait_ge(quarters_used[s], r * NQ)
                    act.activation(onehot[s][:, :, :].rearrange("p j d -> p (j d)"), onehot_bf[s][:, :, :].rearrange("p j d -> p (j d)"),
                                   ACT.Copy).then_inc(onehot_wide[s], 1)

                def weights(s, joined):
                    r = count_of(act, rounds[s])
                    rows = gathered0[s].rearrange("p (j c) -> p j c", c=TW)
                    act.wait_ge(shifted_ready[s], r)
                    if joined:
                        act.activation(rescale[s][:, :], rescale[s][:, :], ACT.Exp)
                    act.activation(run_m[s][:, :], node_m[s][:, :], ACT.Copy)
                    act.activation(rows[:, :, D:TW], alpha2[s][:, :, :], ACT.Exp).then_inc(weights_ready[s], 1)

                def self_exp(s, i):
                    act.wait_ge(self_shifted[s], i + 1)
                    act.activation(selfw[s][:, :], selfw[s][:, :], ACT.Exp).then_inc(self_weight[s], 1)

                def copy_attended(s, i):
                    act.wait_ge(att_turned[s], i + 1)
                    act.activation(attT[s][:, :, :].rearrange("p k n -> p (k n)"), mix_ps[s][:, 256:256 + 2 * NB],
                                   ACT.Copy).then_inc(att_copied[s], 1)

                def first_round(s, i, before, done, after):
                    if before is not None:
                        self_exp(*before)
                    begin_block(s, i)
                    if after is not None:
                        prepare(after[0])
                    weights(s, False)
                    if before is not None:
                        copy_attended(*before)
                    if after is not None:
                        widen(after[0])

                def more_rounds(s, i):
                    lo, hi = edge_range(act, 2 * i + s)
                    with act.If(hi > lo + RE):
                        with act.Fori(lo + RE, hi, RE) as at:
                            prepare(s)
                            widen(s)
                            weights(s, True)

                prepare(0)
                widen(0)
                over_blocks(act, first_round, more_rounds)
                self_exp(1, PAIRS - 1)
                copy_attended(1, PAIRS - 1)

            @block.tensor
            def _(pe):
                rounds = counters(pe, "pe_rounds")
                for s in range(2):
                    pe.sem_inc(quarters_used[s], NQ)

                def sums(s, i, q):
                    r = count_of(pe, rounds[s])
                    rows = gathered0[s].rearrange("p (j c) -> p j c", c=TW)
                    pe.wait_ge(weighted[s], r * NQ + q + 1)
                    if q == 0:
                        pe.wait_ge(onehot_wide[s], r)
                        pe.wait_ge(block_done[s], i + 1)
                    j0, j1 = QUARTERS[q]
                    for j in range(j0, j1):
                        last = pe.matmul(acc_ps[s][0:NB, 0:TW], onehot[s][:, j, :], rows[:, j, :], start=(j == 0), stop=(j == T - 1),
                                         skip_group_check=True)
                    last.then_inc(quarters_used[s], 1)

                def prepare(s, chunks):
                    before = count_of(pe, rounds[s])
                    if chunks[0] == 0:
                        pe.wait_ge(bias_ready[s], before + 1)
                        pe.transpose(mix_ps[s][0:HEADS, P:2 * P], bias[s][:, :], identity[:, :]).then_inc(bias_turned[s], 1)
                        pe.wait_ge(onehot_ready[s], before + 1)
                    for c in chunks:
                        j0, j1 = CHUNKS[c]
                        if c >= 2:
                            pe.wait_ge(T_copied[s], before * (len(CHUNKS) - 1) + c - 1)
                        for j in range(j0, j1):
                            last = pe.matmul(turn_ps[c % 2][0:NB, (j - j0) * P:(j - j0 + 1) * P], onehot_bf[s][:, j, :], identity_bf[:, :],
                                             start=True, stop=True)
                        last.then_inc(T_ready[s], 1)

                def turn_tops(s, r):
                    pe.wait_ge(scan1_ready[s], r)
                    pe.transpose(mix_ps[s][0:HEADS, 0:P], local[s][:, :, T - 1], identity[:, :]).then_inc(tops_turned[s], 1)

                def turn_carries(s, r):
                    wait_apart(pe, scan_ready[s], r, 1)
                    pe.transpose(node_ps[s][:, 288:288 + HEADS], scanned[s][:, 0:P], identity[0:HEADS, 0:HEADS]).then_inc(carry_ready[s], 1)

                def select_maxima(s, r):
                    pe.wait_ge(prepared[s], r)
                    pe.wait_ge(ends_ready[s], r + 1)
                    for j in range(T):
                        for k in range(3):
                            last = pe.matmul(node_ps[s][0:NB, 272:273 + HEADS], onehot_bf[s][:, j, :], ends_parts[s][:, k, j, :],
                                             start=(j == 0 and k == 0), stop=(j == T - 1 and k == 2))
                    last.then_inc(max_selected[s], 1)

                def spread_nodes(s, r):
                    pe.wait_ge(block_begun[s], 1)
                    pe.wait_ge(node_ready[s], r)
                    for j in range(T):
                        for k in range(3):
                            last = pe.matmul(node_ps[s][:, j * 2 * HEADS:(j + 1) * 2 * HEADS], onehotT[s][:, j, :], node_parts[s][:, k, :],
                                             start=(k == 0), stop=(k == 2))
                    last.then_inc(spread_ready[s], 1)

                def project(s, i):
                    pe.wait_ge(attended[s], i + 1)
                    for k in range(2):
                        last = pe.transpose(mix_ps[s][:, 256 + k * NB:256 + (k + 1) * NB], self_row[s][:, k * P:(k + 1) * P],
                                            identity[0:NB, 0:NB])
                    last.then_inc(att_turned[s], 1)
                    pe.wait_ge(att_copied[s], i + 1)
                    for m in range(2):
                        for k in range(2):
                            last = pe.matmul(acc_ps[s][:, m * NB:(m + 1) * NB], wo_sb[:, k, m * P:(m + 1) * P], attT[s][:, k, :],
                                             start=(k == 0), stop=(k == 1))
                    last.then_inc(projected[s], 1)

                every = range(len(CHUNKS))

                def first_round(s, i, before, done, after):
                    r = count_of(pe, rounds[s])
                    turn_tops(s, r)
                    turn_carries(s, r)
                    if before is not None:
                        sums(before[0], before[1], 2)
                        sums(before[0], before[1], 3)
                    select_maxima(s, r)
                    if after is not None:
                        prepare(after[0], every[0:2])
                    spread_nodes(s, r)
                    if after is not None:
                        prepare(after[0], every[2:])
                    if before is not None:
                        project(*before)
                    if after is not None:
                        next_round(pe, rounds[after[0]])
                    sums(s, i, 0)
                    sums(s, i, 1)

                def more_rounds(s, i):
                    lo, hi = edge_range(pe, 2 * i + s)
                    with pe.If(hi > lo + RE):
                        with pe.Fori(lo + RE, hi, RE) as at:
                            sums(s, i, 2)
                            sums(s, i, 3)
                            prepare(s, every)
                            next_round(pe, rounds[s])
                            r = count_of(pe, rounds[s])
                            for step in (turn_tops, turn_carries, select_maxima, spread_nodes):
                                step(s, r)
                            sums(s, i, 0)
                            sums(s, i, 1)

                prepare(0, every)
                next_round(pe, rounds[0])
                over_blocks(pe, first_round, more_rounds)
                sums(1, PAIRS - 1, 2)
                sums(1, PAIRS - 1, 3)
                project(1, PAIRS - 1)

        def norm_affine(dve, order, n, variance_ready, spread_ready):
            for m in range(2):
                order.step(dve.bn_aggr(moments[:, m, :], stats[:, m, :, :].rearrange("p b c -> p (b c)")))
            dve.sem_inc(variance_ready, 1)
            dve.wait_ge(spread_ready, 1)
            order.step(dve.reciprocal(spread[:, :], spread[:, :]))
            order.step(dve.tensor_tensor(gain[:, :], spread[:, :], bnT[:, 2 * n, :], ALU.mult))
            order.step(dve.tensor_tensor(shift[:, :], moments[:, :, 0], gain[:, :], ALU.mult))
            order.step(dve.tensor_tensor(shift[:, :], bnT[:, 2 * n + 1, :], shift[:, :], ALU.subtract))

        with ExitStack() as phase:
            sem = phase_semaphores(phase)

            def pair(name):
                return [sem(f"f_{name}{s}") for s in range(2)]

            variance_ready, spread_ready = sem("f_variance"), sem("f_spread")
            normed, up_ready, hidden_ready, down_ready, out_read = (pair("normed"), pair("up_ready"), pair("hidden_ready"),
                                                                    pair("down_ready"), pair("out_read"))
            dve_order = sem("dve_order4")
            hidden = [phase.enter_context(nc.sbuf_tensor(f"hidden{s}", [P, 4, NB], F32)) for s in range(2)]
            up_ps, down_ps = banks[0:2], banks[2:4]
            block = phase.enter_context(nc.Block())

            @block.vector
            def _(dve):
                order = InOrder(dve, dve_order)
                norm_affine(dve, order, 0, variance_ready, spread_ready)
                order.restart()
                for s in range(2):
                    dve.sem_inc(out_read[s], 1)

                def normalise(s, b):
                    for m in range(2):
                        order.step(dve.tensor_scalar(node_columns(m, b), node_columns(m, b), gain[:, m:m + 1], shift[:, m:m + 1],
                                                     ALU.mult, ALU.add))
                    dve.sem_inc(normed[s], 1)
                    order.restart()

                def finish(s, i):
                    b = 2 * i + s
                    dve.wait_ge(down_ready[s], i + 1)
                    for m in range(2):
                        order.step(dve.scalar_tensor_tensor(node_columns(m, b), down_ps[s][:, m * NB:(m + 1) * NB], b2T[:, m:m + 1],
                                                            node_columns(m, b), ALU.add, ALU.add))
                        order.step(dve.bn_stats(stats[:, m, bass.ds(b, 1), :].rearrange("p o c -> p (o c)"), node_columns(m, b)))
                    dve.sem_inc(out_read[s], 1)
                    order.restart()

                normalise(0, 0)
                with dve.Fori(0, PAIRS - 1) as i:
                    normalise(1, 2 * i + 1)
                    finish(0, i)
                    normalise(0, 2 * i + 2)
                    finish(1, i)
                normalise(1, BLOCKS - 1)
                finish(0, PAIRS - 1)
                finish(1, PAIRS - 1)

            @block.scalar
            def _(act):
                act.wait_ge(variance_ready, 1)
                act.activation(spread[:, :], moments[:, :, 1], ACT.Sqrt, bias=eps_bn[:, :]).then_inc(spread_ready, 1)
                with act.Fori(0, PAIRS) as i:
                    for s in range(2):
                        act.wait_ge(up_ready[s], i + 1)
                        for m in range(4):
                            last = act.activation(hidden[s][:, m, :], up_ps[s][:, m * NB:(m + 1) * NB], ACT.Relu, bias=b1T[:, m:m + 1])
                        last.then_inc(hidden_ready[s], 1)

            @block.tensor
            def _(pe):
                def up(s, i):
                    pe.wait_ge(normed[s], i + 1)
                    for m in range(4):
                        for k in range(2):
                            last = pe.matmul(up_ps[s][:, m * NB:(m + 1) * NB], wf1_sb[:, k, m * P:(m + 1) * P],
                                             node_columns(k, 2 * i + s), start=(k == 0), stop=(k == 1))
                    last.then_inc(up_ready[s], 1)

                def down(s, i):
                    pe.wait_ge(hidden_ready[s], i + 1)
                    pe.wait_ge(out_read[s], i + 1)
                    for m in range(2):
                        for k in range(4):
                            last = pe.matmul(down_ps[s][:, m * NB:(m + 1) * NB], wf2_sb[:, k, m * P:(m + 1) * P], hidden[s][:, k, :],
                                             start=(k == 0), stop=(k == 3))
                    last.then_inc(down_ready[s], 1)

                up(0, 0)
                with pe.Fori(0, PAIRS - 1) as i:
                    up(1, i)
                    down(0, i)
                    up(0, i + 1)
                    down(1, i)
                up(1, PAIRS - 1)
                down(0, PAIRS - 1)
                down(1, PAIRS - 1)

        with ExitStack() as phase:
            sem = phase_semaphores(phase)

            def pair(name):
                return [sem(f"g_{name}{s}") for s in range(2)]

            def tiles(name, shape):
                return [phase.enter_context(nc.sbuf_tensor(f"g_{name}{s}", shape, F32)) for s in range(2)]

            variance_ready, spread_ready = sem("g_variance"), sem("g_spread")
            x_loaded, x_used, normed, turned = pair("x_loaded"), pair("x_used"), pair("normed"), pair("turned")
            var_ready, std_ready = pair("var_ready"), pair("std_ready")
            x1_ready, x1_stored, centred, h_ready, h_stored = (pair("x1_ready"), pair("x1_stored"), pair("centred"),
                                                               pair("h_ready"), pair("h_stored"))
            dve_order = sem("dve_order5")
            x_sb, yT, x1_sb, norm, h_sb = (tiles("x_sb", [NB, D]), tiles("yT", [P, 2, NB]), tiles("x1_sb", [NB, D]),
                                           tiles("norm", [NB, D]), tiles("h_sb", [NB, D]))
            six, two, std = tiles("six", [NB, 6]), tiles("two", [NB, 2]), tiles("std", [NB, 1])
            y_ps = banks[0:2]
            block = phase.enter_context(nc.Block())

            @block.sync
            def _(sp):
                with sp.Fori(0, PAIRS) as i:
                    for s in range(2):
                        sp.wait_ge(x_used[s], i + 1)
                        sp.dma_start(x_sb[s][:, :], block_rows(x, 2 * i + s)).then_inc(x_loaded[s], 16)

            @block.vector
            def _(dve):
                order = InOrder(dve, dve_order)
                norm_affine(dve, order, 1, variance_ready, spread_ready)
                order.restart()
                for s in range(2):
                    dve.sem_inc(x_used[s], 1)
                    dve.sem_inc(std_ready[s], 1)

                def affine(s, i):
                    for m in range(2):
                        order.step(dve.tensor_scalar(yT[s][:, m, :], node_columns(m, 2 * i + s), gain[:, m:m + 1], shift[:, m:m + 1],
                                                     ALU.mult, ALU.add))
                    dve.sem_inc(normed[s], 1)
                    order.restart()

                def residual(s, i):
                    dve.wait_ge(turned[s], i + 1)
                    dve.wait_ge(x_loaded[s], (i + 1) * 16)
                    dve.wait_ge(x1_stored[s], (i + 1) * 16)
                    order.step(dve.tensor_tensor(x1_sb[s][:, :], y_ps[s][0:NB, 0:D], x_sb[s][:, :], ALU.add))
                    dve.sem_inc(x1_ready[s], 1)
                    dve.sem_inc(x_used[s], 1)
                    order.step(dve.bn_stats(six[s][:, :], x1_sb[s][:, :]))
                    order.step(dve.bn_aggr(two[s][:, :], six[s][:, :]))
                    dve.sem_inc(var_ready[s], 1)
                    order.restart()

                def centre(s, i):
                    dve.wait_ge(std_ready[s], i + 2)
                    dve.wait_ge(h_ready[s], i + 1)
                    order.step(dve.reciprocal(std[s][:, :], std[s][:, :]))
                    order.step(dve.tensor_scalar(norm[s][:, :], x1_sb[s][:, :], two[s][:, 0:1], std[s][:, 0:1],
                                                 ALU.subtract, ALU.mult))
                    dve.sem_inc(centred[s], 1)
                    order.restart()

                affine(0, 0)
                affine(1, 0)
                residual(0, 0)
                with dve.Fori(0, PAIRS - 1) as i:
                    residual(1, i)
                    affine(0, i + 1)
                    centre(0, i)
                    affine(1, i + 1)
                    residual(0, i + 1)
                    centre(1, i)
                residual(1, PAIRS - 1)
                centre(0, PAIRS - 1)
                centre(1, PAIRS - 1)

            @block.scalar
            def _(act):
                for s in range(2):
                    act.sem_inc(h_ready[s], 1)
                act.wait_ge(variance_ready, 1)
                act.activation(spread[:, :], moments[:, :, 1], ACT.Sqrt, bias=eps_bn[:, :]).then_inc(spread_ready, 1)

                def deviation(s, i):
                    act.wait_ge(var_ready[s], i + 1)
                    act.activation(std[s][:, :], two[s][:, 1:2], ACT.Sqrt, bias=eps_ln[0:NB, :]).then_inc(std_ready[s], 1)

                def rectify(s, i):
                    act.wait_ge(centred[s], i + 1)
                    act.wait_ge(h_stored[s], (i + 1) * 16)
                    act.activation(h_sb[s][:, :], norm[s][:, :], ACT.Relu).then_inc(h_ready[s], 1)

                deviation(0, 0)
                with act.Fori(0, PAIRS - 1) as i:
                    deviation(1, i)
                    rectify(0, i)
                    deviation(0, i + 1)
                    rectify(1, i)
                deviation(1, PAIRS - 1)
                rectify(0, PAIRS - 1)
                rectify(1, PAIRS - 1)

            @block.gpsimd
            def _(pool):
                for s in range(2):
                    first_store(pool, x1_stored[s])
                    first_store(pool, h_stored[s])
                with pool.Fori(0, PAIRS) as i:
                    for s in range(2):
                        wait_apart(pool, x1_ready[s], i + 1, 1)
                        pool.dma_start(block_rows(x1, 2 * i + s), x1_sb[s][:, :]).then_inc(x1_stored[s], 16)
                        wait_apart(pool, h_ready[s], i + 2, 1)
                        pool.dma_start(block_rows(table1, 2 * i + s), h_sb[s][:, :]).then_inc(h_stored[s], 16)
                for s in range(2):
                    pool.wait_ge(x1_stored[s], 16 * (PAIRS + 1))
                    pool.wait_ge(h_stored[s], 16 * (PAIRS + 1))

            @block.tensor
            def _(pe):
                with pe.Fori(0, PAIRS) as i:
                    for s in range(2):
                        pe.wait_ge(normed[s], i + 1)
                        for m in range(2):
                            last = pe.transpose(y_ps[s][0:NB, m * P:(m + 1) * P], yT[s][:, m, :], identity[:, :])
                        last.then_inc(turned[s], 1)

        def graph_layer(n, table, w):
            last_layer = n == 2
            k_tiles = w // P
            with ExitStack() as phase:
                sem = phase_semaphores(phase)

                def pair(name):
                    return [sem(f"l{n}_{name}{s}") for s in range(2)]

                def tiles(name, shape):
                    return [phase.enter_context(nc.sbuf_tensor(f"l{n}_{name}{s}", shape, F32)) for s in range(2)]

                record_loaded, rows_gathered, round_used = pair("record_loaded"), pair("rows_gathered"), pair("round_used")
                onehot_ready, sums_ready, sums_read = pair("onehot_ready"), pair("sums_ready"), pair("sums_read")
                own_loaded, own_used, sum_turned, zT_ready = pair("own_loaded"), pair("own_used"), pair("sum_turned"), pair("zT_ready")
                product, hidden_ready, result_read, result_ready, stored = (pair("product"), pair("hidden_ready"),
                                                                            pair("result_read"), pair("result_ready"), pair("stored"))
                hidden_product = pair("hidden_product")
                dve_order = sem(f"dve_order{6 + n}")
                own = tiles("own", [NB, w])
                z = tiles("z", [NB, w])
                zT = tiles("zT", [P, 4, NB]) if not last_layer else None
                x1_sb = tiles("x1_sb", [NB, D]) if last_layer else None
                hiddenT = tiles("hiddenT", [P, 4, NB]) if n == 1 else None
                width = (HID, D, D)[n]
                z2 = tiles("z2", [NB, HID]) if n == 0 else None
                result = tiles("result", [NB, width])
                sum_ps, turn_ps, product_ps, hidden_ps = banks[0:2], banks[2:4], banks[4:6], banks[6:8]
                target = (table2, table3, out)[n]
                block = phase.enter_context(nc.Block())

                def edge_range(engine, b):
                    lo = engine.value_load(first_edge[0:1, bass.ds(b, 1)], min_val=0, max_val=E)
                    hi = engine.value_load(first_edge[0:1, bass.ds(b + 1, 1)], min_val=0, max_val=E)
                    return lo, hi

                def counters(engine, name):
                    regs = [engine.alloc_register(f"{name}{n}_{s}") for s in range(2)]
                    for r in regs:
                        engine.reg_mov(r, 0)
                    return regs

                def next_round(engine, reg):
                    engine.reg_add(reg, reg, 1)
                    return engine.snap(reg, min_val=1, max_val=4 * BLOCKS)

                own_loads = 32 if last_layer else 16

                @block.sync
                def _(sp):
                    rounds = counters(sp, "sp_r")
                    with sp.Fori(0, PAIRS) as i:
                        for s in range(2):
                            lo, hi = edge_range(sp, 2 * i + s)
                            with sp.Fori(lo, hi, RE) as at:
                                r = next_round(sp, rounds[s])
                                sp.wait_ge(round_used[s], r)
                                sp.dma_start(record[s][:, :, :].rearrange("p j c -> p (j c)"),
                                             edges[bass.ds(at, RE), :].rearrange("(p j) c -> p (j c)", j=T)).then_inc(record_loaded[s], 16)
                            sp.wait_ge(own_used[s], i + 1)
                            sp.dma_start(own[s][:, :], block_rows(table, 2 * i + s)).then_inc(own_loaded[s], 16)
                            if last_layer:
                                sp.dma_start(x1_sb[s][:, :], block_rows(x1, 2 * i + s)).then_inc(own_loaded[s], 16)

                @block.gpsimd
                def _(pool):
                    rounds = counters(pool, "pool_r")
                    with pool.Fori(0, PAIRS) as i:
                        for s in range(2):
                            lo, hi = edge_range(pool, 2 * i + s)
                            with pool.Fori(lo, hi, RE) as at:
                                r = next_round(pool, rounds[s])
                                pool.wait_ge(round_used[s], r)
                                wait_apart(pool, record_loaded[s], r * 16, 16)
                                for j in range(T):
                                    pool.indirect_dma_start(
                                        out=gathered(s, w)[:, j * w:(j + 1) * w], out_offset=None, in_=table,
                                        in_offset=bass.IndirectOffsetOnAxis(ap=record[s][:, j, 0:1], axis=0),
                                    ).then_inc(rows_gathered[s], 16)

                @block.vector
                def _(dve):
                    order = InOrder(dve, dve_order)
                    rounds = counters(dve, "dve_r")
                    for s in range(2):
                        dve.sem_inc(own_used[s], 1)
                        dve.sem_inc(sums_read[s], 1)
                        dve.sem_inc(result_read[s], 1)

                    def rounds_of(s, b):
                        lo, hi = edge_range(dve, b)
                        with dve.Fori(lo, hi, RE) as at:
                            r = next_round(dve, rounds[s])
                            dve.wait_ge(record_loaded[s], r * 16)
                            dve.wait_ge(round_used[s], r)
                            order.step(dve.tensor_scalar(relative[s][:, :], record[s][:, :, 1].bitcast(F32),
                                                         minus_base[:, bass.ds(b, 1)], None, ALU.add))
                            dve.tensor_tensor(onehot[s][:, :, :], column[:, :].unsqueeze(1).broadcast_to([P, T, NB]),
                                              relative[s][:, :].unsqueeze(2).broadcast_to([P, T, NB]),
                                              ALU.is_equal).then_inc(onehot_ready[s], 1)
                            order.restart()

                    def finish(s, i):
                        dve.wait_ge(sums_ready[s], i + 1)
                        dve.wait_ge(own_loaded[s], (i + 1) * own_loads)
                        order.step(dve.scalar_tensor_tensor(z[s][:, :], own[s][:, :], one_eps[0:NB, n:n + 1],
                                                            sum_ps[s][0:NB, 0:w], ALU.mult, ALU.add))
                        dve.sem_inc(sums_read[s], 1)
                        if last_layer:
                            order.step(dve.tensor_tensor(z[s][:, :], z[s][:, :], c3_sb[:, :], ALU.add))
                            dve.wait_ge(stored[s], (i + 1) * 16)
                            order.step(dve.tensor_tensor(result[s][:, :], z[s][:, :], x1_sb[s][:, :], ALU.add))
                            dve.sem_inc(result_ready[s], 1)
                            dve.sem_inc(own_used[s], 1)
                        else:
                            dve.sem_inc(own_used[s], 1)
                        if n == 0:
                            dve.wait_ge(product[s], i + 1)
                            dve.wait_ge(result_ready[s], i + 1)
                            order.step(dve.tensor_tensor(z2[s][:, :], product_ps[s][0:NB, :], c1_sb[:, :], ALU.add))
                            dve.sem_inc(result_read[s], 1)
                        order.restart()

                    rounds_of(0, 0)
                    with dve.Fori(0, PAIRS - 1) as i:
                        rounds_of(1, 2 * i + 1)
                        finish(0, i)
                        rounds_of(0, 2 * i + 2)
                        finish(1, i)
                    rounds_of(1, BLOCKS - 1)
                    finish(0, PAIRS - 1)
                    finish(1, PAIRS - 1)

                @block.scalar
                def _(act):
                    if n == 0:
                        for s in range(2):
                            act.sem_inc(result_ready[s], 1)
                    for s in range(2):
                        first_store(act, stored[s])

                    def finish(s, i):
                        if not last_layer:
                            act.wait_ge(sum_turned[s], i + 1)
                            act.activation(zT[s][:, 0:k_tiles, :].rearrange("p k n -> p (k n)"), turn_ps[s][:, 0:k_tiles * NB],
                                           ACT.Copy).then_inc(zT_ready[s], 1)
                        if n == 0:
                            act.wait_ge(result_read[s], i + 2)
                            act.wait_ge(stored[s], (i + 1) * 16)
                            act.activation(result[s][:, :], z2[s][:, :], ACT.Relu).then_inc(result_ready[s], 1)
                            act.wait_ge(result_ready[s], i + 2)
                        if n == 1:
                            act.wait_ge(hidden_product[s], i + 1)
                            for m in range(4):
                                last = act.activation(hiddenT[s][:, m, :], hidden_ps[s][:, m * NB:(m + 1) * NB], ACT.Relu,
                                                      bias=c2T[:, m:m + 1])
                            last.then_inc(hidden_ready[s], 1)
                            act.wait_ge(product[s], i + 1)
                            act.wait_ge(stored[s], (i + 1) * 16)
                            act.activation(result[s][:, :], product_ps[s][0:NB, 0:D], ACT.Copy).then_inc(result_ready[s], 1)
                            act.wait_ge(result_ready[s], i + 1)
                        if last_layer:
                            act.wait_ge(result_ready[s], i + 1)
                        act.dma_start(block_rows(target, 2 * i + s), result[s][:, :]).then_inc(stored[s], 16)

                    with act.Fori(0, PAIRS) as i:
                        finish(0, i)
                        finish(1, i)
                    for s in range(2):
                        act.wait_ge(stored[s], 16 * (PAIRS + 1))

                @block.tensor
                def _(pe):
                    rounds = counters(pe, "pe_r")
                    for s in range(2):
                        pe.sem_inc(round_used[s], 1)

                    def rounds_of(s, b, i):
                        rows = gathered(s, w).rearrange("p (j c) -> p j c", c=w)
                        lo, hi = edge_range(pe, b)
                        pe.wait_ge(sums_read[s], i + 1)
                        pe.matmul(sum_ps[s][0:NB, 0:w], zeros[:, 0:NB], zeros[:, 0:w], start=True, stop=True)
                        with pe.Fori(lo, hi, RE) as at:
                            r = next_round(pe, rounds[s])
                            pe.wait_ge(onehot_ready[s], r)
                            pe.wait_ge(rows_gathered[s], r * GATHERED)
                            for j in range(T):
                                last = pe.matmul(sum_ps[s][0:NB, 0:w], onehot[s][:, j, :], rows[:, j, :], start=False,
                                                 stop=(j == T - 1), skip_group_check=True)
                            last.then_inc(round_used[s], 1)
                        pe.matmul(sum_ps[s][0:NB, 0:2], zeros[:, 0:NB], zeros[:, 0:2], start=False, stop=True,
                                  skip_group_check=True).then_inc(sums_ready[s], 1)

                    def finish(s, i):
                        if last_layer:
                            return
                        pe.wait_ge(sums_read[s], i + 2)
                        for k in range(k_tiles):
                            last = pe.transpose(turn_ps[s][:, k * NB:(k + 1) * NB], z[s][:, k * P:(k + 1) * P], identity[0:NB, 0:NB])
                        last.then_inc(sum_turned[s], 1)
                        pe.wait_ge(zT_ready[s], i + 1)
                        if n == 0:
                            pe.wait_ge(result_read[s], i + 1)
                            for k in range(2):
                                last = pe.matmul(product_ps[s][0:NB, :], zT[s][:, k, :], w1_sb[:, k, :], start=(k == 0), stop=(k == 1))
                            last.then_inc(product[s], 1)
                        else:
                            for m in range(4):
                                for k in range(4):
                                    last = pe.matmul(hidden_ps[s][:, m * NB:(m + 1) * NB], w2_sb[:, k, m * P:(m + 1) * P], zT[s][:, k, :],
                                                     start=(k == 0), stop=(k == 3))
                            last.then_inc(hidden_product[s], 1)
                            pe.wait_ge(hidden_ready[s], i + 1)
                            for k in range(4):
                                last = pe.matmul(product_ps[s][0:NB, 0:D], hiddenT[s][:, k, :], w3_sb[:, k, :], start=(k == 0), stop=(k == 3))
                            last.then_inc(product[s], 1)

                    rounds_of(0, 0, 0)
                    with pe.Fori(0, PAIRS - 1) as i:
                        rounds_of(1, 2 * i + 1, i)
                        finish(0, i)
                        rounds_of(0, 2 * i + 2, i + 1)
                        finish(1, i)
                    rounds_of(1, BLOCKS - 1, PAIRS - 1)
                    finish(0, PAIRS - 1)
                    finish(1, PAIRS - 1)

        graph_layer(0, table1, D)
        graph_layer(1, table2, HID)
        graph_layer(2, table3, D)


_INS = ['x', 'src', 'dst', 'L0_gnn_Wq', 'L0_gnn_bq', 'L0_gnn_Wk', 'L0_gnn_bk', 'L0_gnn_Wv', 'L0_gnn_bv', 'L0_gnn_Wo', 'L0_gnn_bo',
        'L0_gnn_W1', 'L0_gnn_b1', 'L0_gnn_W2', 'L0_gnn_b2', 'L0_gnn_bn1_g', 'L0_gnn_bn1_b', 'L0_gnn_bn2_g', 'L0_gnn_bn2_b',
        'L1_gnn_w1', 'L1_gnn_b1', 'L1_gnn_eps1', 'L1_gnn_w2', 'L1_gnn_b2', 'L1_gnn_eps2', 'L1_gnn_w3', 'L1_gnn_b3', 'L1_gnn_eps3']


def kernel(**inputs):
    import numpy as np
    import concourse.bacc as bacc
    from concourse.bass_utils import run_bass_kernel_spmd

    nc = bacc.Bacc("TRN2", target_bir_lowering=False, num_devices=1)
    arrays, args = {}, []
    for name in _INS:
        a = np.ascontiguousarray(inputs[name])
        if a.ndim == 0:
            a = a.reshape(1)
        arrays[f"in_{name}"] = a
        args.append(nc.dram_tensor(f"in_{name}", a.shape, mybir.dt.from_np(a.dtype), kind="ExternalInput").ap())
    args.append(nc.dram_tensor("out_0", (N, D), F32, kind="ExternalOutput").ap())
    build(nc, *args)
    r = run_bass_kernel_spmd(nc, [arrays], core_ids=[0])
    return r.results[0]["out_0"]
```

```python
import concourse.bass as bass
from concourse import mybir
from contextlib import ExitStack
import itertools

F32 = mybir.dt.float32
BF16 = mybir.dt.bfloat16
I32 = mybir.dt.int32
ALU = mybir.AluOpType
ACT = mybir.ActivationFunctionType
AX = mybir.AxisListType

N = 6250
E = 100000
D = 256
HEADS = 8
DH = D // HEADS
DFF = 512
HID = 512
P = 128
NB = 125
BLOCKS = N // NB
PAIRS = BLOCKS // 2
NU = 2 * NB
UNITS = N // NU
UNIT_PAIRS = UNITS // 2
T = 17
RE = T * P
TW = D + HEADS
EPP = 800
EP = E // EPP
REC = 4
GATHERED = 16 * T
BIG = 1.0e30
LN_EPS = 1e-5
BN_EPS = 1e-5
SLOPE = 0.2


WAIT_REGISTERS = itertools.count()


def wait_apart(engine, sem, value, least):
    if not isinstance(value, int):
        held = engine.alloc_register(f"wait_value{next(WAIT_REGISTERS)}")
        engine.reg_mov(held, value)
        value = engine.snap(held, min_val=1, max_val=1 << 20)
    engine.wait_ge(sem, least)
    engine.wait_ge(sem, value)


class InOrder:

    def __init__(self, engine, sem):
        self.engine, self.sem, self.n = engine, sem, 0

    def step(self, instruction):
        self.n += 1
        instruction.then_inc(self.sem, 1)
        self.engine.wait_ge(self.sem, self.n)

    def restart(self):
        if self.n:
            self.engine.sem_clear(self.sem)
        self.n = 0


def build(nc, x, src, dst, Wq, bq, Wk, bk, Wv, bv, Wo, bo, W1, b1, W2, b2, g1, be1, g2, be2,
          w1, c1, eps1, w2, c2, eps2, w3, c3, eps3, out):
    edges = nc.dram_tensor("edge_records", (E + RE, REC), I32).ap()
    table0 = nc.dram_tensor("table0", (N, TW), F32).ap()
    table1 = nc.dram_tensor("table1", (N, D), F32).ap()
    table2 = nc.dram_tensor("table2", (N, HID), F32).ap()
    table3 = nc.dram_tensor("table3", (N, D), F32).ap()
    x1 = nc.dram_tensor("x1", (N, D), F32).ap()
    spare = nc.dram_tensor("spare", (16, P), F32).ap()
    spare_rows = iter(range(16))

    with ExitStack() as ctx:
        def sb(name, shape, dt=F32):
            return ctx.enter_context(nc.sbuf_tensor(name, shape, dt))

        banks = [ctx.enter_context(nc.psum_tensor(f"bank{n}", [P, 512], F32)) for n in range(8)]

        arena = sb("arena", [P, 2 * N + 2 * T * TW])
        hT = arena[:, 0:2 * N].rearrange("p (k n) -> p k n", k=2)
        gathered0 = [arena[:, 2 * N + s * T * TW:2 * N + (s + 1) * T * TW] for s in range(2)]

        def gathered(s, w):
            return arena[:, s * T * w:(s + 1) * T * w]

        onehot = [sb(f"onehot{s}", [P, T, NB]) for s in range(2)]
        record = [sb(f"record{s}", [P, T, REC], I32) for s in range(2)]
        relative = [sb(f"relative{s}", [P, T]) for s in range(2)]
        identity = sb("identity", [P, P])
        identity_bf = sb("identity_bf", [P, P], BF16)
        column = sb("column", [P, NB])
        minus_base = sb("minus_base", [P, BLOCKS])
        zeros = sb("zeros", [P, 512], BF16)
        ones = sb("ones", [P, 1])
        end_mask = sb("end_mask", [P, T])
        eps_ln = sb("eps_ln", [P, 1])
        eps_bn = sb("eps_bn", [P, 1])
        counts = sb("counts", [P, BLOCKS + 1])
        first_edge = sb("first_edge", [1, BLOCKS + 1], I32)
        scores = sb("scores", [NB, BLOCKS, HEADS])
        stats = sb("stats", [P, 2, BLOCKS, 6])
        moments = sb("moments", [P, 2, 2])
        gain = sb("gain", [P, 2])
        shift = sb("shift", [P, 2])
        spread = sb("spread", [P, 2])
        wqkv_sb = sb("wqkv_sb", [P, 2, 3 * D])
        bqkv_sb = sb("bqkv_sb", [NB, 3 * D])
        wo_sb = sb("wo_sb", [P, 2, D])
        wf1_sb = sb("wf1_sb", [P, 2, DFF])
        wf2_sb = sb("wf2_sb", [P, 4, D])
        w1_sb = sb("w1_sb", [P, 2, HID])
        w2_sb = sb("w2_sb", [P, 4, HID])
        w3_sb = sb("w3_sb", [P, 4, D])
        c2_sb = sb("c2_sb", [NB, HID])
        c3_sb = sb("c3_sb", [NB, D])
        boT = sb("boT", [P, 2])
        b1T = sb("b1T", [P, 4])
        b2T = sb("b2T", [P, 2])
        bnT = sb("bnT", [P, 4, 2])
        c1T = sb("c1T", [P, 4])
        one_eps = sb("one_eps", [P, 3])

        def phase_semaphores(phase):
            taken = []

            def clear():
                nc.clear_and_free_semaphores(taken)
                nc.all_engine_barrier()

            def sem(name):
                taken.append(nc.alloc_semaphore(name))
                return taken[-1]

            phase.callback(clear)
            return sem

        def first_store(engine, stored):
            n = next(spare_rows)
            engine.dma_start(spare[n:n + 1, :], identity[0:1, :]).then_inc(stored, 16)

        def block_rows(table, b):
            return table[bass.ds(b * NB, NB), :]

        def node_columns(k, b):
            return hT[:, k, bass.ds(b * NB, NB)]

        with ExitStack() as phase:
            sem = phase_semaphores(phase)

            loaded = sem("weights_loaded")
            dst_loaded = sem("dst_loaded")
            src_loaded = sem("src_loaded")
            edge_memset = sem("edge_memset")
            made = sem("constants_made")
            masks = sem("masks_made")
            records_made = sem("records_made")
            records_stored = sem("records_stored")
            counted = sem("edges_counted")
            summed = sem("counts_summed")
            dve_order = sem("dve_order")
            pool_order = sem("pool_order")

            dst_int = arena[0:EP, 0:EPP + 2].bitcast(I32)
            dst_f = arena[0:EP, 1000:1000 + EPP + 2]
            record_all = arena[0:EP, 2000:2000 + EPP * REC].rearrange("p (e c) -> p e c", c=REC)
            compared = arena[0:EP, 6000:6000 + EPP]
            src_int = arena[0:EP, 7000:7000 + EPP].bitcast(I32)
            tail = arena[:, 8000:8000 + T * REC].rearrange("p (e c) -> p e c", c=REC)
            eps_f = arena[:, 9000:9003]
            block = phase.enter_context(nc.Block())

            @block.sync
            def _(sp):
                sp.wait_ge(edge_memset, 1)
                sp.dma_start(dst_int[:, 1:EPP + 1], dst.rearrange("(p e) -> p e", e=EPP)).then_inc(dst_loaded, 16)
                dst_rows = dst.rearrange("(p e) -> p e", e=EPP)
                with nc.allow_non_contiguous_dma("one neighbour per partition"):
                    sp.dma_start(dst_int[1:EP, 0:1], dst_rows[0:EP - 1, EPP - 1:EPP]).then_inc(dst_loaded, 16)
                    sp.dma_start(dst_int[0:EP - 1, EPP + 1:EPP + 2], dst_rows[1:EP, 0:1]).then_inc(dst_loaded, 16)
                sp.dma_start(src_int, src.rearrange("(p e) -> p e", e=EPP)).then_inc(src_loaded, 16)
                for n, w in enumerate((Wq, Wk, Wv)):
                    sp.dma_start(wqkv_sb[:, :, n * D:(n + 1) * D], w.rearrange("(k p) n -> p k n", p=P)).then_inc(loaded, 16)
                for n, b in enumerate((bq, bk, bv)):
                    sp.dma_start(bqkv_sb[:, n * D:(n + 1) * D], b.partition_broadcast(NB)).then_inc(loaded, 16)
                for tile, w in ((wo_sb, Wo), (wf1_sb, W1), (wf2_sb, W2), (w1_sb, w1), (w2_sb, w2), (w3_sb, w3)):
                    sp.dma_start(tile[:, :, :], w.rearrange("(k p) n -> p k n", p=P)).then_inc(loaded, 16)
                sp.dma_start(c2_sb[:, :], c2.partition_broadcast(NB)).then_inc(loaded, 16)
                sp.dma_start(c3_sb[:, :], c3.partition_broadcast(NB)).then_inc(loaded, 16)
                n_loads = 14
                sp.wait_ge(records_made, 1)
                sp.dma_start(edges[0:E, :].rearrange("(p e) c -> p (e c)", e=EPP),
                             record_all.bitcast(I32).rearrange("p e c -> p (e c)")).then_inc(records_stored, 16)
                sp.dma_start(edges[E:E + RE, :].rearrange("(p e) c -> p (e c)", e=T),
                             tail.bitcast(I32).rearrange("p e c -> p (e c)")).then_inc(records_stored, 16)
                sp.wait_ge(loaded, 16 * n_loads)
                sp.wait_ge(records_stored, 32)

            @block.scalar
            def _(act):
                with nc.allow_non_contiguous_dma("vectors of one value per channel"):
                    loads = [(boT[:, :], bo), (b1T[:, :], b1), (b2T[:, :], b2), (c1T[:, :], c1),
                             (bnT[:, 0, :], g1), (bnT[:, 1, :], be1), (bnT[:, 2, :], g2), (bnT[:, 3, :], be2)]
                    for tile, v in loads:
                        act.dma_start(tile, v.rearrange("(k p) -> p k", p=P)).then_inc(made, 16)
                    for n, e in enumerate((eps1, eps2, eps3)):
                        act.dma_start(eps_f[:, n:n + 1], e.partition_broadcast(P)).then_inc(made, 16)
                act.wait_ge(made, 16 * (len(loads) + 3))

            @block.gpsimd
            def _(pool):
                order = InOrder(pool, pool_order)
                order.step(pool.memset(identity[:, :], 0.0))
                pool.affine_select(out=identity[:, :], in_=identity[:, :], compare_op=ALU.not_equal, fill=1.0,
                                   base=0, pattern=[[-1, P]], channel_multiplier=1).then_inc(masks, 1)
                order.step(pool.memset(end_mask[:, :], 0.0))
                pool.affine_select(out=end_mask[:, :], in_=end_mask[:, :], compare_op=ALU.not_equal, fill=1.0,
                                   base=-(T - 1) - (P - 1), pattern=[[1, T]], channel_multiplier=1)
                pool.iota(column[:, :], pattern=[[1, NB]], base=0, channel_multiplier=0,
                          allow_small_or_imprecise_dtypes=True).then_inc(masks, 1)
                pool.iota(minus_base[:, :], pattern=[[-NB, BLOCKS]], base=0, channel_multiplier=0,
                          allow_small_or_imprecise_dtypes=True).then_inc(masks, 1)
                pool.memset(zeros[:, :], 0.0).then_inc(masks, 1)
                pool.memset(ones[:, :], 1.0).then_inc(masks, 1)
                pool.memset(eps_ln[:, :], LN_EPS).then_inc(masks, 1)
                pool.memset(eps_bn[:, :], BN_EPS).then_inc(masks, 1)

            @block.vector
            def _(dve):
                order = InOrder(dve, dve_order)
                dve.memset(dst_int, -1).then_inc(edge_memset, 1)
                order.step(dve.memset(tail, 0.0))
                order.step(dve.memset(tail[:, :, 1], BIG))
                dve.wait_ge(dst_loaded, 48)
                order.step(dve.tensor_copy(dst_f, dst_int))
                own = dst_f[:, 1:EPP + 1]
                order.step(dve.tensor_copy(record_all[:, :, 1], own))
                order.step(dve.tensor_tensor(compared, own, dst_f[:, 0:EPP], ALU.not_equal))
                order.step(dve.tensor_scalar(record_all[:, :, 2], compared, -BIG, None, ALU.mult))
                order.step(dve.tensor_tensor(record_all[:, :, 3], own, dst_f[:, 2:EPP + 2], ALU.not_equal))
                dve.wait_ge(src_loaded, 16)
                dve.tensor_copy(record_all[:, :, 0].bitcast(I32), src_int).then_inc(records_made, 1)
                for b in range(BLOCKS + 1):
                    order.step(dve.tensor_scalar(compared, own, float(b * NB), 0.0, ALU.is_lt, ALU.add,
                                                 accum_out=counts[0:EP, b:b + 1]))
                dve.wait_ge(made, 16 * 11)
                order.step(dve.tensor_scalar(one_eps[:, :], eps_f, 1.0, None, ALU.add))
                order.restart()
                dve.sem_inc(counted, 1)
                dve.wait_ge(summed, 1)
                order.step(dve.tensor_copy(first_edge[:, :], banks[0][0:1, 0:BLOCKS + 1]))

            @block.tensor
            def _(pe):
                pe.wait_ge(counted, 1)
                pe.wait_ge(masks, 7)
                pe.matmul(banks[0][0:1, 0:BLOCKS + 1], ones[0:EP, :], counts[0:EP, :], start=True, stop=True).then_inc(summed, 1)

        with ExitStack() as phase:
            sem = phase_semaphores(phase)

            def pair(name):
                return [sem(f"{name}{s}") for s in range(2)]

            def tiles(name, shape):
                return [phase.enter_context(nc.sbuf_tensor(f"{name}{s}", shape, F32)) for s in range(2)]

            x_loaded, x_used = pair("x_loaded"), pair("x_used")
            var_ready, std_ready = sem("var_ready"), sem("std_ready")
            norm_ready, norm_transposed, hT_ready = pair("norm_ready"), pair("norm_transposed"), pair("hT_ready")
            qkv_ready, row_ready, row_stored = pair("qkv_ready"), pair("row_ready"), pair("row_stored")
            dve_order = sem("dve_order2")
            x_sb, norm, row = tiles("x_sb", [NB, D]), tiles("norm", [NB, D]), tiles("row", [NB, TW])
            hTs, qk = tiles("hTs", [P, 2, NB]), tiles("qk", [NB, 2 * D])
            six, two = tiles("six", [NB, 6]), tiles("two", [NB, 2])
            std, head_sum = tiles("std", [NB, 1]), tiles("head_sum", [NB, HEADS])
            qk_ps, v_ps, t_ps = banks[0:2], banks[2:4], banks[4:6]
            block = phase.enter_context(nc.Block())

            @block.sync
            def _(sp):
                with sp.Fori(0, PAIRS) as i:
                    for s in range(2):
                        sp.wait_ge(x_used[s], i + 1)
                        sp.dma_start(x_sb[s][:, :], block_rows(x, 2 * i + s)).then_inc(x_loaded[s], 16)

            @block.vector
            def _(dve):
                order = InOrder(dve, dve_order)
                for s in range(2):
                    dve.sem_inc(x_used[s], 1)
                    dve.sem_inc(row_ready[s], 1)

                def normalise(s, i):
                    dve.wait_ge(x_loaded[s], (i + 1) * 16)
                    order.step(dve.bn_stats(six[s][:, :], x_sb[s][:, :]))
                    order.step(dve.bn_aggr(two[s][:, :], six[s][:, :]))
                    dve.sem_inc(var_ready, 1)
                    dve.wait_ge(std_ready, i * 2 + s + 1)
                    order.step(dve.reciprocal(std[s][:, :], std[s][:, :]))
                    order.step(dve.tensor_scalar(norm[s][:, :], x_sb[s][:, :], two[s][:, 0:1], std[s][:, 0:1],
                                                 ALU.subtract, ALU.mult))
                    dve.sem_inc(norm_ready[s], 1)
                    dve.sem_inc(x_used[s], 1)
                    order.restart()

                def finish(s, i):
                    dve.wait_ge(qkv_ready[s], i + 1)
                    dve.wait_ge(row_stored[s], (i + 1) * 16)
                    order.step(dve.tensor_tensor(qk[s][:, :], qk_ps[s][0:NB, :], bqkv_sb[:, 0:2 * D], ALU.add))
                    order.step(dve.tensor_tensor(qk[s][:, 0:D], qk[s][:, 0:D], qk[s][:, D:2 * D], ALU.mult))
                    order.step(dve.tensor_reduce(head_sum[s][:, :], qk[s][:, 0:D].rearrange("p (h c) -> p h c", c=DH),
                                                 op=ALU.add, axis=AX.X))
                    dve.tensor_scalar(scores[:, bass.ds(2 * i + s, 1), :], head_sum[s][:, :], float(DH) ** -0.5, None, ALU.mult)
                    dve.tensor_scalar(row[s][:, D:TW], head_sum[s][:, :], float(DH) ** -0.5, None, ALU.mult)
                    order.step(dve.tensor_tensor(row[s][:, 0:D], v_ps[s][0:NB, 0:D], bqkv_sb[:, 2 * D:3 * D], ALU.add))
                    dve.sem_inc(row_ready[s], 1)
                    order.restart()

                normalise(0, 0)
                with dve.Fori(0, PAIRS - 1) as i:
                    normalise(1, i)
                    finish(0, i)
                    normalise(0, i + 1)
                    finish(1, i)
                normalise(1, PAIRS - 1)
                finish(0, PAIRS - 1)
                finish(1, PAIRS - 1)

            @block.gpsimd
            def _(pool):
                for s in range(2):
                    first_store(pool, row_stored[s])
                with pool.Fori(0, PAIRS) as i:
                    for s in range(2):
                        wait_apart(pool, row_ready[s], i + 2, 1)
                        pool.dma_start(block_rows(table0, 2 * i + s), row[s][:, :]).then_inc(row_stored[s], 16)
                for s in range(2):
                    pool.wait_ge(row_stored[s], 16 * (PAIRS + 1))

            @block.scalar
            def _(act):
                with act.Fori(0, PAIRS) as i:
                    for s in range(2):
                        act.wait_ge(var_ready, i * 2 + s + 1)
                        act.activation(std[s][:, :], two[s][:, 1:2], ACT.Sqrt, bias=eps_ln[0:NB, :]).then_inc(std_ready, 1)
                        act.wait_ge(norm_transposed[s], i + 1)
                        for k in range(2):
                            act.activation(node_columns(k, 2 * i + s), t_ps[s][:, k * NB:(k + 1) * NB], ACT.Relu)
                        act.activation(hTs[s][:, :, :].rearrange("p k n -> p (k n)"), t_ps[s][:, 0:2 * NB],
                                       ACT.Relu).then_inc(hT_ready[s], 1)

            @block.tensor
            def _(pe):
                with pe.Fori(0, PAIRS) as i:
                    for s in range(2):
                        pe.wait_ge(norm_ready[s], i + 1)
                        for k in range(2):
                            last = pe.transpose(t_ps[s][:, k * NB:(k + 1) * NB], norm[s][:, k * P:(k + 1) * P],
                                                identity[0:NB, 0:NB])
                        last.then_inc(norm_transposed[s], 1)
                        pe.wait_ge(hT_ready[s], i + 1)
                        pe.wait_ge(row_ready[s], i + 1)
                        for ps, w in ((qk_ps[s][0:NB, :], wqkv_sb[:, :, 0:2 * D]), (v_ps[s][0:NB, 0:D], wqkv_sb[:, :, 2 * D:3 * D])):
                            for k in range(2):
                                last = pe.matmul(ps, hTs[s][:, k, :], w[:, k, :], start=(k == 0), stop=(k == 1))
                        last.then_inc(qkv_ready[s], 1)

        with ExitStack() as phase:
            sem = phase_semaphores(phase)

            def pair(name):
                return [sem(f"a_{name}{s}") for s in range(2)]

            def tiles(name, shape, dt=F32):
                return [phase.enter_context(nc.sbuf_tensor(f"a_{name}{s}", shape, dt)) for s in range(2)]

            record_loaded, rows_gathered, quarters_used = pair("record_loaded"), pair("rows_gathered"), pair("quarters_used")
            onehot_wide = pair("onehot_wide")
            onehot_ready, T_ready, T_copied, prepared = pair("onehot_ready"), pair("T_ready"), pair("T_copied"), pair("prepared")
            bias_ready, bias_turned, bias_copied = pair("bias_ready"), pair("bias_turned"), pair("bias_copied")
            scan1_ready, tops_turned = pair("scan1_ready"), pair("tops_turned")
            scan_ready, carry_ready, ends_ready, max_selected = (pair("scan_ready"), pair("carry_ready"), pair("ends_ready"),
                                                                 pair("max_selected"))
            node_ready, spread_ready, shifted_ready, weights_ready = (pair("node_ready"), pair("spread_ready"), pair("shifted_ready"),
                                                                      pair("weights_ready"))
            weighted, block_begun = pair("weighted"), pair("block_begun")
            self_loaded, self_shifted, self_weight = pair("self_loaded"), pair("self_shifted"), pair("self_weight")
            attended, att_turned, att_copied, projected = pair("attended"), pair("att_turned"), pair("att_copied"), pair("projected")
            block_done = pair("block_done")
            tables_ready = sem("tables_ready")
            dve_order = sem("dve_order3")

            onehot_bf, onehotT = tiles("onehot_bf", [P, T, NB], BF16), tiles("onehotT", [NB, T, P], BF16)
            last_flag, reset, data = tiles("last_flag", [P, T]), tiles("reset", [P, HEADS, T]), tiles("data", [P, HEADS, T])
            local, bias = tiles("local", [P, HEADS, T]), tiles("bias", [P, HEADS])
            biasT, scanned = tiles("biasT", [HEADS, P]), tiles("scanned", [HEADS, P + 1])
            ends, ends_parts = tiles("ends", [P, T, HEADS]), tiles("ends_parts", [P, 3, T, HEADS + 1], BF16)
            run_max, run_m, node_m = tiles("run_max", [NB, HEADS]), tiles("run_m", [NB, HEADS]), tiles("node_m", [NB, HEADS])
            node_parts = tiles("node_parts", [NB, 3, 2 * HEADS], BF16)
            tmp8, none_bias = tiles("tmp8", [NB, HEADS]), tiles("none_bias", [NB, 1])
            rescale, alpha, alpha2 = tiles("rescale", [NB, HEADS]), tiles("alpha", [P, T, HEADS]), tiles("alpha2", [P, T, HEADS])
            acc, self_row, selfw = tiles("acc", [NB, TW]), tiles("self_row", [NB, D]), tiles("selfw", [NB, HEADS])
            attT = tiles("attT", [P, 2, NB])
            self_alpha = phase.enter_context(nc.sbuf_tensor("self_alpha", [NB, BLOCKS, HEADS], F32))
            score_parts = phase.enter_context(nc.sbuf_tensor("score_parts", [NB, BLOCKS, 3, HEADS], BF16))
            score_rest = phase.enter_context(nc.sbuf_tensor("score_rest", [NB, BLOCKS, HEADS], F32))
            turn_ps, acc_ps, mix_ps, node_ps = banks[0:2], banks[2:4], banks[4:6], banks[6:8]
            CHUNKS = [(c, min(c + 4, T)) for c in range(0, T, 4)]
            QUARTERS = [(0, 4), (4, 8), (8, 12), (12, T)]
            NQ = len(QUARTERS)
            MOST = 4 * BLOCKS
            block = phase.enter_context(nc.Block())

            def edge_range(engine, b):
                lo = engine.value_load(first_edge[0:1, bass.ds(b, 1)], min_val=0, max_val=E)
                hi = engine.value_load(first_edge[0:1, bass.ds(b + 1, 1)], min_val=0, max_val=E)
                return lo, hi

            def counters(engine, name):
                regs = [engine.alloc_register(f"{name}{s}") for s in range(2)]
                for r in regs:
                    engine.reg_mov(r, 0)
                return regs

            def count_of(engine, reg):
                return engine.snap(reg, min_val=0, max_val=MOST)

            def next_round(engine, reg):
                engine.reg_add(reg, reg, 1)
                return engine.snap(reg, min_val=1, max_val=MOST)

            def over_blocks(engine, first_round, more_rounds):
                def one_pair(i, first=False, last=False):
                    first_round(0, i, None if first else (1, i - 1), None if first else (0, i - 1), (1, i))
                    more_rounds(0, i)
                    first_round(1, i, (0, i), None if first else (1, i - 1), None if last else (0, i + 1))
                    more_rounds(1, i)

                one_pair(0, first=True)
                with engine.Fori(1, PAIRS - 1) as i:
                    one_pair(i)
                one_pair(PAIRS - 1, last=True)

            def in_order_of_use(engine, one_round):
                def first(s, b):
                    lo, hi = edge_range(engine, b)
                    one_round(s, lo)

                def further(s, b):
                    lo, hi = edge_range(engine, b)
                    with engine.If(hi > lo + RE):
                        with engine.Fori(lo + RE, hi, RE) as at:
                            one_round(s, at)

                first(0, 0)
                with engine.Fori(0, PAIRS - 1) as i:
                    first(1, 2 * i + 1)
                    further(0, 2 * i)
                    first(0, 2 * i + 2)
                    further(1, 2 * i + 1)
                first(1, BLOCKS - 1)
                further(0, BLOCKS - 2)
                further(1, BLOCKS - 1)

            @block.sync
            def _(sp):
                rounds = counters(sp, "sp_rounds")

                def load_records(s, at):
                    sp.wait_ge(ends_ready[s], count_of(sp, rounds[s]) + 1)
                    sp.dma_start(record[s][:, :, :].rearrange("p j c -> p (j c)"),
                                 edges[bass.ds(at, RE), :].rearrange("(p j) c -> p (j c)", j=T)).then_inc(record_loaded[s], 16)
                    next_round(sp, rounds[s])

                in_order_of_use(sp, load_records)

            @block.gpsimd
            def _(pool):
                rounds = counters(pool, "pool_rounds")

                def gather(s, at):
                    before = count_of(pool, rounds[s])
                    wait_apart(pool, record_loaded[s], before * 16 + 16, 16)
                    for q, (j0, j1) in enumerate(QUARTERS):
                        wait_apart(pool, quarters_used[s], before * NQ + q + 1, 1)
                        for j in range(j0, j1):
                            pool.indirect_dma_start(
                                out=gathered0[s][:, j * TW:(j + 1) * TW], out_offset=None, in_=table0,
                                in_offset=bass.IndirectOffsetOnAxis(ap=record[s][:, j, 0:1], axis=0),
                            ).then_inc(rows_gathered[s], 16)
                    next_round(pool, rounds[s])

                in_order_of_use(pool, gather)

            @block.vector
            def _(dve):
                order = InOrder(dve, dve_order)
                rounds = counters(dve, "dve_rounds")
                extra = counters(dve, "dve_extra")
                for s in range(2):
                    dve.memset(scanned[s][:, 0:1], -BIG)
                    dve.memset(acc[s][:, :], 0.0)
                    dve.memset(reset[s][:, :, 0], -BIG)
                    order.step(dve.memset(ends_parts[s][:, :, :, :], 0.0))
                    dve.sem_inc(block_done[s], 1)
                    dve.sem_inc(weighted[s], NQ)
                    dve.sem_inc(ends_ready[s], 1)
                order.step(dve.tensor_copy(identity_bf[:, :], identity[:, :]))
                order.step(dve.tensor_tensor(score_rest[:, :, :], scores[:, :, :], scores[:, :, :], ALU.add))
                order.step(dve.scalar_tensor_tensor(self_alpha[:, :, :], score_rest[:, :, :], SLOPE, score_rest[:, :, :],
                                                    ALU.mult, ALU.max))
                order.step(dve.tensor_copy(score_parts[:, :, 0, :], scores[:, :, :]))
                order.step(dve.tensor_tensor(score_rest[:, :, :], scores[:, :, :], score_parts[:, :, 0, :], ALU.subtract))
                order.step(dve.tensor_copy(score_parts[:, :, 1, :], score_rest[:, :, :]))
                order.step(dve.tensor_tensor(score_parts[:, :, 2, :], score_rest[:, :, :], score_parts[:, :, 1, :], ALU.subtract))
                dve.sem_inc(tables_ready, 1)
                order.restart()
                flat = "p h j -> p (h j)"

                def heads(t):
                    return t.unsqueeze(2).broadcast_to([NB, HEADS, DH])

                def by_head(t):
                    return t.rearrange("p (h c) -> p h c", c=DH)

                def prepare_small(s, b):
                    before = count_of(dve, rounds[s])
                    rec = record[s][:, :, :].bitcast(F32)
                    dve.wait_ge(record_loaded[s], before * 16 + 16)
                    dve.tensor_scalar(relative[s][:, :], rec[:, :, 1], minus_base[:, bass.ds(b, 1)], None, ALU.add)
                    dve.tensor_tensor(last_flag[s][:, :], rec[:, :, 3], end_mask[:, :], ALU.max)
                    order.step(dve.tensor_reduce(bias[s][:, 0:1], rec[:, :, 2], op=ALU.min, axis=AX.X))
                    order.step(dve.tensor_copy(bias[s][:, 1:HEADS], bias[s][:, 0:1].broadcast_to([P, HEADS - 1])))
                    dve.sem_inc(bias_ready[s], 1)

                def prepare_onehot(s):
                    dve.tensor_tensor(onehot_bf[s][:, :, :], column[:, :].unsqueeze(1).broadcast_to([P, T, NB]),
                                      relative[s][:, :].unsqueeze(2).broadcast_to([P, T, NB]), ALU.is_equal).then_inc(onehot_ready[s], 1)

                def scan_edges(s):
                    return dve.tensor_tensor_scan(local[s][:, :, :].rearrange(flat), reset[s][:, :, :].rearrange(flat),
                                                  data[s][:, :, :].rearrange(flat), -BIG, ALU.add, ALU.max)

                def scores_of(s):
                    r = count_of(dve, rounds[s])
                    rows = gathered0[s].rearrange("p (j c) -> p j c", c=TW)
                    dve.wait_ge(prepared[s], r)
                    dve.wait_ge(rows_gathered[s], r * GATHERED)
                    order.step(dve.tensor_copy(data[s][:, :, :], rows[:, :, D:TW].rearrange("p j h -> p h j")))
                    scan_edges(s).then_inc(scan1_ready[s], 1)
                    return r

                def scan_partitions(s, r):
                    dve.wait_ge(tops_turned[s], r)
                    dve.wait_ge(bias_copied[s], r)
                    dve.tensor_tensor_scan(scanned[s][:, 1:P + 1], biasT[s][:, :], mix_ps[s][0:HEADS, 0:P],
                                           -BIG, ALU.add, ALU.max).then_inc(scan_ready[s], 1)

                def segment_maxima(s, r):
                    rec = record[s][:, :, :].bitcast(F32)
                    dve.wait_ge(carry_ready[s], r)
                    order.step(dve.scalar_tensor_tensor(data[s][:, :, 0], node_ps[s][:, 288:288 + HEADS], rec[:, 0, 2:3],
                                                        data[s][:, :, 0], ALU.add, ALU.max))
                    order.step(scan_edges(s))
                    order.step(dve.tensor_tensor(ends[s][:, :, :], local[s][:, :, :].rearrange("p h j -> p j h"),
                                                 last_flag[s][:, :].unsqueeze(2).broadcast_to([P, T, HEADS]), ALU.mult))
                    parts = ends_parts[s]
                    dve.tensor_copy(parts[:, 0, :, HEADS], last_flag[s][:, :])
                    order.step(dve.tensor_copy(parts[:, 0, :, 0:HEADS], ends[s][:, :, :]))
                    order.step(dve.tensor_tensor(ends[s][:, :, :], ends[s][:, :, :], parts[:, 0, :, 0:HEADS], ALU.subtract))
                    order.step(dve.tensor_copy(parts[:, 1, :, 0:HEADS], ends[s][:, :, :]))
                    dve.tensor_tensor(parts[:, 2, :, 0:HEADS], ends[s][:, :, :], parts[:, 1, :, 0:HEADS],
                                      ALU.subtract).then_inc(ends_ready[s], 1)

                def node_maxima(s, b, r):
                    own = scores[:, bass.ds(b, 1), :].rearrange("p o h -> p (o h)")
                    parts = node_parts[s]
                    dve.wait_ge(max_selected[s], r)
                    order.step(dve.tensor_scalar(none_bias[s][:, :], node_ps[s][0:NB, 272 + HEADS:273 + HEADS], BIG, -BIG,
                                                 ALU.mult, ALU.add))
                    order.step(dve.scalar_tensor_tensor(run_max[s][:, :], node_ps[s][0:NB, 272:272 + HEADS], none_bias[s][:, :],
                                                        run_max[s][:, :], ALU.add, ALU.max))
                    order.step(dve.tensor_tensor(tmp8[s][:, :], run_max[s][:, :], own, ALU.add))
                    order.step(dve.scalar_tensor_tensor(node_m[s][:, :], tmp8[s][:, :], SLOPE, tmp8[s][:, :], ALU.mult, ALU.max))
                    order.step(dve.tensor_copy(parts[:, 0, HEADS:2 * HEADS], node_m[s][:, :]))
                    order.step(dve.tensor_tensor(tmp8[s][:, :], node_m[s][:, :], parts[:, 0, HEADS:2 * HEADS], ALU.subtract))
                    order.step(dve.tensor_copy(parts[:, 1, HEADS:2 * HEADS], tmp8[s][:, :]))
                    dve.tensor_tensor(parts[:, 2, HEADS:2 * HEADS], tmp8[s][:, :], parts[:, 1, HEADS:2 * HEADS],
                                      ALU.subtract).then_inc(node_ready[s], 1)

                def shifted_alpha(s, r):
                    rows = gathered0[s].rearrange("p (j c) -> p j c", c=TW)
                    by_edge = node_ps[s][:, 0:T * 2 * HEADS].rearrange("p (j c) -> p j c", c=2 * HEADS)
                    dve.wait_ge(spread_ready[s], r)
                    order.step(dve.tensor_tensor(alpha[s][:, :, :], by_edge[:, :, 0:HEADS], rows[:, :, D:TW], ALU.add))
                    order.step(dve.scalar_tensor_tensor(alpha2[s][:, :, :], alpha[s][:, :, :], SLOPE, alpha[s][:, :, :], ALU.mult, ALU.max))
                    order.step(dve.tensor_tensor(alpha[s][:, :, :], alpha2[s][:, :, :], by_edge[:, :, HEADS:2 * HEADS], ALU.subtract))
                    dve.tensor_scalar(alpha2[s][:, :, :], alpha[s][:, :, :], 0.0, None, ALU.min).then_inc(shifted_ready[s], 1)

                def weigh(s, r):
                    rows = gathered0[s].rearrange("p (j c) -> p j c", c=TW)
                    values = rows[:, :, 0:D].rearrange("p j (h c) -> p j h c", c=DH)
                    dve.wait_ge(weights_ready[s], r)
                    for j0, j1 in QUARTERS:
                        dve.tensor_tensor(values[:, j0:j1], values[:, j0:j1],
                                          rows[:, j0:j1, D:TW].unsqueeze(3).broadcast_to([P, j1 - j0, HEADS, DH]),
                                          ALU.mult).then_inc(weighted[s], 1)

                def self_shift(s, i):
                    own = self_alpha[:, bass.ds(2 * i + s, 1), :].rearrange("p o h -> p (o h)")
                    dve.tensor_tensor(selfw[s][:, :], own, node_m[s][:, :], ALU.subtract).then_inc(self_shifted[s], 1)

                def self_values(s, i):
                    dve.wait_ge(self_weight[s], i + 1)
                    dve.wait_ge(self_loaded[s], (i + 1) * 16)
                    order.step(dve.tensor_tensor(by_head(self_row[s][:, :]), by_head(self_row[s][:, :]), heads(selfw[s][:, :]), ALU.mult))

                def attend(s):
                    dve.wait_ge(quarters_used[s], count_of(dve, rounds[s]) * NQ + NQ)
                    order.step(dve.tensor_tensor(self_row[s][:, :], self_row[s][:, :], acc_ps[s][0:NB, 0:D], ALU.add))
                    order.step(dve.tensor_tensor(selfw[s][:, :], selfw[s][:, :], acc_ps[s][0:NB, D:TW], ALU.add))
                    order.restart()
                    with dve.If(count_of(dve, extra[s]) > 0):
                        order.step(dve.tensor_tensor(self_row[s][:, :], self_row[s][:, :], acc[s][:, 0:D], ALU.add))
                        order.step(dve.tensor_tensor(selfw[s][:, :], selfw[s][:, :], acc[s][:, D:TW], ALU.add))
                        order.step(dve.memset(acc[s][:, :], 0.0))
                        order.restart()
                    dve.reg_mov(extra[s], 0)
                    order.step(dve.reciprocal(tmp8[s][:, :], selfw[s][:, :]))
                    dve.tensor_tensor(by_head(self_row[s][:, :]), by_head(self_row[s][:, :]), heads(tmp8[s][:, :]),
                                      ALU.mult).then_inc(attended[s], 1)

                def residual(s, i):
                    b = 2 * i + s
                    dve.wait_ge(projected[s], i + 1)
                    for m in range(2):
                        last = dve.scalar_tensor_tensor(node_columns(m, b), acc_ps[s][:, m * NB:(m + 1) * NB], boT[:, m:m + 1],
                                                        node_columns(m, b), ALU.add, ALU.add)
                    order.step(last)
                    dve.bn_stats(stats[:, 0, bass.ds(b, 1), :].rearrange("p o c -> p (o c)"), node_columns(0, b))
                    order.step(dve.bn_stats(stats[:, 1, bass.ds(b, 1), :].rearrange("p o c -> p (o c)"), node_columns(1, b)))
                    dve.sem_inc(block_done[s], 1)

                def first_round(s, i, before, done, after):
                    if before is not None:
                        self_shift(*before)
                    r = scores_of(s)
                    if before is not None:
                        self_values(*before)
                    if done is not None:
                        residual(*done)
                    scan_partitions(s, r)
                    segment_maxima(s, r)
                    if after is not None:
                        prepare_small(after[0], 2 * after[1] + after[0])
                        prepare_onehot(after[0])
                    dve.wait_ge(block_begun[s], i + 1)
                    node_maxima(s, 2 * i + s, r)
                    if before is not None:
                        attend(before[0])
                    if after is not None:
                        next_round(dve, rounds[after[0]])
                    shifted_alpha(s, r)
                    weigh(s, r)
                    order.restart()

                def more_rounds(s, i):
                    b = 2 * i + s
                    lo, hi = edge_range(dve, b)
                    with dve.If(hi > lo + RE):
                        with dve.Fori(lo + RE, hi, RE) as at:
                            dve.reg_add(extra[s], extra[s], 1)
                            before = count_of(dve, rounds[s])
                            dve.wait_ge(quarters_used[s], before * NQ + NQ)
                            order.step(dve.tensor_tensor(acc[s][:, :], acc[s][:, :], acc_ps[s][0:NB, 0:TW], ALU.add))
                            prepare_small(s, b)
                            prepare_onehot(s)
                            next_round(dve, rounds[s])
                            r = scores_of(s)
                            scan_partitions(s, r)
                            segment_maxima(s, r)
                            node_maxima(s, b, r)
                            order.step(dve.tensor_tensor(rescale[s][:, :], run_m[s][:, :], node_m[s][:, :], ALU.subtract))
                            shifted_alpha(s, r)
                            weigh(s, r)
                            order.step(dve.tensor_tensor(by_head(acc[s][:, 0:D]), by_head(acc[s][:, 0:D]), heads(rescale[s][:, :]), ALU.mult))
                            order.step(dve.tensor_tensor(acc[s][:, D:TW], acc[s][:, D:TW], rescale[s][:, :], ALU.mult))
                            order.restart()

                prepare_small(0, 0)
                prepare_onehot(0)
                next_round(dve, rounds[0])
                order.restart()
                over_blocks(dve, first_round, more_rounds)
                residual(0, PAIRS - 1)
                self_shift(1, PAIRS - 1)
                self_values(1, PAIRS - 1)
                attend(1)
                residual(1, PAIRS - 1)
                order.restart()

            @block.scalar
            def _(act):
                rounds = counters(act, "act_rounds")
                act.wait_ge(tables_ready, 1)

                def begin_block(s, i):
                    b = 2 * i + s
                    act.wait_ge(block_done[s], i + 1)
                    act.dma_start(self_row[s][:, :], table0[bass.ds(b * NB, NB), 0:D]).then_inc(self_loaded[s], 16)
                    act.activation(run_max[s][:, :], scores[:, bass.ds(b, 1), :].rearrange("p o h -> p (o h)"), ACT.Copy)
                    act.activation(node_parts[s][:, :, 0:HEADS], score_parts[:, bass.ds(b, 1), :, :].rearrange("p o k h -> p (o k) h"),
                                   ACT.Copy).then_inc(block_begun[s], 1)

                def prepare(s):
                    before = count_of(act, rounds[s])
                    rec = record[s][:, :, :].bitcast(F32)
                    act.wait_ge(bias_ready[s], before + 1)
                    act.activation(reset[s][:, :, 1:T], rec[:, 1:T, 2].unsqueeze(1).broadcast_to([P, HEADS, T - 1]), ACT.Copy)
                    act.wait_ge(bias_turned[s], before + 1)
                    act.activation(biasT[s][:, :], mix_ps[s][0:HEADS, P:2 * P], ACT.Copy).then_inc(bias_copied[s], 1)
                    for c, (j0, j1) in enumerate(CHUNKS):
                        act.wait_ge(T_ready[s], before * len(CHUNKS) + c + 1)
                        act.activation(onehotT[s][:, j0:j1, :].rearrange("p j e -> p (j e)"),
                                       turn_ps[c % 2][0:NB, 0:(j1 - j0) * P], ACT.Copy).then_inc(
                                           T_copied[s] if j1 < T else prepared[s], 1)
                    next_round(act, rounds[s])

                def widen(s):
                    r = count_of(act, rounds[s])
                    act.wait_ge(quarters_used[s], r * NQ)
                    act.activation(onehot[s][:, :, :].rearrange("p j d -> p (j d)"), onehot_bf[s][:, :, :].rearrange("p j d -> p (j d)"),
                                   ACT.Copy).then_inc(onehot_wide[s], 1)

                def weights(s, joined):
                    r = count_of(act, rounds[s])
                    rows = gathered0[s].rearrange("p (j c) -> p j c", c=TW)
                    act.wait_ge(shifted_ready[s], r)
                    if joined:
                        act.activation(rescale[s][:, :], rescale[s][:, :], ACT.Exp)
                    act.activation(run_m[s][:, :], node_m[s][:, :], ACT.Copy)
                    act.activation(rows[:, :, D:TW], alpha2[s][:, :, :], ACT.Exp).then_inc(weights_ready[s], 1)

                def self_exp(s, i):
                    act.wait_ge(self_shifted[s], i + 1)
                    act.activation(selfw[s][:, :], selfw[s][:, :], ACT.Exp).then_inc(self_weight[s], 1)

                def copy_attended(s, i):
                    act.wait_ge(att_turned[s], i + 1)
                    act.activation(attT[s][:, :, :].rearrange("p k n -> p (k n)"), mix_ps[s][:, 256:256 + 2 * NB],
                                   ACT.Copy).then_inc(att_copied[s], 1)

                def first_round(s, i, before, done, after):
                    if before is not None:
                        self_exp(*before)
                    begin_block(s, i)
                    if after is not None:
                        prepare(after[0])
                    weights(s, False)
                    if before is not None:
                        copy_attended(*before)
                    if after is not None:
                        widen(after[0])

                def more_rounds(s, i):
                    lo, hi = edge_range(act, 2 * i + s)
                    with act.If(hi > lo + RE):
                        with act.Fori(lo + RE, hi, RE) as at:
                            prepare(s)
                            widen(s)
                            weights(s, True)

                prepare(0)
                widen(0)
                over_blocks(act, first_round, more_rounds)
                self_exp(1, PAIRS - 1)
                copy_attended(1, PAIRS - 1)

            @block.tensor
            def _(pe):
                rounds = counters(pe, "pe_rounds")
                for s in range(2):
                    pe.sem_inc(quarters_used[s], NQ)

                def sums(s, i, q):
                    r = count_of(pe, rounds[s])
                    rows = gathered0[s].rearrange("p (j c) -> p j c", c=TW)
                    pe.wait_ge(weighted[s], r * NQ + q + 1)
                    if q == 0:
                        pe.wait_ge(onehot_wide[s], r)
                        pe.wait_ge(block_done[s], i + 1)
                    j0, j1 = QUARTERS[q]
                    for j in range(j0, j1):
                        last = pe.matmul(acc_ps[s][0:NB, 0:TW], onehot[s][:, j, :], rows[:, j, :], start=(j == 0), stop=(j == T - 1),
                                         skip_group_check=True)
                    last.then_inc(quarters_used[s], 1)

                def prepare(s, chunks):
                    before = count_of(pe, rounds[s])
                    if chunks[0] == 0:
                        pe.wait_ge(bias_ready[s], before + 1)
                        pe.transpose(mix_ps[s][0:HEADS, P:2 * P], bias[s][:, :], identity[:, :]).then_inc(bias_turned[s], 1)
                        pe.wait_ge(onehot_ready[s], before + 1)
                    for c in chunks:
                        j0, j1 = CHUNKS[c]
                        if c >= 2:
                            pe.wait_ge(T_copied[s], before * (len(CHUNKS) - 1) + c - 1)
                        for j in range(j0, j1):
                            last = pe.matmul(turn_ps[c % 2][0:NB, (j - j0) * P:(j - j0 + 1) * P], onehot_bf[s][:, j, :], identity_bf[:, :],
                                             start=True, stop=True)
                        last.then_inc(T_ready[s], 1)

                def turn_tops(s, r):
                    pe.wait_ge(scan1_ready[s], r)
                    pe.transpose(mix_ps[s][0:HEADS, 0:P], local[s][:, :, T - 1], identity[:, :]).then_inc(tops_turned[s], 1)

                def turn_carries(s, r):
                    wait_apart(pe, scan_ready[s], r, 1)
                    pe.transpose(node_ps[s][:, 288:288 + HEADS], scanned[s][:, 0:P], identity[0:HEADS, 0:HEADS]).then_inc(carry_ready[s], 1)

                def select_maxima(s, r):
                    pe.wait_ge(prepared[s], r)
                    pe.wait_ge(ends_ready[s], r + 1)
                    for j in range(T):
                        for k in range(3):
                            last = pe.matmul(node_ps[s][0:NB, 272:273 + HEADS], onehot_bf[s][:, j, :], ends_parts[s][:, k, j, :],
                                             start=(j == 0 and k == 0), stop=(j == T - 1 and k == 2))
                    last.then_inc(max_selected[s], 1)

                def spread_nodes(s, r):
                    pe.wait_ge(block_begun[s], 1)
                    pe.wait_ge(node_ready[s], r)
                    for j in range(T):
                        for k in range(3):
                            last = pe.matmul(node_ps[s][:, j * 2 * HEADS:(j + 1) * 2 * HEADS], onehotT[s][:, j, :], node_parts[s][:, k, :],
                                             start=(k == 0), stop=(k == 2))
                    last.then_inc(spread_ready[s], 1)

                def project(s, i):
                    pe.wait_ge(attended[s], i + 1)
                    for k in range(2):
                        last = pe.transpose(mix_ps[s][:, 256 + k * NB:256 + (k + 1) * NB], self_row[s][:, k * P:(k + 1) * P],
                                            identity[0:NB, 0:NB])
                    last.then_inc(att_turned[s], 1)
                    pe.wait_ge(att_copied[s], i + 1)
                    for m in range(2):
                        for k in range(2):
                            last = pe.matmul(acc_ps[s][:, m * NB:(m + 1) * NB], wo_sb[:, k, m * P:(m + 1) * P], attT[s][:, k, :],
                                             start=(k == 0), stop=(k == 1))
                    last.then_inc(projected[s], 1)

                every = range(len(CHUNKS))

                def first_round(s, i, before, done, after):
                    r = count_of(pe, rounds[s])
                    turn_tops(s, r)
                    turn_carries(s, r)
                    if before is not None:
                        sums(before[0], before[1], 2)
                        sums(before[0], before[1], 3)
                    select_maxima(s, r)
                    if after is not None:
                        prepare(after[0], every[0:2])
                    spread_nodes(s, r)
                    if after is not None:
                        prepare(after[0], every[2:])
                    if before is not None:
                        project(*before)
                    if after is not None:
                        next_round(pe, rounds[after[0]])
                    sums(s, i, 0)
                    sums(s, i, 1)

                def more_rounds(s, i):
                    lo, hi = edge_range(pe, 2 * i + s)
                    with pe.If(hi > lo + RE):
                        with pe.Fori(lo + RE, hi, RE) as at:
                            sums(s, i, 2)
                            sums(s, i, 3)
                            prepare(s, every)
                            next_round(pe, rounds[s])
                            r = count_of(pe, rounds[s])
                            for step in (turn_tops, turn_carries, select_maxima, spread_nodes):
                                step(s, r)
                            sums(s, i, 0)
                            sums(s, i, 1)

                prepare(0, every)
                next_round(pe, rounds[0])
                over_blocks(pe, first_round, more_rounds)
                sums(1, PAIRS - 1, 2)
                sums(1, PAIRS - 1, 3)
                project(1, PAIRS - 1)

        def norm_affine(dve, order, n, groups, variance_ready, spread_ready):
            for m in range(2):
                order.step(dve.bn_aggr(moments[:, m, :], stats[:, m, 0:groups, :].rearrange("p b c -> p (b c)")))
            dve.sem_inc(variance_ready, 1)
            dve.wait_ge(spread_ready, 1)
            order.step(dve.reciprocal(spread[:, :], spread[:, :]))
            order.step(dve.tensor_tensor(gain[:, :], spread[:, :], bnT[:, 2 * n, :], ALU.mult))
            order.step(dve.tensor_tensor(shift[:, :], moments[:, :, 0], gain[:, :], ALU.mult))
            order.step(dve.tensor_tensor(shift[:, :], bnT[:, 2 * n + 1, :], shift[:, :], ALU.subtract))

        with ExitStack() as phase:
            sem = phase_semaphores(phase)

            def pair(name):
                return [sem(f"f_{name}{s}") for s in range(2)]

            variance_ready, spread_ready = sem("f_variance"), sem("f_spread")
            normed, up_ready, hidden_ready, down_ready, out_read = (pair("normed"), pair("up_ready"), pair("hidden_ready"),
                                                                    pair("down_ready"), pair("out_read"))
            dve_order = sem("dve_order4")
            hidden = [phase.enter_context(nc.sbuf_tensor(f"hidden{s}", [P, 4, NU], F32)) for s in range(2)]
            up_ps, down_ps = [banks[0:2], banks[2:4]], banks[4:6]
            block = phase.enter_context(nc.Block())

            def unit_columns(k, u):
                return hT[:, k, bass.ds(u * NU, NU)]

            @block.vector
            def _(dve):
                order = InOrder(dve, dve_order)
                norm_affine(dve, order, 0, BLOCKS, variance_ready, spread_ready)
                order.restart()
                for s in range(2):
                    dve.sem_inc(out_read[s], 1)

                def normalise(s, u):
                    for m in range(2):
                        dve.tensor_scalar(unit_columns(m, u), unit_columns(m, u), gain[:, m:m + 1], shift[:, m:m + 1],
                                          ALU.mult, ALU.add).then_inc(normed[s], 1)

                def finish(s, i):
                    u = 2 * i + s
                    dve.wait_ge(down_ready[s], i + 1)
                    for m in range(2):
                        last = dve.scalar_tensor_tensor(unit_columns(m, u), down_ps[s][:, m * NU:(m + 1) * NU], b2T[:, m:m + 1],
                                                        unit_columns(m, u), ALU.add, ALU.add)
                    order.step(last)
                    dve.sem_inc(out_read[s], 1)
                    for m in range(2):
                        last = dve.bn_stats(stats[:, m, bass.ds(u, 1), :].rearrange("p o c -> p (o c)"), unit_columns(m, u))
                    order.step(last)
                    order.restart()

                normalise(0, 0)
                normalise(1, 1)
                with dve.Fori(0, UNIT_PAIRS - 1) as i:
                    normalise(0, 2 * i + 2)
                    finish(0, i)
                    normalise(1, 2 * i + 3)
                    finish(1, i)
                normalise(0, UNITS - 1)
                finish(0, UNIT_PAIRS - 1)
                finish(1, UNIT_PAIRS - 1)
                finish(0, UNIT_PAIRS)

            @block.scalar
            def _(act):
                act.wait_ge(variance_ready, 1)
                act.activation(spread[:, :], moments[:, :, 1], ACT.Sqrt, bias=eps_bn[:, :]).then_inc(spread_ready, 1)

                def rectify(s, i):
                    act.wait_ge(up_ready[s], i + 1)
                    for m in range(4):
                        act.activation(hidden[s][:, m, :], up_ps[s][m // 2][:, (m % 2) * NU:(m % 2 + 1) * NU], ACT.Relu,
                                       bias=b1T[:, m:m + 1]).then_inc(hidden_ready[s], 1)

                with act.Fori(0, UNIT_PAIRS) as i:
                    rectify(0, i)
                    rectify(1, i)
                rectify(0, UNIT_PAIRS)

            @block.tensor
            def _(pe):
                def up(s, i):
                    pe.wait_ge(normed[s], 2 * i + 2)
                    for m in range(4):
                        for k in range(2):
                            last = pe.matmul(up_ps[s][m // 2][:, (m % 2) * NU:(m % 2 + 1) * NU], wf1_sb[:, k, m * P:(m + 1) * P],
                                             unit_columns(k, 2 * i + s), start=(k == 0), stop=(k == 1))
                    last.then_inc(up_ready[s], 1)

                def down(s, i):
                    pe.wait_ge(hidden_ready[s], 4 * i + 4)
                    pe.wait_ge(out_read[s], i + 1)
                    for m in range(2):
                        for k in range(4):
                            last = pe.matmul(down_ps[s][:, m * NU:(m + 1) * NU], wf2_sb[:, k, m * P:(m + 1) * P], hidden[s][:, k, :],
                                             start=(k == 0), stop=(k == 3))
                    last.then_inc(down_ready[s], 1)

                up(0, 0)
                with pe.Fori(0, UNIT_PAIRS) as i:
                    up(1, i)
                    down(0, i)
                    up(0, i + 1)
                    down(1, i)
                down(0, UNIT_PAIRS)

        with ExitStack() as phase:
            sem = phase_semaphores(phase)

            def pair(name):
                return [sem(f"g_{name}{s}") for s in range(2)]

            def tiles(name, shape):
                return [phase.enter_context(nc.sbuf_tensor(f"g_{name}{s}", shape, F32)) for s in range(2)]

            variance_ready, spread_ready = sem("g_variance"), sem("g_spread")
            x_loaded, x_used, normed, turned = pair("x_loaded"), pair("x_used"), pair("normed"), pair("turned")
            var_ready, std_ready = pair("var_ready"), pair("std_ready")
            x1_ready, x1_stored, centred, h_ready, h_stored = (pair("x1_ready"), pair("x1_stored"), pair("centred"),
                                                               pair("h_ready"), pair("h_stored"))
            dve_order = sem("dve_order5")
            x_sb, yT, x1_sb, norm, h_sb = (tiles("x_sb", [NB, D]), tiles("yT", [P, 2, NB]), tiles("x1_sb", [NB, D]),
                                           tiles("norm", [NB, D]), tiles("h_sb", [NB, D]))
            six, two, std = tiles("six", [NB, 6]), tiles("two", [NB, 2]), tiles("std", [NB, 1])
            y_ps = banks[0:2]
            block = phase.enter_context(nc.Block())

            @block.sync
            def _(sp):
                with sp.Fori(0, PAIRS) as i:
                    for s in range(2):
                        sp.wait_ge(x_used[s], i + 1)
                        sp.dma_start(x_sb[s][:, :], block_rows(x, 2 * i + s)).then_inc(x_loaded[s], 16)

            @block.vector
            def _(dve):
                order = InOrder(dve, dve_order)
                norm_affine(dve, order, 1, UNITS, variance_ready, spread_ready)
                order.restart()
                for s in range(2):
                    dve.sem_inc(x_used[s], 1)
                    dve.sem_inc(std_ready[s], 1)

                def affine(s, i):
                    for m in range(2):
                        order.step(dve.tensor_scalar(yT[s][:, m, :], node_columns(m, 2 * i + s), gain[:, m:m + 1], shift[:, m:m + 1],
                                                     ALU.mult, ALU.add))
                    dve.sem_inc(normed[s], 1)
                    order.restart()

                def residual(s, i):
                    dve.wait_ge(turned[s], i + 1)
                    dve.wait_ge(x_loaded[s], (i + 1) * 16)
                    dve.wait_ge(x1_stored[s], (i + 1) * 16)
                    order.step(dve.tensor_tensor(x1_sb[s][:, :], y_ps[s][0:NB, 0:D], x_sb[s][:, :], ALU.add))
                    dve.sem_inc(x1_ready[s], 1)
                    dve.sem_inc(x_used[s], 1)
                    order.step(dve.bn_stats(six[s][:, :], x1_sb[s][:, :]))
                    order.step(dve.bn_aggr(two[s][:, :], six[s][:, :]))
                    dve.sem_inc(var_ready[s], 1)
                    order.restart()

                def centre(s, i):
                    dve.wait_ge(std_ready[s], i + 2)
                    dve.wait_ge(h_ready[s], i + 1)
                    order.step(dve.reciprocal(std[s][:, :], std[s][:, :]))
                    order.step(dve.tensor_scalar(norm[s][:, :], x1_sb[s][:, :], two[s][:, 0:1], std[s][:, 0:1],
                                                 ALU.subtract, ALU.mult))
                    dve.sem_inc(centred[s], 1)
                    order.restart()

                affine(0, 0)
                affine(1, 0)
                residual(0, 0)
                with dve.Fori(0, PAIRS - 1) as i:
                    residual(1, i)
                    affine(0, i + 1)
                    centre(0, i)
                    affine(1, i + 1)
                    residual(0, i + 1)
                    centre(1, i)
                residual(1, PAIRS - 1)
                centre(0, PAIRS - 1)
                centre(1, PAIRS - 1)

            @block.scalar
            def _(act):
                for s in range(2):
                    act.sem_inc(h_ready[s], 1)
                act.wait_ge(variance_ready, 1)
                act.activation(spread[:, :], moments[:, :, 1], ACT.Sqrt, bias=eps_bn[:, :]).then_inc(spread_ready, 1)

                def deviation(s, i):
                    act.wait_ge(var_ready[s], i + 1)
                    act.activation(std[s][:, :], two[s][:, 1:2], ACT.Sqrt, bias=eps_ln[0:NB, :]).then_inc(std_ready[s], 1)

                def rectify(s, i):
                    act.wait_ge(centred[s], i + 1)
                    act.wait_ge(h_stored[s], (i + 1) * 16)
                    act.activation(h_sb[s][:, :], norm[s][:, :], ACT.Relu).then_inc(h_ready[s], 1)

                deviation(0, 0)
                with act.Fori(0, PAIRS - 1) as i:
                    deviation(1, i)
                    rectify(0, i)
                    deviation(0, i + 1)
                    rectify(1, i)
                deviation(1, PAIRS - 1)
                rectify(0, PAIRS - 1)
                rectify(1, PAIRS - 1)

            @block.gpsimd
            def _(pool):
                for s in range(2):
                    first_store(pool, x1_stored[s])
                    first_store(pool, h_stored[s])
                with pool.Fori(0, PAIRS) as i:
                    for s in range(2):
                        wait_apart(pool, x1_ready[s], i + 1, 1)
                        pool.dma_start(block_rows(x1, 2 * i + s), x1_sb[s][:, :]).then_inc(x1_stored[s], 16)
                        wait_apart(pool, h_ready[s], i + 2, 1)
                        pool.dma_start(block_rows(table1, 2 * i + s), h_sb[s][:, :]).then_inc(h_stored[s], 16)
                for s in range(2):
                    pool.wait_ge(x1_stored[s], 16 * (PAIRS + 1))
                    pool.wait_ge(h_stored[s], 16 * (PAIRS + 1))

            @block.tensor
            def _(pe):
                with pe.Fori(0, PAIRS) as i:
                    for s in range(2):
                        pe.wait_ge(normed[s], i + 1)
                        for m in range(2):
                            last = pe.transpose(y_ps[s][0:NB, m * P:(m + 1) * P], yT[s][:, m, :], identity[:, :])
                        last.then_inc(turned[s], 1)

        def graph_layer(n, table, w):
            last_layer = n == 2
            k_tiles = w // P
            with ExitStack() as phase:
                sem = phase_semaphores(phase)

                def pair(name):
                    return [sem(f"l{n}_{name}{s}") for s in range(2)]

                def tiles(name, shape):
                    return [phase.enter_context(nc.sbuf_tensor(f"l{n}_{name}{s}", shape, F32)) for s in range(2)]

                QUARTERS = [(0, 4), (4, 8), (8, 12), (12, T)]
                NQ = len(QUARTERS)
                record_loaded, round_gathered, quarters_used = pair("record_loaded"), pair("round_gathered"), pair("quarters_used")
                rows_gathered = [[sem(f"l{n}_rows_gathered{s}_{q}") for q in range(NQ)] for s in range(2)]
                onehot_ready, sums_ready, sums_read, z_ready = (pair("onehot_ready"), pair("sums_ready"), pair("sums_read"),
                                                                pair("z_ready"))
                own_loaded, own_used, sum_turned, zT_ready = pair("own_loaded"), pair("own_used"), pair("sum_turned"), pair("zT_ready")
                product, hidden_product, hidden_ready = pair("product"), pair("hidden_product"), pair("hidden_ready")
                result_ready, stored = pair("result_ready"), pair("stored")
                dve_order = sem(f"dve_order{6 + n}")
                own, z = tiles("own", [NB, w]), tiles("z", [NB, w])
                zT = tiles("zT", [P, k_tiles, NB]) if not last_layer else None
                x1_sb = tiles("x1_sb", [NB, D]) if last_layer else None
                hiddenT = tiles("hiddenT", [P, 4, NB]) if n == 0 else None
                width = (HID, D, D)[n]
                result = tiles("result", [NB, width])
                sum_ps, turn_ps, product_ps, hidden_ps = banks[0:2], banks[2:4], banks[4:6], banks[6:8]
                target = (table2, table3, out)[n]
                own_loads = 32 if last_layer else 16

                def over_steps(engine, stages):
                    def step(b, j=0):
                        for stage, lag in stages:
                            if 0 <= b - lag < BLOCKS:
                                stage((b - lag) % 2, j + (b - lag) // 2)

                    for b in range(4):
                        step(b)
                    with engine.Fori(0, PAIRS - 2) as j:
                        step(4, j)
                        step(5, j)
                    for b in range(BLOCKS, BLOCKS + 3):
                        step(b)

                block = phase.enter_context(nc.Block())

                def edge_range(engine, b):
                    lo = engine.value_load(first_edge[0:1, bass.ds(b, 1)], min_val=0, max_val=E)
                    hi = engine.value_load(first_edge[0:1, bass.ds(b + 1, 1)], min_val=0, max_val=E)
                    return lo, hi

                def counters(engine, name):
                    regs = [engine.alloc_register(f"{name}{n}_{s}") for s in range(2)]
                    for r in regs:
                        engine.reg_mov(r, 0)
                    return regs

                def count_of(engine, reg):
                    return engine.snap(reg, min_val=0, max_val=4 * BLOCKS)

                @block.sync
                def _(sp):
                    rounds = counters(sp, "sp_r")
                    with sp.Fori(0, PAIRS) as i:
                        for s in range(2):
                            lo, hi = edge_range(sp, 2 * i + s)
                            with sp.Fori(lo, hi, RE) as at:
                                sp.wait_ge(round_gathered[s], count_of(sp, rounds[s]) + 1)
                                sp.dma_start(record[s][:, :, :].rearrange("p j c -> p (j c)"),
                                             edges[bass.ds(at, RE), :].rearrange("(p j) c -> p (j c)", j=T)).then_inc(record_loaded[s], 16)
                                sp.reg_add(rounds[s], rounds[s], 1)
                            sp.wait_ge(own_used[s], i + 1)
                            sp.dma_start(own[s][:, :], block_rows(table, 2 * i + s)).then_inc(own_loaded[s], 16)
                            if last_layer:
                                sp.dma_start(x1_sb[s][:, :], block_rows(x1, 2 * i + s)).then_inc(own_loaded[s], 16)

                @block.gpsimd
                def _(pool):
                    rounds = counters(pool, "pool_r")
                    with pool.Fori(0, PAIRS) as i:
                        for s in range(2):
                            lo, hi = edge_range(pool, 2 * i + s)
                            with pool.Fori(lo, hi, RE) as at:
                                before = count_of(pool, rounds[s])
                                wait_apart(pool, record_loaded[s], before * 16 + 16, 16)
                                for q, (j0, j1) in enumerate(QUARTERS):
                                    wait_apart(pool, quarters_used[s], before * NQ + q + 1, 1)
                                    for j in range(j0, j1):
                                        pool.indirect_dma_start(
                                            out=gathered(s, w)[:, j * w:(j + 1) * w], out_offset=None, in_=table,
                                            in_offset=bass.IndirectOffsetOnAxis(ap=record[s][:, j, 0:1], axis=0),
                                        ).then_inc(rows_gathered[s][q], 16)
                                pool.reg_add(rounds[s], rounds[s], 1)

                @block.vector
                def _(dve):
                    order = InOrder(dve, dve_order)
                    rounds = counters(dve, "dve_r")
                    for s in range(2):
                        dve.sem_inc(own_used[s], 1)
                        dve.sem_inc(sums_read[s], 1)

                    def rounds_of(s, b):
                        lo, hi = edge_range(dve, b)
                        with dve.Fori(lo, hi, RE) as at:
                            before = count_of(dve, rounds[s])
                            dve.wait_ge(record_loaded[s], before * 16 + 16)
                            order.step(dve.tensor_scalar(relative[s][:, :], record[s][:, :, 1].bitcast(F32),
                                                         minus_base[:, bass.ds(b, 1)], None, ALU.add))
                            dve.wait_ge(quarters_used[s], before * NQ + NQ)
                            dve.tensor_tensor(onehot[s][:, :, :], column[:, :].unsqueeze(1).broadcast_to([P, T, NB]),
                                              relative[s][:, :].unsqueeze(2).broadcast_to([P, T, NB]),
                                              ALU.is_equal).then_inc(onehot_ready[s], 1)
                            dve.reg_add(rounds[s], rounds[s], 1)
                            order.restart()

                    def finish(s, i):
                        dve.wait_ge(sums_ready[s], i + 1)
                        dve.wait_ge(own_loaded[s], (i + 1) * own_loads)
                        if not last_layer:
                            dve.wait_ge(sum_turned[s], i + 1)
                        order.step(dve.scalar_tensor_tensor(z[s][:, :], own[s][:, :], one_eps[0:NB, n:n + 1],
                                                            sum_ps[s][0:NB, 0:w], ALU.mult, ALU.add))
                        dve.sem_inc(sums_read[s], 1)
                        if n == 1:
                            order.step(dve.tensor_tensor(z[s][:, :], z[s][:, :], c2_sb[:, :], ALU.add))
                        if last_layer:
                            order.step(dve.tensor_tensor(z[s][:, :], z[s][:, :], c3_sb[:, :], ALU.add))
                            dve.wait_ge(stored[s], (i + 1) * 16)
                            order.step(dve.tensor_tensor(result[s][:, :], z[s][:, :], x1_sb[s][:, :], ALU.add))
                            dve.sem_inc(result_ready[s], 1)
                        else:
                            dve.sem_inc(z_ready[s], 1)
                        dve.sem_inc(own_used[s], 1)
                        order.restart()

                    rounds_of(0, 0)
                    with dve.Fori(0, PAIRS - 1) as i:
                        rounds_of(1, 2 * i + 1)
                        finish(0, i)
                        rounds_of(0, 2 * i + 2)
                        finish(1, i)
                    rounds_of(1, BLOCKS - 1)
                    finish(0, PAIRS - 1)
                    finish(1, PAIRS - 1)

                @block.scalar
                def _(act):
                    for s in range(2):
                        act.sem_inc(result_ready[s], 1)
                        first_store(act, stored[s])

                    def copy_turned(s, i):
                        act.wait_ge(sum_turned[s], i + 2)
                        act.activation(zT[s][:, :, :].rearrange("p k n -> p (k n)"), turn_ps[s][:, 0:k_tiles * NB],
                                       ACT.Relu if n == 1 else ACT.Copy).then_inc(zT_ready[s], 1)

                    def rectify(s, i):
                        act.wait_ge(hidden_product[s], i + 1)
                        for m in range(4):
                            act.activation(hiddenT[s][:, m, :], hidden_ps[s][:, m * NB:(m + 1) * NB], ACT.Relu,
                                           bias=c1T[:, m:m + 1]).then_inc(hidden_ready[s], 1)

                    def store(s, i):
                        if not last_layer:
                            act.wait_ge(product[s], i + 1)
                            act.wait_ge(stored[s], (i + 1) * 16)
                            act.activation(result[s][:, :], product_ps[s][0:NB, 0:width], ACT.Copy).then_inc(result_ready[s], 1)
                        act.wait_ge(result_ready[s], i + 2)
                        act.dma_start(block_rows(target, 2 * i + s), result[s][:, :]).then_inc(stored[s], 16)

                    if n == 0:
                        over_steps(act, [(copy_turned, 1), (rectify, 2), (store, 3)])
                    elif n == 1:
                        over_steps(act, [(copy_turned, 1), (store, 2)])
                    else:
                        over_steps(act, [(store, 1)])
                    for s in range(2):
                        act.wait_ge(stored[s], 16 * (PAIRS + 1))

                @block.tensor
                def _(pe):
                    rounds = counters(pe, "pe_r")
                    for s in range(2):
                        pe.sem_inc(quarters_used[s], NQ)
                        pe.sem_inc(round_gathered[s], 1)
                        if not last_layer:
                            pe.sem_inc(sum_turned[s], 1)

                    def rounds_of(s, i):
                        rows = gathered(s, w).rearrange("p (j c) -> p j c", c=w)
                        lo, hi = edge_range(pe, 2 * i + s)
                        pe.wait_ge(sums_read[s], i + 1)
                        pe.matmul(sum_ps[s][0:NB, 0:w], zeros[:, 0:NB], zeros[:, 0:w], start=True, stop=True)
                        with pe.Fori(lo, hi, RE) as at:
                            before = count_of(pe, rounds[s])
                            pe.wait_ge(onehot_ready[s], before + 1)
                            for q, (j0, j1) in enumerate(QUARTERS):
                                pe.wait_ge(rows_gathered[s][q], (before + 1) * (16 * (j1 - j0)))
                                for j in range(j0, j1):
                                    last = pe.matmul(sum_ps[s][0:NB, 0:w], onehot[s][:, j, :], rows[:, j, :], start=False,
                                                     stop=(j == T - 1), skip_group_check=True)
                                    if j == T - 2:
                                        last.then_inc(round_gathered[s], 1)
                                last.then_inc(quarters_used[s], 1)
                            pe.reg_add(rounds[s], rounds[s], 1)
                        pe.matmul(sum_ps[s][0:NB, 0:2], zeros[:, 0:NB], zeros[:, 0:2], start=False, stop=True,
                                  skip_group_check=True).then_inc(sums_ready[s], 1)

                    def turn(s, i):
                        pe.wait_ge(z_ready[s], i + 1)
                        for k in range(k_tiles):
                            last = pe.transpose(turn_ps[s][:, k * NB:(k + 1) * NB], z[s][:, k * P:(k + 1) * P], identity[0:NB, 0:NB])
                        last.then_inc(sum_turned[s], 1)

                    def up(s, i):
                        pe.wait_ge(zT_ready[s], i + 1)
                        for m in range(4):
                            for k in range(k_tiles):
                                last = pe.matmul(hidden_ps[s][:, m * NB:(m + 1) * NB], w1_sb[:, k, m * P:(m + 1) * P], zT[s][:, k, :],
                                                 start=(k == 0), stop=(k == k_tiles - 1))
                        last.then_inc(hidden_product[s], 1)

                    def down(s, i):
                        if n == 0:
                            pe.wait_ge(hidden_ready[s], 4 * i + 4)
                            factor, weights = hiddenT[s], w2_sb
                        else:
                            pe.wait_ge(zT_ready[s], i + 1)
                            factor, weights = zT[s], w3_sb
                        pe.wait_ge(result_ready[s], i + 1)
                        for k in range(4):
                            last = pe.matmul(product_ps[s][0:NB, 0:width], factor[:, k, :], weights[:, k, :], start=(k == 0), stop=(k == 3))
                        last.then_inc(product[s], 1)

                    if n == 0:
                        over_steps(pe, [(rounds_of, 0), (turn, 1), (up, 2), (down, 3)])
                    elif n == 1:
                        over_steps(pe, [(rounds_of, 0), (turn, 1), (down, 2)])
                    else:
                        over_steps(pe, [(rounds_of, 0)])

        graph_layer(0, table1, D)
        graph_layer(1, table2, HID)
        graph_layer(2, table3, D)


_INS = ['x', 'src', 'dst', 'L0_gnn_Wq', 'L0_gnn_bq', 'L0_gnn_Wk', 'L0_gnn_bk', 'L0_gnn_Wv', 'L0_gnn_bv', 'L0_gnn_Wo', 'L0_gnn_bo',
        'L0_gnn_W1', 'L0_gnn_b1', 'L0_gnn_W2', 'L0_gnn_b2', 'L0_gnn_bn1_g', 'L0_gnn_bn1_b', 'L0_gnn_bn2_g', 'L0_gnn_bn2_b',
        'L1_gnn_w1', 'L1_gnn_b1', 'L1_gnn_eps1', 'L1_gnn_w2', 'L1_gnn_b2', 'L1_gnn_eps2', 'L1_gnn_w3', 'L1_gnn_b3', 'L1_gnn_eps3']


def kernel(**inputs):
    import numpy as np
    import concourse.bacc as bacc
    from concourse.bass_utils import run_bass_kernel_spmd

    nc = bacc.Bacc("TRN2", target_bir_lowering=False, num_devices=1)
    arrays, args = {}, []
    for name in _INS:
        a = np.ascontiguousarray(inputs[name])
        if a.ndim == 0:
            a = a.reshape(1)
        arrays[f"in_{name}"] = a
        args.append(nc.dram_tensor(f"in_{name}", a.shape, mybir.dt.from_np(a.dtype), kind="ExternalInput").ap())
    args.append(nc.dram_tensor("out_0", (N, D), F32, kind="ExternalOutput").ap())
    build(nc, *args)
    r = run_bass_kernel_spmd(nc, [arrays], core_ids=[0])
    return r.results[0]["out_0"]
```
